# Optimizing a Trainium2 kernel written in Bass

```python
import numpy as np
import jax
import jax.numpy as jnp

def _softmax(x, axis=-1):
    return jax.nn.softmax(x, axis=axis)

def _gelu(x):
    return jax.nn.gelu(x, approximate=True)

def _silu(x):
    return jax.nn.silu(x)

def _sigmoid(x):
    return jax.nn.sigmoid(x)

def _layernorm(x, axis=-1, eps=1e-05):
    m = jnp.mean(x, axis=axis, keepdims=True)
    v = jnp.var(x, axis=axis, keepdims=True)
    return (x - m) / jnp.sqrt(v + eps)

def _scatter_add(tgt, idx, src, axis=0):
    return tgt.at[idx].add(src)

def _segment_sum(src, seg, n):
    return jax.ops.segment_sum(src, seg, n)
kernel_name = 'mk_gnn_resnorm_d4_gnn_r32_7622fe'

def setup_inputs(seed: int=0):
    np.random.seed(seed)
    _w = jnp.asarray

    def _rec_inputs():
        import jax
        import jax.numpy as jnp
        _gk = jax.random.key(seed)
        x = -0.000202 + 1 * jax.random.normal(jax.random.fold_in(_gk, 1), (50000, 128), jnp.float32)
        src = jax.random.randint(jax.random.fold_in(_gk, 2), (50000,), 0, 50000, jnp.int32)
        dst = jax.random.randint(jax.random.fold_in(_gk, 3), (50000,), 0, 50000, jnp.int32)
        _o = jnp.argsort(dst, stable=True)
        src = src[_o]
        dst = dst[_o]
        edge_attr_128 = 4.59472e-05 + 1.00006 * jax.random.normal(jax.random.fold_in(_gk, 12), (50000, 128), jnp.float32)
        return (x, src, dst, edge_attr_128)
    x, src, dst, edge_attr_128 = _rec_inputs()

    def _L0_gnn_setup():
        import jax, jax.numpy as jnp
        import numpy as np
        N_NODES = 50000
        N_HEDGES = 10000
        NNZ = 20000
        D_IN, D_HID, D_OUT = (128, 128, 128)

        def _glorot(key, fan_in, fan_out):
            s = jnp.sqrt(6.0 / (fan_in + fan_out)).astype(jnp.float32)
            return jax.random.uniform(key, (fan_in, fan_out), jnp.float32, -s, s)

        def _hconv(x, W, b, row, col):
            xw = x @ W
            ones = jnp.ones(row.shape[0], xw.dtype)
            deg_n = jax.ops.segment_sum(ones, row, num_segments=N_NODES)
            deg_e = jax.ops.segment_sum(ones, col, num_segments=N_HEDGES)
            d_inv = jnp.where(deg_n > 0, 1.0 / deg_n, 0.0)
            b_inv = jnp.where(deg_e > 0, 1.0 / deg_e, 0.0)
            m = jax.ops.segment_sum(xw[row], col, num_segments=N_HEDGES) * b_inv[:, None]
            out = jax.ops.segment_sum(m[col], row, num_segments=N_NODES) * d_inv[:, None]
            return out + b
        key = jax.random.key(seed)
        k_x, k_r, k_c, k_w1, k_w2 = jax.random.split(key, 5)
        x = jax.random.normal(k_x, (N_NODES, D_IN), jnp.float32)
        row = jax.random.randint(k_r, (NNZ,), 0, N_NODES)
        col = jax.random.randint(k_c, (NNZ,), 0, N_HEDGES)
        edge_index = jnp.stack([row, col]).astype(jnp.int64)
        return {'x': x, 'edge_index': edge_index, 'W1': _glorot(k_w1, D_IN, D_HID), 'b1': jnp.zeros((D_HID,), jnp.float32), 'W2': _glorot(k_w2, D_HID, D_OUT), 'b2': jnp.zeros((D_OUT,), jnp.float32)}
    _L0_gnn_all = _L0_gnn_setup()
    _L0_gnn_in = {k: v for k, v in _L0_gnn_all.items() if k in ('W1', 'b1', 'W2', 'b2')}
    del _L0_gnn_all

    def _L1_gnn_setup():
        import jax, jax.numpy as jnp
        import numpy as np
        N_NODES = 3125
        N_EDGES = 50000
        IN_DIM = 128
        HEADS = 4
        OUT_DIM = 32
        NEG_SLOPE = 0.2
        key = jax.random.key(seed)
        k_x, k_e, k_w, k_as, k_ad = jax.random.split(key, 5)
        x = jax.random.normal(k_x, (N_NODES, IN_DIM), dtype=jnp.float32)
        edge_index = jax.random.randint(k_e, (2, N_EDGES), 0, N_NODES, dtype=jnp.int64)
        W = jax.random.normal(k_w, (IN_DIM, HEADS * OUT_DIM), dtype=jnp.float32) / np.sqrt(IN_DIM)
        att_src = jax.random.normal(k_as, (HEADS, OUT_DIM), dtype=jnp.float32) / np.sqrt(OUT_DIM)
        att_dst = jax.random.normal(k_ad, (HEADS, OUT_DIM), dtype=jnp.float32) / np.sqrt(OUT_DIM)
        bias = jnp.zeros((HEADS * OUT_DIM,), dtype=jnp.float32)
        return {'x': x, 'edge_index': edge_index, 'W': W, 'att_src': att_src, 'att_dst': att_dst, 'bias': bias}
    _L1_gnn_all = _L1_gnn_setup()
    _L1_gnn_in = {k: v for k, v in _L1_gnn_all.items() if k in ('W', 'att_src', 'att_dst', 'bias')}
    del _L1_gnn_all

    def _L2_gnn_setup():
        import jax, jax.numpy as jnp
        import numpy as np
        N_NODE = 50000
        N_EDGE = 625000
        FDIM = 128
        HID = 128
        EPS = 1e-05
        key = jax.random.key(seed)
        ks = jax.random.split(key, 12)
        node_feature = jax.random.normal(ks[0], (N_NODE, FDIM), dtype=jnp.float32)
        edge_matrix = jax.random.randint(ks[1], (2, N_EDGE), 0, N_NODE, dtype=jnp.int32)
        edge_feature = jax.random.normal(ks[2], (N_EDGE, FDIM), dtype=jnp.float32)
        in_dim = FDIM + FDIM
        s1 = 1.0 / np.sqrt(in_dim)
        s2 = 1.0 / np.sqrt(HID)
        W1 = jax.random.uniform(ks[3], (in_dim, HID), jnp.float32, -s1, s1)
        b1 = jax.random.uniform(ks[4], (HID,), jnp.float32, -s1, s1)
        W2 = jax.random.uniform(ks[5], (HID, HID), jnp.float32, -s2, s2)
        b2 = jax.random.uniform(ks[6], (HID,), jnp.float32, -s2, s2)
        W3 = jax.random.uniform(ks[7], (HID, FDIM), jnp.float32, -s2, s2)
        b3 = jax.random.uniform(ks[8], (FDIM,), jnp.float32, -s2, s2)
        gamma = jnp.ones((FDIM,), jnp.float32)
        beta = jnp.zeros((FDIM,), jnp.float32)
        return {'node_feature': node_feature, 'edge_matrix': edge_matrix, 'edge_feature': edge_feature, 'W1': W1, 'b1': b1, 'W2': W2, 'b2': b2, 'W3': W3, 'b3': b3, 'gamma': gamma, 'beta': beta}
    _L2_gnn_all = _L2_gnn_setup()
    _L2_gnn_in = {k: v for k, v in _L2_gnn_all.items() if k in ('W1', 'b1', 'W2', 'b2', 'W3', 'b3', 'gamma', 'beta')}
    del _L2_gnn_all

    def _L3_gnn_setup():
        import jax, jax.numpy as jnp
        import numpy as np
        N_NODES = 3125
        N_EDGES = 100000
        FEAT = 128
        K = 4

        def spmm(x, edge_index, deg_inv_sqrt, num_nodes):
            src, dst = (edge_index[0], edge_index[1])
            norm = deg_inv_sqrt[src] * deg_inv_sqrt[dst]
            msg = x[src] * norm[:, None]
            return jax.ops.segment_sum(msg, dst, num_segments=num_nodes)
        key = jax.random.key(seed)
        k1, k2, k3, k4 = jax.random.split(key, 4)
        x = jax.random.normal(k1, (N_NODES, FEAT), dtype=jnp.float32)
        edge_index_with_loops = jax.random.randint(k2, (2, N_EDGES), 0, N_NODES, dtype=jnp.int32)
        deg_inv_sqrt = jax.random.uniform(k3, (N_NODES,), dtype=jnp.float32)
        weights = jax.random.normal(k4, (K, FEAT, FEAT), dtype=jnp.float32) * 0.01
        return {'x': x, 'edge_index_with_loops': edge_index_with_loops, 'deg_inv_sqrt': deg_inv_sqrt, 'num_nodes': N_NODES, 'weights': weights}
    _L3_gnn_all = _L3_gnn_setup()
    _L3_gnn_in = {k: v for k, v in _L3_gnn_all.items() if k in ('weights',)}
    del _L3_gnn_all
    return {'x': x, 'src': src, 'dst': dst, 'edge_attr_128': edge_attr_128, 'L0_gnn_W1': _L0_gnn_in['W1'], 'L0_gnn_b1': _L0_gnn_in['b1'], 'L0_gnn_W2': _L0_gnn_in['W2'], 'L0_gnn_b2': _L0_gnn_in['b2'], 'L1_gnn_W': _L1_gnn_in['W'], 'L1_gnn_att_src': _L1_gnn_in['att_src'], 'L1_gnn_att_dst': _L1_gnn_in['att_dst'], 'L1_gnn_bias': _L1_gnn_in['bias'], 'L2_gnn_W1': _L2_gnn_in['W1'], 'L2_gnn_b1': _L2_gnn_in['b1'], 'L2_gnn_W2': _L2_gnn_in['W2'], 'L2_gnn_b2': _L2_gnn_in['b2'], 'L2_gnn_W3': _L2_gnn_in['W3'], 'L2_gnn_b3': _L2_gnn_in['b3'], 'L2_gnn_gamma': _L2_gnn_in['gamma'], 'L2_gnn_beta': _L2_gnn_in['beta'], 'L3_gnn_weights': _L3_gnn_in['weights']}

def reference(x, src, dst, edge_attr_128, L0_gnn_W1, L0_gnn_b1, L0_gnn_W2, L0_gnn_b2, L1_gnn_W, L1_gnn_att_src, L1_gnn_att_dst, L1_gnn_bias, L2_gnn_W1, L2_gnn_b1, L2_gnn_W2, L2_gnn_b2, L2_gnn_W3, L2_gnn_b3, L2_gnn_gamma, L2_gnn_beta, L3_gnn_weights):
    import jax
    import jax.numpy as jnp

    def _L0_gnn_ref(x, edge_index, W1, b1, W2, b2):
        import jax, jax.numpy as jnp
        import numpy as np
        N_NODES = 50000
        N_HEDGES = 10000
        NNZ = 20000
        D_IN, D_HID, D_OUT = (128, 128, 128)

        def _glorot(key, fan_in, fan_out):
            s = jnp.sqrt(6.0 / (fan_in + fan_out)).astype(jnp.float32)
            return jax.random.uniform(key, (fan_in, fan_out), jnp.float32, -s, s)

        def _hconv(x, W, b, row, col):
            xw = x @ W
            ones = jnp.ones(row.shape[0], xw.dtype)
            deg_n = jax.ops.segment_sum(ones, row, num_segments=N_NODES)
            deg_e = jax.ops.segment_sum(ones, col, num_segments=N_HEDGES)
            d_inv = jnp.where(deg_n > 0, 1.0 / deg_n, 0.0)
            b_inv = jnp.where(deg_e > 0, 1.0 / deg_e, 0.0)
            m = jax.ops.segment_sum(xw[row], col, num_segments=N_HEDGES) * b_inv[:, None]
            out = jax.ops.segment_sum(m[col], row, num_segments=N_NODES) * d_inv[:, None]
            return out + b
        row, col = (edge_index[0], edge_index[1])
        h = jax.nn.relu(_hconv(x, W1, b1, row, col))
        return _hconv(h, W2, b2, row, col)

    def _L1_gnn_ref(x, edge_index, W, att_src, att_dst, bias):
        import jax, jax.numpy as jnp
        import numpy as np
        N_NODES = 3125
        N_EDGES = 50000
        IN_DIM = 128
        HEADS = 4
        OUT_DIM = 32
        NEG_SLOPE = 0.2
        N = x.shape[0]
        H, D = att_src.shape
        loop = jnp.arange(N, dtype=edge_index.dtype)
        src = jnp.concatenate([edge_index[0], loop])
        dst = jnp.concatenate([edge_index[1], loop])
        h = (x @ W).reshape(N, H, D)
        a_src = jnp.einsum('nhd,hd->nh', h, att_src)
        a_dst = jnp.einsum('nhd,hd->nh', h, att_dst)
        e = jax.nn.leaky_relu(a_src[src] + a_dst[dst], NEG_SLOPE)
        e_max = jax.ops.segment_max(e, dst, num_segments=N)
        e_max = jnp.where(jnp.isfinite(e_max), e_max, jnp.float32(0))
        ex = jnp.exp(e - e_max[dst])
        denom = jax.ops.segment_sum(ex, dst, num_segments=N)
        alpha = ex / (denom[dst] + jnp.float32(1e-16))
        msg = h[src] * alpha[:, :, None]
        out = jax.ops.segment_sum(msg, dst, num_segments=N)
        out = out.reshape(N, H * D) + bias
        return jax.nn.elu(out)

    def _L2_gnn_ref(node_feature, edge_matrix, edge_feature, W1, b1, W2, b2, W3, b3, gamma, beta):
        import jax, jax.numpy as jnp
        import numpy as np
        N_NODE = 50000
        N_EDGE = 625000
        FDIM = 128
        HID = 128
        EPS = 1e-05
        receiver_idx = edge_matrix[1]
        agg = jax.ops.segment_sum(edge_feature, receiver_idx, num_segments=node_feature.shape[0])
        x = jnp.concatenate([node_feature, agg], axis=-1)
        h = jax.nn.relu(x @ W1 + b1)
        h = jax.nn.relu(h @ W2 + b2)
        h = h @ W3 + b3
        mu = jnp.mean(h, axis=-1, keepdims=True)
        var = jnp.mean((h - mu) ** 2, axis=-1, keepdims=True)
        h = (h - mu) * jax.lax.rsqrt(var + EPS) * gamma + beta
        return h + node_feature

    def _L3_gnn_ref(x, edge_index_with_loops, deg_inv_sqrt, num_nodes, weights):
        import jax, jax.numpy as jnp
        import numpy as np
        N_NODES = 3125
        N_EDGES = 100000
        FEAT = 128
        K = 4

        def spmm(x, edge_index, deg_inv_sqrt, num_nodes):
            src, dst = (edge_index[0], edge_index[1])
            norm = deg_inv_sqrt[src] * deg_inv_sqrt[dst]
            msg = x[src] * norm[:, None]
            return jax.ops.segment_sum(msg, dst, num_segments=num_nodes)
        Kk = weights.shape[0]
        T = [x]
        if Kk > 1:
            T.append(spmm(x, edge_index_with_loops, deg_inv_sqrt, num_nodes))
        for k in range(2, Kk):
            T.append(2.0 * spmm(T[k - 1], edge_index_with_loops, deg_inv_sqrt, num_nodes) - T[k - 2])
        Ts = jnp.stack(T, axis=0)
        return jnp.einsum('knf,kfo->no', Ts, weights)
    edge_index = jnp.stack([src, dst])
    deg = jnp.maximum(jax.ops.segment_sum(jnp.ones(dst.shape, jnp.float32), dst, num_segments=50000), 1.0)
    deg_isqrt = deg ** (-0.5)
    x = _layernorm(x + _L0_gnn_ref(x, edge_index, L0_gnn_W1, L0_gnn_b1, L0_gnn_W2, L0_gnn_b2), axis=-1)
    x = _layernorm(x + _L1_gnn_ref(x, edge_index, L1_gnn_W, L1_gnn_att_src, L1_gnn_att_dst, L1_gnn_bias), axis=-1)
    x = _layernorm(x + _L2_gnn_ref(x, edge_index, edge_attr_128, L2_gnn_W1, L2_gnn_b1, L2_gnn_W2, L2_gnn_b2, L2_gnn_W3, L2_gnn_b3, L2_gnn_gamma, L2_gnn_beta), axis=-1)
    x = _layernorm(x + _L3_gnn_ref(x, edge_index, deg_isqrt, 50000, L3_gnn_weights), axis=-1)
    return x

_drawn_inputs = setup_inputs


def setup_inputs(seed=0):
    import zlib

    import numpy as np

    out = dict(_drawn_inputs(seed))
    spreads = {'L0_gnn_b1': (0.0, 0.1),
     'L0_gnn_b2': (0.0, 0.1),
     'L1_gnn_bias': (0.0, 0.1),
     'L2_gnn_gamma': (1.0, 0.2),
     'L2_gnn_beta': (0.0, 0.1)}
    factors = {}
    for name, (base, spread) in spreads.items():
        noise = np.random.default_rng([zlib.crc32(name.encode()), seed]).standard_normal(out[name].shape)
        drawn = base * np.exp(spread * noise) if base else spread * noise
        out[name] = jnp.asarray(drawn.astype(out[name].dtype))
    for name, factor in factors.items():
        out[name] = (out[name] * factor).astype(out[name].dtype)
    return out
```

```python
import numpy as np
import concourse.bass as bass
from concourse import mybir
from contextlib import ExitStack

FP32 = mybir.dt.float32
FP16 = mybir.dt.float16
BF16 = mybir.dt.bfloat16
I32 = mybir.dt.int32
ALU = mybir.AluOpType
ACT = mybir.ActivationFunctionType
AX = mybir.AxisListType

N = 50000
E = 50000
D = 128
P = 128
TN = 100
GT = 4
GN = TN * GT
T = N // TN
G = N // GN
HE = 10000
HG = HE // GN
NJ = 400
EP = P * NJ
JB = NJ // GT
PAD = 60000
HA, HB = 25, 20
MAGIC = 12582912.0
BIG = 1.0e30
HEADS, HD = 4, 32
TW = D + 2 * HEADS
EPS = 1e-5


class Mem:

    def __init__(self, nc, ctx, phase):
        self.nc, self.ctx, self.phase, self.sems = nc, ctx, phase, []
        ctx.callback(self.clear)

    def sb(self, name, shape, dt=FP32):
        return self.ctx.enter_context(self.nc.sbuf_tensor(f"{self.phase}_{name}", shape, dt))

    def ps(self, name, shape, dt=FP32):
        return self.ctx.enter_context(self.nc.psum_tensor(f"{self.phase}_{name}", shape, dt))

    def sem(self, name):
        self.sems.append(self.nc.alloc_semaphore(f"{self.phase}_{name}"))
        return self.sems[-1]

    def clear(self):
        self.nc.clear_and_free_semaphores(self.sems)
        self.nc.all_engine_barrier()


def prep_phase(nc, K, edges, row_dram, bin_dram, by_src):
    with ExitStack() as ctx:
        m = Mem(nc, ctx, "prep")
        passed = m.sem("passed")
        pa = m.sb("pa", [P, NJ, 2], I32)
        pb = m.sb("pb", [JB, GT, P, 2], I32)
        srcf = m.sb("srcf", [P, NJ])
        dstf = m.sb("dstf", [P, NJ])
        grp = m.sb("grp", [P, NJ])
        rem = m.sb("rem", [P, NJ])
        io16 = m.sb("io16", [P, GN], FP16)
        dgrp = m.sb("dgrp", [P, NJ])
        drem = m.sb("drem", [P, NJ])
        ohk = m.sb("ohk", [P, NJ, G], BF16)
        og = m.sb("og", [P, 4, P], BF16)
        orr = m.sb("orr", [P, 4, GN], BF16)
        rs = m.sb("rs", [JB, GT, P])
        rd = m.sb("rd", [JB, GT, P])
        rk = m.sb("rk", [JB, GT, P])
        rl = m.sb("rl", [JB, GT, P])
        kcol = m.sb("kcol", [P, NJ])
        pay = m.sb("pay", [P, NJ, 2], I32)
        curp = m.sb("curp", [P, 4, 1], I32)
        curv = m.sb("curv", [P, 4, 2], I32)
        hist = m.sb("hist", [G, GT])
        hscan = m.sb("hscan", [G, GT])
        histn = m.sb("histn", [G, GN])
        cnt = m.sb("cnt", [G, NJ])
        scan = m.sb("scan", [G, NJ])
        binb = m.sb("binb", [G, 1])
        baset = m.sb("baset", [JB, GT, G])
        prod = m.sb("prod", [P, 4, G])
        pos = m.sb("pos", [P, NJ])
        posi = m.sb("posi", [P, NJ], I32)
        histd = m.sb("histd", [G, GN])
        rowi = m.sb("rowi", [G, GT], I32)
        cnti = m.sb("cnti", [G, GT], I32)
        bini = m.sb("bini", [G, 2], I32)
        small = m.sb("small", [P, 4])
        nlow = m.sb("nlow", [1, 4])
        nlowi = m.sb("nlowi", [1, 1], I32)
        blank = m.sb("blank", [P, NJ, 2], I32)
        p_h = m.ps("p_h", [G, GN])
        p_d = m.ps("p_d", [G, GN])
        p_c = m.ps("p_c", [G, NJ])
        p_t = [m.ps(f"p_t{i}", [P, 512]) for i in range(2)]
        p_r = [m.ps(f"p_r{i}", [P, 512]) for i in range(2)]
        s_ld = m.sem("load")
        s_v = m.sem("dve")
        s_pe = m.sem("pe")
        s_og = m.sem("onehot_src")
        s_ogu = m.sem("onehot_src_used")
        s_io = m.sem("iota")
        s_rank = m.sem("rank")
        s_pos = m.sem("pos")
        s_scat = [m.sem(f"scatter{i}") for i in range(4)]
        s_cur = m.sem("scatter_operands")
        s_st = m.sem("store")
        s_bl = m.sem("blank_list")
        with nc.Block() as block:
            at = {}

            @block.sync
            def _(sp):
                sp.dma_start(pa[:, :, :], edges.rearrange("(p j) c -> p j c", p=P)).then_inc(s_ld, 16)
                sp.dma_start(pb[:, :, :, :], edges.rearrange("(b q p) c -> q b p c", b=GT, q=JB)).then_inc(s_ld, 16)
                sp.wait_ge(s_io, 3)
                sp.dma_start(by_src.rearrange("(p j) c -> p j c", p=P), blank[:, :, :]).then_inc(s_bl, 16)
                sp.wait_ge(s_bl, 16)
                sp.wait_ge(s_st, 1)
                sp.dma_start(row_dram[0, :].rearrange("(a b) -> a b", a=G), rowi[:, :]).then_inc(s_st, 16)
                sp.dma_start(row_dram[1, :].rearrange("(a b) -> a b", a=G), cnti[:, :]).then_inc(s_st, 16)
                sp.wait_ge(s_st, 34)
                sp.dma_start(bin_dram.rearrange("c g -> g c"), bini[:, :], allow_slow_non_contiguous=True).then_inc(s_st, 16)
                sp.wait_ge(s_st, 50)

            @block.gpsimd
            def _(pool):
                nc.gpsimd.iota(io16[:, :], [[1, GN]], 0, 0, allow_small_or_imprecise_dtypes=True).then_inc(s_io, 1)
                nc.gpsimd.memset(blank[:, :, 1:2], 0).then_inc(s_io, 1)
                nc.gpsimd.memset(blank[:, :, 0:1], PAD).then_inc(s_io, 1)
                pool.wait_ge(s_bl, 16)
                pool.wait_ge(s_pos, 1)
                quads = pool.value_load(nlowi[0:1, 0:1], min_val=1, max_val=JB)
                with pool.Fori(0, quads) as i:
                    alone(pool, s_cur, i + 1, passed)
                    for c in range(4):
                        pool.indirect_dma_start(by_src[:, :], bass.IndirectOffsetOnAxis(ap=curp[:, c, :], axis=0),
                                                curv[:, c, :], None, bounds_check=E - 1, oob_is_err=False)\
                            .then_inc(s_scat[c], 16)
                for c in range(4):
                    alone(pool, s_scat[c], 16 * quads, passed)

            @block.scalar
            def _(act):
                act.wait_ge(s_pos, 1)
                quads = act.value_load(nlowi[0:1, 0:1], min_val=1, max_val=JB)
                with act.Fori(0, 1) as _one:
                    nc.scalar.copy(curp[:, :, 0], posi[:, 0:4])
                    nc.scalar.copy(curv[:, :, :], pay[:, 0:4, :]).then_inc(s_cur, 1)
                with act.If(quads > 1):
                    with act.Fori(1, quads) as i:
                        for c in range(4):
                            act.wait_ge(s_scat[c], 16 * i)
                        nc.scalar.copy(curp[:, :, 0], posi[:, bass.ds(4 * i, 4)])
                        nc.scalar.copy(curv[:, :, :], pay[:, bass.ds(4 * i, 4), :]).then_inc(s_cur, 1)

            @block.vector
            def _(dve):
                n = [0]

                def seq(ins):
                    n[0] += 1
                    ins.then_inc(s_v, 1)
                    dve.wait_ge(s_v, n[0])

                def whole(out, x, a, b):
                    seq(nc.vector.tensor_scalar(out, x, a, b, ALU.mult, ALU.add))
                    seq(nc.vector.tensor_scalar(out, out, MAGIC, -MAGIC, ALU.add, ALU.add))

                dve.wait_ge(s_ld, 32)
                dve.wait_ge(s_io, 1)
                seq(nc.vector.tensor_copy(srcf[:, :], pa[:, :, 0]))
                seq(nc.vector.tensor_copy(dstf[:, :], pa[:, :, 1]))
                whole(dgrp[:, :], dstf[:, :], 1.0 / GN, 0.5 / GN - 0.5)
                seq(nc.vector.scalar_tensor_tensor(drem[:, :], dgrp[:, :], -float(GN), dstf[:, :], ALU.mult, ALU.add))
                with dve.Fori(0, JB) as i:
                    dve.wait_ge(s_ogu, 4 * i + 1)
                    for c in range(4):
                        nc.vector.tensor_scalar(og[:, c, 0:G], io16[:, 0:G], dgrp[:, bass.ds(4 * i + c, 1)], None, ALU.is_equal)
                        nc.vector.tensor_scalar(orr[:, c, :], io16[:, :], drem[:, bass.ds(4 * i + c, 1)], None,
                                                ALU.is_equal).then_inc(s_og, 1)
                whole(grp[:, :], srcf[:, :], 1.0 / GN, 0.5 / GN - 0.5)
                seq(nc.vector.scalar_tensor_tensor(rem[:, :], grp[:, :], -float(GN), srcf[:, :], ALU.mult, ALU.add))
                seq(nc.vector.tensor_copy(rs[:, :, :], pb[:, :, :, 0]))
                seq(nc.vector.tensor_copy(rd[:, :, :], pb[:, :, :, 1]))
                whole(rk[:, :, :], rs[:, :, :], 1.0 / GN, 0.5 / GN - 0.5)
                seq(nc.vector.tensor_scalar(rl[:, :, :], rd[:, :, :], float(HE - 1), 1000.0, ALU.is_ge, ALU.mult))
                seq(nc.vector.tensor_tensor(rk[:, :, :], rk[:, :, :], rl[:, :, :], ALU.add))
                at["rows"] = n[0]
                for x in range(3):
                    dve.wait_ge(s_pe, x + 2)
                    if x < 2:
                        seq(nc.vector.tensor_copy(pay[:, :, x], p_t[x % 2][:, 0:NJ]))
                    else:
                        seq(nc.vector.tensor_copy(kcol[:, :], p_t[x % 2][:, 0:NJ]))
                    at[f"evac{x}"] = n[0]
                seq(nc.vector.tensor_tensor(ohk[:, :, :], kcol[:, :].unsqueeze(2).to_broadcast([P, NJ, G]),
                                            io16[:, 0:G].unsqueeze(1).to_broadcast([P, NJ, G]), ALU.is_equal))
                at["key_onehots"] = n[0]
                dve.wait_ge(s_pe, 1)
                seq(nc.vector.tensor_copy(histn[:, :], p_h[:, :]))
                seq(nc.vector.tensor_reduce(hist[:, :], histn[:, :].rearrange("g (t n) -> g t n", t=GT), AX.X, ALU.add))
                seq(nc.vector.tensor_tensor_scan(hscan[:, :], hist[:, :], hist[:, :], 0.0, ALU.add, ALU.bypass))
                at["hist"] = n[0]
                dve.wait_ge(s_pe, 5)
                seq(nc.vector.tensor_copy(K["deg_dst"][:, :].rearrange("p (g t) -> p t g", t=GT),
                                          p_t[0][0:TN, 0:GT * G].rearrange("p (t g) -> p t g", t=GT)))
                at["deg_dst"] = n[0]
                seq(nc.vector.tensor_copy(small[0:G, 1:2], p_t[0][0:G, 501:502]))
                seq(nc.vector.tensor_scalar(hscan[:, :], hscan[:, :], small[0:G, 1:2], None, ALU.add))
                seq(nc.vector.tensor_tensor(hscan[:, :], hscan[:, :], hist[:, :], ALU.subtract))
                seq(nc.vector.tensor_copy(rowi[:, :], hscan[:, :]))
                whole(hist[:, :], hist[:, :], 1.0 / P, -1.0 / P + 0.5 / P - 0.5)
                seq(nc.vector.tensor_scalar(hist[:, :], hist[:, :], 0.0, None, ALU.max))
                seq(nc.vector.tensor_copy(cnti[:, :], hist[:, :]))
                nc.vector.memset(small[:, 3:4], 0.0).then_inc(s_st, 1)
                dve.wait_ge(s_pe, 6)
                seq(nc.vector.tensor_copy(cnt[:, :], p_c[:, :]))
                seq(nc.vector.tensor_tensor_scan(scan[:, :], cnt[:, :], cnt[:, :], 0.0, ALU.add, ALU.bypass))
                at["scan"] = n[0]
                dve.wait_ge(s_pe, 7)
                seq(nc.vector.tensor_copy(binb[:, :], p_t[1][0:G, 500:501]))
                seq(nc.vector.tensor_tensor(cnt[:, :], scan[:, :], cnt[:, :], ALU.subtract))
                seq(nc.vector.tensor_scalar(cnt[:, :], cnt[:, :], binb[:, 0:1], None, ALU.add))
                at["base"] = n[0]
                seq(nc.vector.tensor_copy(bini[:, 0:1], binb[:, :]))
                whole(binb[:, :], scan[:, NJ - 1:NJ], 1.0 / P, -1.0 / P + 0.5 / P - 0.5)
                seq(nc.vector.tensor_scalar(binb[:, :], binb[:, :], 0.0, None, ALU.max))
                seq(nc.vector.tensor_copy(bini[:, 1:2], binb[:, :]))
                nc.vector.memset(small[:, 2:3], 0.0).then_inc(s_st, 1)
                dve.wait_ge(s_pe, 8)
                seq(nc.vector.tensor_copy(baset[:, :, :], p_t[0][0:JB, 0:GT * G].rearrange("q (b g) -> q b g", b=GT)))
                at["baset"] = n[0]
                seq(nc.vector.tensor_scalar(rl[:, :, :], rd[:, :, :], float(HE - 1), None, ALU.is_lt))
                seq(nc.vector.tensor_reduce(small[0:JB, 0:1], rl[:, :, :].rearrange("q b p -> q (b p)"), AX.X, ALU.add))
                at["nlow"] = n[0]
                dve.wait_ge(s_pe, 9)
                seq(nc.vector.tensor_copy(nlow[:, 0:1], p_t[1][0:1, 501:502]))
                whole(nlow[:, 0:1], nlow[:, 0:1], 0.25 / P, 0.5 - 0.125 / P)
                seq(nc.vector.tensor_scalar(nlow[:, 0:1], nlow[:, 0:1], 1.0, None, ALU.max))
                seq(nc.vector.tensor_copy(nlowi[:, :], nlow[:, 0:1]))
                for i in range(JB):
                    dve.wait_ge(s_rank, i + 1)
                    seq(nc.vector.tensor_tensor(prod[:, :, :], ohk[:, 4 * i:4 * i + 4, :],
                                                p_r[i % 2][:, 0:4 * G].rearrange("p (c g) -> p c g", c=4), ALU.mult))
                    at[f"prod{i}"] = n[0]
                    seq(nc.vector.tensor_reduce(pos[:, 4 * i:4 * i + 4], prod[:, :, :], AX.X, ALU.add))
                seq(nc.vector.tensor_scalar(kcol[:, :], kcol[:, :], float(G), 1.0e6, ALU.is_ge, ALU.mult))
                seq(nc.vector.tensor_tensor(pos[:, :], pos[:, :], kcol[:, :], ALU.add))
                nc.vector.tensor_copy(posi[:, :], pos[:, :]).then_inc(s_pos, 1)
                with dve.Fori(0, JB) as i:
                    dve.wait_ge(s_ogu, 4 * i + NJ + 2)
                    for c in range(4):
                        nc.vector.tensor_scalar(og[:, c, 0:G], io16[:, 0:G], grp[:, bass.ds(4 * i + c, 1)], None, ALU.is_equal)
                        nc.vector.tensor_scalar(orr[:, c, :], io16[:, :], rem[:, bass.ds(4 * i + c, 1)], None,
                                                ALU.is_equal).then_inc(s_og, 1)
                dve.wait_ge(s_pe, 10)
                seq(nc.vector.tensor_copy(histd[:, :], p_d[:, :]))
                at["histd"] = n[0]
                dve.wait_ge(s_pe, 11)
                nc.vector.tensor_copy(K["deg_src"][:, :].rearrange("p (g t) -> p t g", t=GT),
                                      p_t[0][0:TN, 0:GT * G].rearrange("p (t g) -> p t g", t=GT))

            @block.tensor
            def _(pe):
                idn, ones_bf, ltri_bf = K["ident"], K["ones_bf"], K["ltri_bf"]

                def count_nodes(pe, out, used):
                    nc.tensor.matmul(out[:, :], K["zeros_bf"][:, 0:G], K["zeros_bf"][:, 0:1].to_broadcast([P, GN]),
                                     start=True, stop=False).then_inc(s_ogu, 1)
                    seen = used - 1 if used else 0
                    with pe.Fori(0, JB) as i:
                        for c in range(4):
                            pe.wait_ge(s_og, 4 * i + c + 1 + seen)
                            nc.tensor.matmul(out[:, :], og[:, c, 0:G], orr[:, c, :], start=False, stop=False).then_inc(s_ogu, 1)
                    nc.tensor.matmul(out[:, :], K["zeros_bf"][:, 0:G], K["zeros_bf"][:, 0:1].to_broadcast([P, GN]),
                                     start=False, stop=True).then_inc(s_pe, 1)

                count_nodes(pe, p_h, 0)
                pe.wait_ge(s_v, at["rows"])
                for x, rows in enumerate((rs, rd, rk)):
                    if x == 2:
                        pe.wait_ge(s_v, at["evac0"])
                    for b in range(GT):
                        last = nc.tensor.transpose(p_t[x % 2][:, b * JB:(b + 1) * JB], rows[:, b, :], idn[0:JB, 0:JB])
                    last.then_inc(s_pe, 1)
                pe.wait_ge(s_v, at["hist"])
                for b in range(GT):
                    nc.tensor.transpose(p_t[0][0:TN, b * G:(b + 1) * G], histn[:, b * TN:(b + 1) * TN], idn[0:G, 0:G])
                nc.tensor.matmul(p_t[0][0:G, 501:502], K["ltri"][0:G, 0:G], hscan[:, GT - 1:GT], start=True, stop=True).then_inc(s_pe, 1)
                pe.wait_ge(s_v, at["key_onehots"])
                for j in range(NJ):
                    last = nc.tensor.matmul(p_c[:, j:j + 1], ohk[:, j, :], ones_bf[:, 0:1], start=True, stop=True)
                last.then_inc(s_pe, 1)
                pe.wait_ge(s_v, at["scan"])
                nc.tensor.matmul(p_t[1][0:G, 500:501], K["ltri"][0:G, 0:G], scan[:, NJ - 1:NJ], start=True, stop=True).then_inc(s_pe, 1)
                pe.wait_ge(s_v, at["base"])
                for b in range(GT):
                    last = nc.tensor.transpose(p_t[0][0:JB, b * G:(b + 1) * G], cnt[:, b * JB:(b + 1) * JB], idn[0:G, 0:G])
                last.then_inc(s_pe, 1)
                pe.wait_ge(s_v, at["nlow"])
                nc.tensor.matmul(p_t[1][0:1, 501:502], small[0:JB, 0:1], K["ones"][0:JB, 0:1], start=True, stop=True).then_inc(s_pe, 1)
                for i in range(JB):
                    if i >= 2:
                        pe.wait_ge(s_v, at[f"prod{i - 2}"])
                    nc.tensor.matmul(p_r[i % 2][:, 0:4 * G], ltri_bf[:, :],
                                     ohk[:, 4 * i:4 * i + 4, :].rearrange("p c g -> p (c g)"), start=True, stop=False)
                    for c in range(4):
                        b, q = divmod(4 * i + c, JB)
                        last = nc.tensor.matmul(p_r[i % 2][:, c * G:(c + 1) * G], idn[0:JB, q:q + 1].to_broadcast([JB, P]),
                                                baset[:, b, :], start=False, stop=c == 3)
                    last.then_inc(s_rank, 1)
                count_nodes(pe, p_d, NJ + 1)
                pe.wait_ge(s_v, at["histd"])
                for b in range(GT):
                    last = nc.tensor.transpose(p_t[0][0:TN, b * G:(b + 1) * G], histd[:, b * TN:(b + 1) * TN], idn[0:G, 0:G])
                last.then_inc(s_pe, 1)


def constants_phase(nc, K):
    with ExitStack() as ctx:
        m = Mem(nc, ctx, "const")
        passed = m.sem("passed")
        s_m = m.sem("memset")
        s_d = m.sem("done")
        with nc.Block() as block:
            @block.gpsimd
            def _(pool):
                nc.gpsimd.memset(K["ident"][:, :], 0.0).then_inc(s_m, 1)
                nc.gpsimd.memset(K["ltri"][:, :], 1.0).then_inc(s_m, 1)
                nc.gpsimd.memset(K["ones"][:, :], 1.0).then_inc(s_m, 1)
                nc.gpsimd.memset(K["eps"][:, :], EPS).then_inc(s_m, 1)
                nc.gpsimd.memset(K["ones_bf"][:, :], 1.0).then_inc(s_m, 1)
                nc.gpsimd.memset(K["zeros_bf"][:, :], 0.0).then_inc(s_m, 1)
                nc.gpsimd.iota(K["iota"][:, :], [[1, GN]], 0, 0, allow_small_or_imprecise_dtypes=True).then_inc(s_m, 1)
                nc.gpsimd.iota(K["tbase"][:, :], [[TN, T]], 0, 0, allow_small_or_imprecise_dtypes=True).then_inc(s_m, 1)
                pool.wait_ge(s_m, 8)
                nc.gpsimd.affine_select(out=K["ident"][:, :], in_=K["ident"][:, :], compare_op=ALU.not_equal, fill=1.0,
                                        base=0, pattern=[[-1, P]], channel_multiplier=1).then_inc(s_d, 1)
                nc.gpsimd.affine_select(out=K["ltri"][:, :], in_=K["ltri"][:, :], compare_op=ALU.is_gt, fill=0.0,
                                        base=0, pattern=[[1, P]], channel_multiplier=-1).then_inc(s_d, 1)

            @block.vector
            def _(dve):
                dve.wait_ge(s_d, 2)
                nc.vector.tensor_copy(K["ltri_bf"][:, :], K["ltri"][:, :]).then_inc(s_d, 1)
                dve.wait_ge(s_d, 3)



def index_phase(nc, K, t):
    with ExitStack() as ctx:
        m = Mem(nc, ctx, "index")
        passed = m.sem("passed")
        row = m.sb("row", [1, 2, T], I32)
        bins = m.sb("bins", [1, 2, G], I32)
        de = m.sb("de", [P, T, 2], I32)
        se = m.sb("se", [P, G, 2], I32)
        f = m.sb("f", [P, T])
        s_row = m.sem("rows")
        s_de = m.sem("dst_chunks")
        s_se = m.sem("src_chunks")
        s_v = m.sem("dve")
        s_deg = m.sem("degree")
        s_isq = m.sem("inverse_root")
        with nc.Block() as block:
            @block.sync
            def _(sp):
                sp.dma_start(row[:, :, :], t["row_dram"].unsqueeze(0)).then_inc(s_row, 16)
                sp.dma_start(bins[:, :, :], t["bin_dram"].unsqueeze(0)).then_inc(s_row, 16)
                sp.wait_ge(s_row, 32)
                with sp.Fori(0, G) as g:
                    for c in range(GT):
                        first = sp.value_load(row[0:1, 0, bass.ds(GT * g + c, 1)], min_val=0, max_val=E)
                        sp.dma_start(de[:, bass.ds(GT * g + c, 1), :].rearrange("p o c -> p (o c)"),
                                     t["edges"][bass.ds(first, P), :]).then_inc(s_de, 16)

            @block.scalar
            def _(act):
                act.wait_ge(s_row, 32)
                with act.Fori(0, G) as g:
                    first = act.value_load(bins[0:1, 0, bass.ds(g, 1)], min_val=0, max_val=E)
                    act.dma_start(se[:, bass.ds(g, 1), :].rearrange("p o c -> p (o c)"),
                                  t["by_src"][bass.ds(first, P), :]).then_inc(s_se, 16)
                act.wait_ge(s_deg, 1)
                nc.scalar.activation(K["isq"][:, :], K["inv_dst"][:, :], ACT.Sqrt).then_inc(s_isq, 1)
                act.wait_ge(s_isq, 1)

            @block.vector
            def _(dve):
                n = [0]

                def seq(ins):
                    n[0] += 1
                    ins.then_inc(s_v, 1)
                    dve.wait_ge(s_v, n[0])

                dve.wait_ge(s_row, 32)
                seq(nc.vector.tensor_copy(K["starts"][:, :], row[:, 0, :]))
                seq(nc.vector.tensor_copy(K["bstarts"][:, :], bins[:, 0, :]))
                seq(nc.vector.tensor_reduce(K["more_dst"][:, :], row[:, 1, :].rearrange("o (g c) -> o g c", c=GT), AX.X, ALU.max))
                seq(nc.vector.tensor_copy(K["more_src"][:, :], bins[:, 1, :]))
                seq(nc.vector.tensor_scalar(f[0:TN, :], K["deg_dst"][:, :], 1.0, None, ALU.max))
                nc.vector.reciprocal(K["inv_dst"][:, :], f[0:TN, :]).then_inc(s_deg, 1)
                dve.wait_ge(s_isq, 1)
                seq(nc.vector.tensor_tensor(f[0:TN, :], f[0:TN, :], K["isq"][:, :], ALU.mult))
                seq(nc.vector.tensor_tensor(f[0:TN, :], f[0:TN, :], K["isq"][:, :], ALU.mult))
                seq(nc.vector.tensor_scalar(f[0:TN, :], f[0:TN, :], -0.5, 1.5, ALU.mult, ALU.add))
                seq(nc.vector.tensor_tensor(K["isq"][:, :], K["isq"][:, :], f[0:TN, :], ALU.mult))
                seq(nc.vector.tensor_scalar(f[0:TN, :], K["deg_src"][:, :], 1.0, None, ALU.max))
                seq(nc.vector.reciprocal(K["inv_src"][:, :], f[0:TN, :]))
                dve.wait_ge(s_se, 16 * G)
                seq(nc.vector.tensor_copy(f[:, 0:G], se[:, :, 0]))
                seq(nc.vector.tensor_tensor(K["rel_src"][:, :], f[:, 0:G], K["tbase"][:, 0:T:GT], ALU.subtract))
                seq(nc.vector.tensor_copy(K["idx_src"][:, :], se[:, :, 1]))
                dve.wait_ge(s_de, 16 * T)
                seq(nc.vector.tensor_copy(f[:, :], de[:, :, 1]))
                seq(nc.vector.tensor_tensor(K["rel_dst"][:, :], f[:, :], K["tbase"][:, :], ALU.subtract))
                seq(nc.vector.tensor_scalar(K["idx_dst"][:, :], de[:, :, 0], N - 1, None, ALU.min))


def groups(eng, n, body):
    body(0, 0)
    body(1, 1)
    with eng.Fori(1, (n - 1) // 2) as i:
        body(2 * i, 0)
        body(2 * i + 1, 1)
    body(n - 1, 0)


def wait(eng, sem, value):
    if not isinstance(value, int) or value > 0:
        eng.wait_ge(sem, value)


def at_most(eng, value, top):
    return (value - (value - top) * (value > top)).with_bounds(min_val=0, max_val=top)


def alone(eng, sem, value, passed):
    if not isinstance(value, int) or value > 0:
        eng.wait_ge(sem, value)
        eng.sem_inc(passed, 1)


class Counter:

    def __init__(self, eng):
        self.eng = eng
        self.reg = eng.alloc_register()
        eng.reg_mov(self.reg, 0)

    def next(self):
        before = self.eng.snap(self.reg, min_val=0, max_val=1 << 20)
        self.eng.reg_add(self.reg, self.reg, 1)
        return before


class Overflow:

    def __init__(self, nc, m, K, t, table, width):
        self.nc, self.K, self.t, self.table, self.width = nc, K, t, table, width
        self.e = m.sb("over_e", [P, GT, 2], I32)
        self.i = m.sb("over_i", [P, GT, 1], I32)
        self.f = m.sb("over_f", [P, GT])
        self.M = m.sb("over_M", [P, GT, TN])
        self.V = m.sb("over_V", [P, GT, width])
        self.s_e = m.sem("over_edges")
        self.s_f = m.sem("over_float")
        self.s_r = m.sem("over_rel")
        self.s_hot = m.sem("over_onehot")
        self.s_g = m.sem("over_gather")
        self.s_mm = m.sem("over_sum")
        self.s_done = m.sem("over_added")


def layer_norm(nc, dve, seq, x, stats, mv, out, s_var, s_std, n, passed):
    for c in range(GT):
        last = nc.vector.bn_stats(stats[:, c, :], x[:, c, :])
    seq(last)
    dve.sem_inc(passed, 1)
    for c in range(GT):
        last = nc.vector.bn_aggr(mv[:, c, :], stats[:, c, :])
    last.then_inc(s_var, 1)
    dve.wait_ge(s_std, n)
    seq(nc.vector.reciprocal(mv[:, :, 1], mv[:, :, 1]))
    seq(nc.vector.tensor_tensor(out, x, mv[:, :, 0:1].to_broadcast([TN, GT, D]), ALU.subtract))
    return nc.vector.tensor_tensor(out, out, mv[:, :, 1:2].to_broadcast([TN, GT, D]), ALU.mult)


def deviation(nc, act, K, mv, s_var, s_std, g):
    act.wait_ge(s_var, g + 1)
    nc.scalar.activation(mv[:, :, 1], mv[:, :, 1], ACT.Sqrt, bias=K["eps"][0:TN, 0:1]).then_inc(s_std, 1)


def sums_pass(nc, K, t, name, n, table, weight, out, scale=None, read_r=None, write_r=None,
              minus=None, twice=1.0, norm=False):
    cheb = read_r is not None
    with ExitStack() as ctx:
        m = Mem(nc, ctx, name)
        passed = m.sem("passed")
        V = m.sb("V", [P, 2, GT, D])
        M = m.sb("M", [P, 2, GT, TN])
        cur = m.sb("cur", [P, 2, GT, 1], I32)
        ST = m.sb("ST", [D, 2, GN])
        R = m.sb("R", [TN, 2, GT, D])
        Y = m.sb("Y", [TN, 2, GT, D])
        yo = m.sb("yo", [TN, 2, GT, D])
        tmp = m.sb("tmp", [TN, GT, D])
        stats = m.sb("stats", [TN, GT, 6])
        mv = m.sb("mv", [TN, GT, 2])
        o = Overflow(nc, m, K, t, table, D)
        pst = [m.ps(f"pst{i}", [P, 512]) for i in range(2)]
        pout = [m.ps(f"pout{i}", [P, 512]) for i in range(2)]
        psn = [m.ps(f"psn{i}", [P, 512]) for i in range(2)]
        pov = m.ps("pov", [P, 512])
        s_cur = m.sem("indices")
        s_g = [m.sem(f"gathered{i}") for i in range(2)]
        s_hot = m.sem("onehot")
        s_sum = m.sem("summed")
        s_ev = m.sem("sum_in_sbuf")
        s_pr = m.sem("projected")
        s_ch = m.sem("dve_chain")
        s_fin = m.sem("finished")
        s_var = m.sem("variance")
        s_std = m.sem("deviation")
        s_ld = [m.sem(f"loaded{i}") for i in range(2)]
        s_st = [m.sem(f"stored{i}") for i in range(2)]
        loads = (1 if cheb else 0) + (1 if minus is not None else 0)
        stores = 1 + (1 if write_r is not None else 0)

        def rows(a, g):
            return a[bass.ds(g * GN, GN), :].rearrange("(c p) d -> p c d", p=TN)

        def scal(a, g):
            return a[:, bass.ds(GT * g, GT)].unsqueeze(2).to_broadcast([TN, GT, D])

        with nc.Block() as block:
            @block.gpsimd
            def _(pool):
                counter = Counter(pool)

                def overflow(g):
                    more = pool.value_load(K["more_dst"][0:1, bass.ds(g, 1)], min_val=0, max_val=NJ)
                    with pool.If(more > 0):
                        with pool.Fori(0, more) as c:
                            k = counter.next() + 1
                            for x in range(GT):
                                first = pool.value_load(K["starts"][0:1, bass.ds(GT * g + x, 1)], min_val=0, max_val=E)
                                at = at_most(pool, first + (c + 1) * P, E)
                                pool.dma_start(o.e[:, x, :], t["edges"][bass.ds(at, P), :]).then_inc(o.s_e, 16)
                            alone(pool, o.s_hot, k, passed)
                            for x in range(GT):
                                pool.indirect_dma_start(o.V[:, x, :], None, table[:, :],
                                                        bass.IndirectOffsetOnAxis(ap=o.i[:, x, :], axis=0)).then_inc(o.s_g, 16)
                            alone(pool, o.s_done, k, passed)

                def body(g, b):
                    alone(pool, s_sum, g - 1, passed)
                    alone(pool, s_cur, g + 1, passed)
                    for x in range(GT):
                        pool.indirect_dma_start(V[:, b, x, :], None, table[:, :],
                                                bass.IndirectOffsetOnAxis(ap=cur[:, b, x, :], axis=0)).then_inc(s_g[b], 16)
                    overflow(g)
                groups(pool, n, body)

            @block.scalar
            def _(act):
                def indices(g, b):
                    wait(act, s_sum, g - 1)
                    nc.scalar.copy(cur[:, b, :, 0], K["idx_dst"][:, bass.ds(GT * g, GT)]).then_inc(s_cur, 1)

                def body(g, b):
                    indices(g, b)
                    act.wait_ge(s_sum, g + 1)
                    wait(act, s_pr, g - 1)
                    nc.scalar.copy(ST[:, b, :], pst[b][:, 0:GN]).then_inc(s_ev, 1)
                    if norm:
                        deviation(nc, act, K, mv, s_var, s_std, g)
                groups(act, n, body)

            @block.tensor
            def _(pe):
                counter = Counter(pe)

                def body(g, b):
                    use = g // 2 if isinstance(g, int) else None
                    pe.wait_ge(s_g[b], 64 * (use + 1) if use is not None else 32 * (g - b) + 64)
                    pe.wait_ge(s_hot, g + 1)
                    wait(pe, s_ev, g - 1)
                    for x in range(GT):
                        last = nc.tensor.matmul(pst[b][:, x * TN:(x + 1) * TN], V[:, b, x, :], M[:, b, x, :], start=True, stop=True)
                    last.then_inc(s_sum, 1)
                    more = pe.value_load(K["more_dst"][0:1, bass.ds(g, 1)], min_val=0, max_val=NJ)
                    with pe.If(more > 0):
                        with pe.Fori(0, more) as c:
                            k = counter.next() + 1
                            pe.wait_ge(o.s_g, k * 64)
                            for x in range(GT):
                                last = nc.tensor.matmul(pov[:, x * TN:(x + 1) * TN], o.V[:, x, :], o.M[:, x, :], start=True, stop=True)
                            last.then_inc(o.s_mm, 1)
                            pe.wait_ge(o.s_done, k)
                    pe.wait_ge(s_ev, g + 1)
                    wait(pe, s_fin, g - 1)
                    for x in range(GT):
                        last = nc.tensor.matmul(pout[b][0:TN, x * D:(x + 1) * D], ST[:, b, x * TN:(x + 1) * TN], weight[:, :], start=True, stop=True)
                    if cheb and not norm:
                        for x in range(GT):
                            last = nc.tensor.transpose(psn[b][0:TN, x * D:(x + 1) * D], ST[:, b, x * TN:(x + 1) * TN], K["ident"][:, :])
                    last.then_inc(s_pr, 1)
                groups(pe, n, body)

            @block.vector
            def _(dve):
                counter = Counter(dve)
                CH = 5 if norm else 1 if minus is None else 2

                def onehot(g, b):
                    wait(dve, s_sum, g - 1)
                    nc.vector.tensor_tensor(M[:, b, :, :], K["iota"][:, 0:TN].unsqueeze(1).to_broadcast([P, GT, TN]),
                                            K["rel_dst"][:, bass.ds(GT * g, GT)].unsqueeze(2).to_broadcast([P, GT, TN]),
                                            ALU.is_equal).then_inc(s_hot, 1)

                def overflow(g, b):
                    more = dve.value_load(K["more_dst"][0:1, bass.ds(g, 1)], min_val=0, max_val=NJ)
                    with dve.If(more > 0):
                        alone(dve, s_ev, g + 1, passed)
                        with dve.Fori(0, more) as c:
                            k = counter.next() + 1
                            dve.wait_ge(o.s_e, k * 64)
                            nc.vector.tensor_scalar(o.i[:, :, 0], o.e[:, :, 0], N - 1, None, ALU.min)
                            nc.vector.tensor_copy(o.f[:, :], o.e[:, :, 1]).then_inc(o.s_f, 1)
                            dve.wait_ge(o.s_f, k)
                            nc.vector.tensor_tensor(o.f[:, :], o.f[:, :], K["tbase"][:, bass.ds(GT * g, GT)], ALU.subtract).then_inc(o.s_r, 1)
                            dve.wait_ge(o.s_r, k)
                            nc.vector.tensor_tensor(o.M[:, :, :], K["iota"][:, 0:TN].unsqueeze(1).to_broadcast([P, GT, TN]),
                                                    o.f[:, :].unsqueeze(2).to_broadcast([P, GT, TN]), ALU.is_equal).then_inc(o.s_hot, 1)
                            dve.wait_ge(o.s_mm, k)
                            nc.vector.tensor_tensor(ST[:, b, :], ST[:, b, :], pov[:, 0:GN], ALU.add).then_inc(o.s_done, 1)
                            dve.wait_ge(o.s_done, k)

                def body(g, b, last=False):
                    if not last:
                        onehot(g + 1, 1 - b)
                    overflow(g, b)
                    n_ch = [0]

                    def seq(ins):
                        n_ch[0] += 1
                        ins.then_inc(s_ch, 1)
                        dve.wait_ge(s_ch, CH * g + n_ch[0])
                    use = g // 2 if isinstance(g, int) else None
                    dve.wait_ge(s_pr, g + 1)
                    wait(dve, s_st[b], 16 * stores * use if use is not None else 8 * stores * (g - b))
                    v = pout[b][0:TN, :].rearrange("p (c d) -> p c d", c=GT)
                    if not cheb:
                        nc.vector.tensor_tensor(yo[:, b, :, :], v, scal(scale, g), ALU.mult).then_inc(s_fin, 1)
                        return
                    wait(dve, s_fin, g)
                    seq(nc.vector.tensor_tensor(tmp[:, :, :], v, scal(K["isq"], g), ALU.mult))
                    dve.wait_ge(s_ld[b], 16 * loads * (use + 1) if use is not None else 8 * loads * (g - b) + 16 * loads)
                    if not norm:
                        nc.vector.tensor_tensor(R[:, b, :, :], R[:, b, :, :], tmp[:, :, :], ALU.add)
                        sn = psn[b][0:TN, :].rearrange("p (c d) -> p c d", c=GT)
                        scaled = nc.vector.tensor_tensor(yo[:, b, :, :], sn, scal(K["inv_dst"], g), ALU.mult)
                        if minus is None:
                            scaled.then_inc(s_fin, 1)
                        else:
                            seq(scaled)
                            nc.vector.scalar_tensor_tensor(yo[:, b, :, :], yo[:, b, :, :], twice, Y[:, b, :, :],
                                                           ALU.mult, ALU.subtract).then_inc(s_fin, 1)
                        return
                    seq(nc.vector.tensor_tensor(tmp[:, :, :], R[:, b, :, :], tmp[:, :, :], ALU.add))
                    layer_norm(nc, dve, seq, tmp[:, :, :], stats, mv, yo[:, b, :, :], s_var, s_std, g + 1, passed).then_inc(s_fin, 1)
                onehot(0, 0)
                body(0, 0)
                body(1, 1)
                with dve.Fori(1, (n - 1) // 2) as i:
                    body(2 * i, 0)
                    body(2 * i + 1, 1)
                body(n - 1, 0, last=True)

            @block.sync
            def _(sp):
                def load(g, b):
                    alone(sp, s_fin, g - 1, passed)
                    if write_r is not None:
                        use = g // 2 if isinstance(g, int) else None
                        alone(sp, s_st[b], 16 * stores * use if use is not None else 8 * stores * (g - b), passed)
                    if cheb:
                        sp.dma_start(R[:, b, :, :], rows(read_r, g)).then_inc(s_ld[b], 16)
                    if minus is not None:
                        sp.dma_start(Y[:, b, :, :], rows(minus, g)).then_inc(s_ld[b], 16)

                def body(g, b, last=False):
                    if not last and loads:
                        load(g + 1, 1 - b)
                    alone(sp, s_fin, g + 1, passed)
                    sp.dma_start(rows(out, g), yo[:, b, :, :]).then_inc(s_st[b], 16)
                    if write_r is not None:
                        sp.dma_start(rows(write_r, g), R[:, b, :, :]).then_inc(s_st[b], 16)
                if loads:
                    load(0, 0)
                body(0, 0)
                body(1, 1)
                with sp.Fori(1, (n - 1) // 2) as i:
                    body(2 * i, 0)
                    body(2 * i + 1, 1)
                body(n - 1, 0, last=True)
                sp.wait_ge(s_st[0], 16 * stores * ((n + 1) // 2))
                sp.wait_ge(s_st[1], 16 * stores * ((n - 1) // 2))


def weights_phase(nc, K, t):
    with ExitStack() as ctx:
        m = Mem(nc, ctx, "weights")
        passed = m.sem("passed")
        att = m.sb("att", [P, 2, D])
        prod = m.sb("prod", [P, 2, D])
        w3 = m.sb("w3", [D, 4, D])
        s_ld = m.sem("loaded")
        s_v = m.sem("dve")
        with nc.Block() as block:
            @block.sync
            def _(sp):
                for dst, src in ((K["W01"], t["L0_gnn_W1"]), (K["W02"], t["L0_gnn_W2"]), (K["W1a"], t["L2_gnn_W1"][0:D, :]),
                                 (K["W1b"], t["L2_gnn_W1"][D:2 * D, :]), (K["W2"], t["L2_gnn_W2"]), (K["W3"], t["L2_gnn_W3"])):
                    sp.dma_start(dst[:, :], src).then_inc(s_ld, 16)
                sp.dma_start(K["Watt"][:, 0:D], t["L1_gnn_W"]).then_inc(s_ld, 16)
                sp.dma_start(w3[:, :, :], t["L3_gnn_weights"].rearrange("k f o -> f k o")).then_inc(s_ld, 16)
                for x, name in enumerate(("L1_gnn_att_src", "L1_gnn_att_dst")):
                    sp.dma_start(att[:, x, :], t[name].rearrange("h d -> (h d)").unsqueeze(0).to_broadcast([P, D])).then_inc(s_ld, 16)
                for key, name in (("b01", "L0_gnn_b1"), ("b02", "L0_gnn_b2"), ("batt", "L1_gnn_bias"), ("b3", "L2_gnn_b3"),
                                  ("gamma", "L2_gnn_gamma"), ("beta", "L2_gnn_beta")):
                    sp.dma_start(K[key][:, :], t[name].unsqueeze(0).to_broadcast([P, D])).then_inc(s_ld, 16)
                for key, name in (("b1c", "L2_gnn_b1"), ("b2c", "L2_gnn_b2")):
                    sp.dma_start(K[key][:, :], t[name].unsqueeze(1)).then_inc(s_ld, 16)
                sp.wait_ge(s_ld, 16 * 18)

            @block.vector
            def _(dve):
                dve.wait_ge(s_ld, 16 * 18)
                nc.vector.tensor_tensor(prod[:, :, :], K["Watt"][:, 0:D].unsqueeze(1).to_broadcast([P, 2, D]), att[:, :, :],
                                        ALU.mult).then_inc(s_v, 1)
                dve.wait_ge(s_v, 1)
                nc.vector.tensor_reduce(K["Watt"][:, D:TW], prod[:, :, :].rearrange("p x (h d) -> p (x h) d", d=HD), AX.X, ALU.add)
                nc.vector.tensor_tensor(K["V0"][:, :], w3[:, 0, :], w3[:, 2, :], ALU.subtract)
                nc.vector.tensor_tensor(K["V1"][:, :], w3[:, 1, :], w3[:, 3, :], ALU.subtract)
                nc.vector.tensor_scalar(K["V2"][:, :], w3[:, 2, :], 2.0, None, ALU.mult)
                nc.vector.tensor_scalar(K["V3"][:, :], w3[:, 3, :], 2.0, None, ALU.mult).then_inc(s_v, 1)
                dve.wait_ge(s_v, 2)


def node_pass(nc, K, t, name, table, bias, out, x_in=None, att_out=None):
    second = x_in is not None
    with ExitStack() as ctx:
        m = Mem(nc, ctx, name)
        passed = m.sem("passed")
        V = m.sb("V", [P, 2, D])
        M = m.sb("M", [P, 2, GN])
        cur = m.sb("cur", [P, 2, 1], I32)
        S = m.sb("S", [TN, 2, GT, D])
        C = m.sb("C", [TN, 2, GT])
        lastrow = m.sb("lastrow", [TN, D])
        X = m.sb("X", [TN, 2, GT, D])
        O = m.sb("O", [TN, 2, GT, D])
        XT = m.sb("XT", [D, 2, GN])
        A = m.sb("A", [TN, 2, GT, TW])
        stats = m.sb("stats", [TN, GT, 6])
        mv = m.sb("mv", [TN, GT, 2])
        oe = m.sb("over_e", [P, 2], I32)
        oi = m.sb("over_i", [P, 1], I32)
        of = m.sb("over_f", [P, 1])
        oM = m.sb("over_M", [P, GN])
        oV = m.sb("over_V", [P, D])
        ps = [m.ps(f"ps{i}", [P, 512]) for i in range(2)]
        pc = m.ps("pc", [P, 512])
        pt = m.ps("pt", [P, 512])
        pa = [m.ps(f"pa{i}", [P, 512]) for i in range(2)]
        pov = m.ps("pov", [P, 512])
        s_row = m.sem("last_row")
        s_cur = m.sem("indices")
        s_g = [m.sem(f"gathered{i}") for i in range(2)]
        s_hot = m.sem("onehot")
        s_sum = m.sem("summed")
        s_ev = m.sem("sum_in_sbuf")
        s_ch = m.sem("dve_chain")
        s_fin = m.sem("finished")
        s_var = m.sem("variance")
        s_std = m.sem("deviation")
        s_tr = m.sem("transposed")
        s_xt = m.sem("transpose_in_sbuf")
        s_at = m.sem("attention_rows")
        s_ac = m.sem("attention_in_sbuf")
        s_ld = [m.sem(f"loaded{i}") for i in range(2)]
        s_st = [m.sem(f"stored{i}") for i in range(2)]
        s_sa = [m.sem(f"stored_att{i}") for i in range(2)]
        so_e, so_f, so_r, so_hot, so_g, so_mm, so_done = [m.sem(f"over_{x}") for x in
                                                          ("edges", "float", "rel", "onehot", "gather", "sum", "added")]

        def rows(a, g):
            return a[bass.ds(g * GN, GN), :].rearrange("(c p) d -> p c d", p=TN)

        def use16(g, b, n=16):
            return n * (g // 2) if isinstance(g, int) else (n // 2) * (g - b)

        with nc.Block() as block:
            @block.gpsimd
            def _(pool):
                counter = Counter(pool)

                def body(g, b):
                    alone(pool, s_sum, g - 1, passed)
                    alone(pool, s_cur, g + 1, passed)
                    pool.indirect_dma_start(V[:, b, :], None, table[:, :],
                                            bass.IndirectOffsetOnAxis(ap=cur[:, b, :], axis=0)).then_inc(s_g[b], 16)
                    more = pool.value_load(K["more_src"][0:1, bass.ds(g, 1)], min_val=0, max_val=NJ)
                    with pool.If(more > 0):
                        with pool.Fori(0, more) as c:
                            before = counter.next()
                            k = before + 1
                            first = pool.value_load(K["bstarts"][0:1, bass.ds(g, 1)], min_val=0, max_val=E)
                            at = at_most(pool, first + (c + 1) * P, E)
                            pool.dma_start(oe[:, :], t["by_src"][bass.ds(at, P), :]).then_inc(so_e, 16)
                            alone(pool, so_hot, k, passed)
                            pool.indirect_dma_start(oV[:, :], None, table[:, :],
                                                    bass.IndirectOffsetOnAxis(ap=oi[:, :], axis=0)).then_inc(so_g, 16)
                            alone(pool, so_done, k, passed)
                groups(pool, G, body)

            @block.scalar
            def _(act):
                def front(g, b):
                    wait(act, s_sum, g - 1)
                    nc.scalar.copy(cur[:, b, :], K["idx_src"][:, bass.ds(g, 1)]).then_inc(s_cur, 1)
                    act.wait_ge(s_sum, g + 1)
                    wait(act, s_fin, g - 1)
                    nc.scalar.copy(S[:, b, :, :], ps[b][0:TN, :].rearrange("p (c d) -> p c d", c=GT))
                    nc.scalar.copy(C[:, b, :], pc[0:TN, b * GT:(b + 1) * GT]).then_inc(s_ev, 1)

                def body(g, b, last=False):
                    if not last:
                        front(g + 1, 1 - b)
                    if second:
                        deviation(nc, act, K, mv, s_var, s_std, g)
                        act.wait_ge(s_tr, g + 1)
                        nc.scalar.copy(XT[:, b, :], pt[:, 0:GN]).then_inc(s_xt, 1)
                        act.wait_ge(s_at, g + 1)
                        wait(act, s_sa[b], use16(g, b))
                        for h in range(2):
                            done = nc.scalar.copy(A[:, b, 2 * h:2 * h + 2, :],
                                                  pa[h][0:TN, 0:2 * TW].rearrange("p (c d) -> p c d", c=2))
                        done.then_inc(s_ac, 1)
                front(0, 0)
                body(0, 0)
                body(1, 1)
                with act.Fori(1, (G - 1) // 2) as i:
                    body(2 * i, 0)
                    body(2 * i + 1, 1)
                body(G - 1, 0, last=True)

            @block.tensor
            def _(pe):
                counter = Counter(pe)

                def front(g, b):
                    pe.wait_ge(s_g[b], use16(g, b) + 16)
                    pe.wait_ge(s_hot, g + 1)
                    wait(pe, s_ev, g - 1)
                    for x in range(GT):
                        nc.tensor.matmul(ps[b][0:TN, x * D:(x + 1) * D], M[:, b, x * TN:(x + 1) * TN], V[:, b, :], start=True, stop=True)
                        last = nc.tensor.matmul(pc[0:TN, b * GT + x:b * GT + x + 1], M[:, b, x * TN:(x + 1) * TN], K["ones"][:, 0:1], start=True, stop=True)
                    last.then_inc(s_sum, 1)
                    more = pe.value_load(K["more_src"][0:1, bass.ds(g, 1)], min_val=0, max_val=NJ)
                    with pe.If(more > 0):
                        with pe.Fori(0, more) as c:
                            before = counter.next()
                            k = before + 1
                            pe.wait_ge(so_g, k * 16)
                            for half in range(2):
                                for x in range(GT):
                                    w = D if half == 0 else 1
                                    last = nc.tensor.matmul(pov[0:TN, x * w:(x + 1) * w], oM[:, x * TN:(x + 1) * TN],
                                                            oV[:, :] if half == 0 else K["ones"][:, 0:1], start=True, stop=True)
                                last.then_inc(so_mm, 1)
                                if half == 0:
                                    pe.wait_ge(so_r, 2 * k)
                            pe.wait_ge(so_done, k)

                def body(g, b, last=False):
                    if not last:
                        front(g + 1, 1 - b)
                    if second:
                        pe.wait_ge(s_fin, g + 1)
                        wait(pe, s_xt, g)
                        for x in range(GT):
                            done = nc.tensor.transpose(pt[:, x * TN:(x + 1) * TN], O[:, b, x, :], K["ident"][0:TN, 0:TN])
                        done.then_inc(s_tr, 1)
                        pe.wait_ge(s_xt, g + 1)
                        wait(pe, s_ac, g)
                        for x in range(GT):
                            done = nc.tensor.matmul(pa[x // 2][0:TN, (x % 2) * TW:(x % 2 + 1) * TW],
                                                    XT[:, b, x * TN:(x + 1) * TN], K["Watt"][:, :], start=True, stop=True)
                        done.then_inc(s_at, 1)
                front(0, 0)
                body(0, 0)
                body(1, 1)
                with pe.Fori(1, (G - 1) // 2) as i:
                    body(2 * i, 0)
                    body(2 * i + 1, 1)
                body(G - 1, 0, last=True)

            @block.vector
            def _(dve):
                counter = Counter(dve)
                CH = 8 if second else 4

                def onehot(g, b):
                    wait(dve, s_sum, g - 1)
                    nc.vector.tensor_scalar(M[:, b, :], K["iota"][:, :], K["rel_src"][:, bass.ds(g, 1)], None,
                                            ALU.is_equal).then_inc(s_hot, 1)

                def body(g, b, last=False):
                    n_ch = [0]

                    def seq(ins):
                        n_ch[0] += 1
                        ins.then_inc(s_ch, 1)
                        dve.wait_ge(s_ch, CH * g + n_ch[0])
                    if not last:
                        onehot(g + 1, 1 - b)
                    dve.wait_ge(s_ev, g + 1)
                    more = dve.value_load(K["more_src"][0:1, bass.ds(g, 1)], min_val=0, max_val=NJ)
                    with dve.If(more > 0):
                        with dve.Fori(0, more) as c:
                            before = counter.next()
                            k = before + 1
                            dve.wait_ge(so_e, k * 16)
                            nc.vector.tensor_copy(oi[:, :], oe[:, 1:2])
                            nc.vector.tensor_copy(of[:, :], oe[:, 0:1]).then_inc(so_f, 1)
                            dve.wait_ge(so_f, k)
                            nc.vector.tensor_tensor(of[:, :], of[:, :], K["tbase"][:, bass.ds(GT * g, 1)], ALU.subtract).then_inc(so_r, 1)
                            dve.wait_ge(so_r, 2 * before + 1)
                            nc.vector.tensor_scalar(oM[:, :], K["iota"][:, :], of[:, 0:1], None, ALU.is_equal).then_inc(so_hot, 1)
                            dve.wait_ge(so_mm, 2 * before + 1)
                            nc.vector.tensor_tensor(S[:, b, :, :], S[:, b, :, :], pov[0:TN, :].rearrange("p (c d) -> p c d", c=GT),
                                                    ALU.add).then_inc(so_r, 1)
                            dve.wait_ge(so_mm, 2 * k)
                            nc.vector.tensor_tensor(C[:, b, :], C[:, b, :], pov[0:TN, 0:GT], ALU.add).then_inc(so_done, 1)
                            dve.wait_ge(so_done, k)
                    if isinstance(g, int) and g == 0:
                        dve.wait_ge(s_row, 16)
                    seq(nc.vector.tensor_tensor(C[:, b, :], K["deg_src"][:, bass.ds(GT * g, GT)], C[:, b, :], ALU.subtract))
                    for x in range(GT):
                        step = nc.vector.scalar_tensor_tensor(S[:, b, x, :], lastrow[:, :], C[:, b, x:x + 1], S[:, b, x, :], ALU.mult, ALU.add)
                    seq(step)
                    seq(nc.vector.tensor_tensor(S[:, b, :, :], S[:, b, :, :],
                                                K["inv_src"][:, bass.ds(GT * g, GT)].unsqueeze(2).to_broadcast([TN, GT, D]), ALU.mult))
                    seq(nc.vector.tensor_tensor(S[:, b, :, :], S[:, b, :, :], bias[0:TN, :].unsqueeze(1).to_broadcast([TN, GT, D]), ALU.add))
                    wait(dve, s_st[b], use16(g, b))
                    if not second:
                        nc.vector.tensor_scalar(O[:, b, :, :], S[:, b, :, :], 0.0, None, ALU.max).then_inc(s_fin, 1)
                        return
                    dve.wait_ge(s_ld[b], use16(g, b) + 16)
                    wait(dve, s_tr, g - 1)
                    seq(nc.vector.tensor_tensor(S[:, b, :, :], S[:, b, :, :], X[:, b, :, :], ALU.add))
                    layer_norm(nc, dve, seq, S[:, b, :, :], stats, mv, O[:, b, :, :], s_var, s_std, g + 1, passed).then_inc(s_fin, 1)
                    assert n_ch[0] == CH, n_ch
                onehot(0, 0)
                body(0, 0)
                body(1, 1)
                with dve.Fori(1, (G - 1) // 2) as i:
                    body(2 * i, 0)
                    body(2 * i + 1, 1)
                body(G - 1, 0, last=True)

            @block.sync
            def _(sp):
                sp.dma_start(lastrow[:, :], table[HE - 1:HE, :].to_broadcast([TN, D])).then_inc(s_row, 16)

                def body(g, b, last=False):
                    if not last and second:
                        alone(sp, s_fin, g, passed)
                        sp.dma_start(X[:, 1 - b, :, :], rows(x_in, g + 1)).then_inc(s_ld[1 - b], 16)
                    alone(sp, s_fin, g + 1, passed)
                    sp.dma_start(rows(out, g), O[:, b, :, :]).then_inc(s_st[b], 16)
                    if second:
                        alone(sp, s_ac, g + 1, passed)
                        sp.dma_start(rows(att_out, g), A[:, b, :, :]).then_inc(s_sa[b], 16)
                if second:
                    sp.dma_start(X[:, 0, :, :], rows(x_in, 0)).then_inc(s_ld[0], 16)
                body(0, 0)
                body(1, 1)
                with sp.Fori(1, (G - 1) // 2) as i:
                    body(2 * i, 0)
                    body(2 * i + 1, 1)
                body(G - 1, 0, last=True)
                for b in range(2):
                    sp.wait_ge(s_st[b], 16 * ((G + 1 - b) // 2))
                    if second:
                        sp.wait_ge(s_sa[b], 16 * ((G + 1 - b) // 2))


def in_pairs(eng, steps):
    def run(pair):
        for step in steps:
            for g, b in pair:
                step(g, b, pair[0][0])
    run([(0, 0), (1, 1)])
    with eng.Fori(1, (G - 1) // 2) as i:
        run([(2 * i, 0), (2 * i + 1, 1)])
    run([(G - 1, 0)])


def attention_pass(nc, K, t):
    with ExitStack() as ctx:
        m = Mem(nc, ctx, "att")
        passed = m.sem("passed")
        V = m.sb("V", [P, 2, GT, TW])
        VX = m.sb("VX", [P, 2, GT, D])
        M = m.sb("M", [P, 2, GT, TN])
        MT = m.sb("MT", [TN, 2, GT, P])
        cur = m.sb("cur", [P, 2, GT, 1], I32)
        EA = m.sb("EA", [P, 2, GT, D])
        SELF = m.sb("SELF", [TN, 2, GT, TW])
        X = m.sb("X", [TN, 2, GT, D])
        A16 = m.sb("A16", [P, 2, 2, GT * HEADS])
        dT = m.sb("dT", [GT * HEADS, 2, P])
        ne = m.sb("ne", [GT * HEADS, 2, P + 1])
        rB = m.sb("rB", [GT * HEADS, 2, P])
        rm = m.sb("rm", [GT * HEADS, 2, P])
        RM = m.sb("RM", [P, 2, GT, HEADS + 1])
        z4 = m.sb("z4", [TN, 2, GT])
        Gm = m.sb("Gm", [TN, 2, GT, HEADS])
        N8 = m.sb("N8", [TN, 2, GT, 2 * HEADS])
        EXS = m.sb("EXS", [TN, 2, GT, HEADS])
        EX = m.sb("EX", [P, 2, GT, HEADS])
        NUM = m.sb("NUM", [TN, 2, GT, D])
        DEN = m.sb("DEN", [TN, 2, GT, HEADS])
        tmp = m.sb("tmp", [TN, 2, GT, D])
        x2 = m.sb("x2", [TN, 2, GT, D])
        XT = m.sb("XT", [D, 2, GN])
        AT = m.sb("AT", [D, 2, GN])
        H1 = m.sb("H1", [D, 2, GN])
        H2 = m.sb("H2", [D, 2, GN])
        y0 = m.sb("y0", [TN, 2, GT, D])
        r0 = m.sb("r0", [TN, 2, GT, D])
        stats = m.sb("stats", [TN, 2, GT, 6])
        mv = m.sb("mv", [TN, 2, GT, 2])
        oe = m.sb("oe", [P, GT, 2], I32)
        oi = m.sb("oi", [P, GT, 1], I32)
        of = m.sb("of", [P, GT])
        oM = m.sb("oM", [P, 1, GT, TN])
        oV = m.sb("oV", [P, 1, GT, TW])
        oMT = m.sb("oMT", [TN, 1, GT, P])
        oEA = m.sb("oEA", [P, 1, GT, D])
        oA16 = m.sb("oA16", [P, 1, 2, GT * HEADS])
        odT = m.sb("odT", [GT * HEADS, 1, P])
        one = m.sb("one", [GT * HEADS, 1, P + 1])
        orB = m.sb("orB", [GT * HEADS, 1, P])
        orm = m.sb("orm", [GT * HEADS, 1, P])
        oRM = m.sb("oRM", [P, 1, GT, HEADS + 1])
        oG = m.sb("oG", [TN, GT, HEADS])
        oEX = m.sb("oEX", [P, 1, GT, HEADS])
        P0, P1, P2, P3 = [[m.ps(f"p{i}{b}", [P, 512]) for b in range(2)] for i in range(4)]
        s_cur, s_hot, s_a16, s_q, s_rm, s_q2, s_rmc, s_pg, s_n8, s_mtp, s_mt, s_pn, s_exa, s_ex, s_vx, s_num, s_exs_in, \
            s_exs, s_agp, s_ag, s_mn, s_elu, s_x2, s_x2p, s_xt, s_h1p, s_h1, s_h2p, s_h2, s_h3p, s_x3, s_x3p, s_x3t, \
            s_r0p, s_fin, s_ch, s_var, s_std = [m.sem(x) for x in (
                "indices", "onehot", "a_columns", "a_rows_psum", "max_rows", "max_columns_psum", "max_columns", "node_max_psum",
                "node_values", "onehot_t_psum", "onehot_t", "edge_values_psum", "edge_exponent", "edge_exp", "messages",
                "sums_psum", "self_exponent", "self_exp", "edge_sums_psum", "edge_sums", "elu_exponent", "elu_exp", "x2",
                "x2_t_psum", "x2_t", "h1_psum", "h1", "h2_psum", "h2", "h3_psum", "x3", "x3_t_psum", "x3_t", "r0_psum",
                "finished", "dve_chain", "variance", "deviation")]
        s_g = [m.sem(f"gathered{i}") for i in range(2)]
        s_ld = [m.sem(f"loaded{i}") for i in range(2)]
        s_st = [m.sem(f"stored{i}") for i in range(2)]
        so_e, so_hot, so_g, so_pe, so_dv, so_ex, so_done, so_ch = [m.sem(f"over_{x}") for x in (
            "edges", "onehot", "gather", "pe_step", "dve_step", "exp", "done", "chain")]

        def rows(a, g):
            return a[bass.ds(g * GN, GN), :].rearrange("(c p) d -> p c d", p=TN)

        def use(g, b, n):
            return n * (g // 2) if isinstance(g, int) else (n // 2) * (g - b)

        def heads(a):
            return a.rearrange("p c (h d) -> p c h d", h=HEADS)

        def over(eng, counter, g, chunk):
            eng.sem_inc(passed, 1)
            more = eng.value_load(K["more_dst"][0:1, bass.ds(g, 1)], min_val=0, max_val=NJ)
            with eng.If(more > 0):
                with eng.Fori(0, more) as c:
                    before = counter.next()
                    chunk(c, before, before + 1)

        OC = 9

        def nth(g, b, g0, n):
            return n * (1 if isinstance(g0, int) and g0 == G - 1 else 2) + b + 1

        with nc.Block() as block:
            @block.gpsimd
            def _(pool):
                counter = Counter(pool)

                def gather(g, b, g0):
                    alone(pool, s_num, g - 1, passed)
                    alone(pool, s_cur, g + 1, passed)
                    for x in range(GT):
                        pool.indirect_dma_start(V[:, b, x, :], None, t["att"][:, :],
                                                bass.IndirectOffsetOnAxis(ap=cur[:, b, x, :], axis=0)).then_inc(s_g[b], 16)

                def over_gather(features):
                    def step(g, b, g0):
                        def chunk(c, before, k):
                            for x in range(GT):
                                first = pool.value_load(K["starts"][0:1, bass.ds(GT * g + x, 1)], min_val=0, max_val=E)
                                at = at_most(pool, first + (c + 1) * P, E)
                                pool.dma_start(oe[:, x, :], t["edges"][bass.ds(at, P), :]).then_inc(so_e, 16)
                                pool.dma_start(oEA[:, 0, x, :], t["edge_attr"][bass.ds(at, P), :]).then_inc(so_e, 16)
                            alone(pool, so_hot, k, passed)
                            for x in range(GT):
                                pool.indirect_dma_start(oV[:, 0, x, :], None, t["att"][:, :],
                                                        bass.IndirectOffsetOnAxis(ap=oi[:, x, :], axis=0)).then_inc(so_g, 16)
                            alone(pool, so_done, k, passed)
                        over(pool, counter, g, chunk)
                    return step
                in_pairs(pool, [gather, over_gather(False), over_gather(True)])

            @block.sync
            def _(sp):
                def load(g, b, g0):
                    alone(sp, s_fin, g - 1, passed)
                    sp.dma_start(SELF[:, b, :, :], rows(t["att"], g)).then_inc(s_ld[b], 16)
                    sp.dma_start(X[:, b, :, :], rows(t["x1"], g)).then_inc(s_ld[b], 16)
                    for x in range(GT):
                        first = sp.value_load(K["starts"][0:1, bass.ds(GT * g + x, 1)], min_val=0, max_val=E)
                        sp.dma_start(EA[:, b, x, :], t["edge_attr"][bass.ds(first, P), :]).then_inc(s_ld[b], 16)

                def store(g, b, g0):
                    alone(sp, s_fin, g + 1, passed)
                    sp.dma_start(rows(t["y0"], g), y0[:, b, :, :]).then_inc(s_st[b], 16)
                    sp.dma_start(rows(t["r0"], g), r0[:, b, :, :]).then_inc(s_st[b], 16)
                in_pairs(sp, [load, store])
                sp.wait_ge(s_st[0], 32 * ((G + 1) // 2))
                sp.wait_ge(s_st[1], 32 * ((G - 1) // 2))

            @block.tensor
            def _(pe):
                counter = Counter(pe)
                idn = K["ident"]

                def a_rows(g, b, g0):
                    pe.wait_ge(s_a16, g + 1)
                    wait(pe, s_fin, g - 1)
                    for x in range(2):
                        done = nc.tensor.transpose(P0[b][0:16, x * P:(x + 1) * P], A16[:, b, x, :], idn[:, :])
                    done.then_inc(s_q, 1)
                    for x in range(GT):
                        done = nc.tensor.transpose(P1[b][0:TN, x * P:(x + 1) * P], M[:, b, x, :], idn[:, :])
                    done.then_inc(s_mtp, 1)

                def edge_sums(g, b, g0):
                    pe.wait_ge(s_ld[b], use(g, b, 96) + 96)
                    for x in range(GT):
                        done = nc.tensor.matmul(P3[b][:, x * TN:(x + 1) * TN], EA[:, b, x, :], M[:, b, x, :], start=True, stop=True)
                    done.then_inc(s_agp, 1)

                def max_columns(g, b, g0):
                    alone(pe, s_rm, g + 1, passed)
                    nc.tensor.transpose(P2[b][:, 0:16], rm[:, b, :], idn[0:16, 0:16]).then_inc(s_q2, 1)

                def node_max(g, b, g0):
                    pe.wait_ge(s_rmc, g + 1)
                    for x in range(GT):
                        done = nc.tensor.matmul(P2[b][0:TN, 64 + 5 * x:69 + 5 * x], M[:, b, x, :], RM[:, b, x, :], start=True, stop=True)
                    done.then_inc(s_pg, 1)

                def over_max(g, b, g0):
                    def chunk(c, before, k):
                        k1 = 3 * before
                        pe.wait_ge(so_dv, k1 + 1)
                        for x in range(2):
                            done = nc.tensor.transpose(P0[b][0:16, x * P:(x + 1) * P], oA16[:, 0, x, :], idn[:, :])
                        done.then_inc(so_pe, 1)
                        alone(pe, so_dv, k1 + 2, passed)
                        nc.tensor.transpose(P0[b][:, 256:272], orm[:, 0, :], idn[0:16, 0:16]).then_inc(so_pe, 1)
                        pe.wait_ge(so_dv, k1 + 3)
                        for x in range(GT):
                            done = nc.tensor.matmul(P0[b][0:TN, 320 + 5 * x:325 + 5 * x], oM[:, 0, x, :], oRM[:, 0, x, :], start=True, stop=True)
                        done.then_inc(so_pe, 1)
                        pe.wait_ge(so_done, k)
                    over(pe, counter, g, chunk)

                def edge_values(g, b, g0):
                    pe.wait_ge(s_mt, g + 1)
                    pe.wait_ge(s_n8, g + 1)
                    for x in range(GT):
                        done = nc.tensor.matmul(P2[b][:, 128 + 8 * x:136 + 8 * x], MT[:, b, x, :], N8[:, b, x, :], start=True, stop=True)
                    done.then_inc(s_pn, 1)

                def sums(g, b, g0):
                    pe.wait_ge(s_vx, g + 1)
                    for x in range(GT):
                        nc.tensor.matmul(P0[b][0:TN, x * D:(x + 1) * D], M[:, b, x, :], VX[:, b, x, :], start=True, stop=True)
                        done = nc.tensor.matmul(P2[b][0:TN, 256 + 4 * x:260 + 4 * x], M[:, b, x, :], EX[:, b, x, :], start=True, stop=True)
                    done.then_inc(s_num, 1)

                def over_sums(g, b, g0):
                    def chunk(c, before, k):
                        k1 = 3 * before
                        pe.wait_ge(so_dv, k1 + 1)
                        for x in range(GT):
                            done = nc.tensor.transpose(P1[b][0:TN, x * P:(x + 1) * P], oM[:, 0, x, :], idn[:, :])
                        done.then_inc(so_pe, 1)
                        pe.wait_ge(so_dv, k1 + 2)
                        for x in range(GT):
                            nc.tensor.matmul(P2[b][:, 300 + 8 * x:308 + 8 * x], oMT[:, 0, x, :], N8[:, b, x, :], start=True, stop=True)
                        for x in range(GT):
                            done = nc.tensor.matmul(P1[b][:, x * TN:(x + 1) * TN], oEA[:, 0, x, :], oM[:, 0, x, :], start=True, stop=True)
                        done.then_inc(so_pe, 1)
                        pe.wait_ge(so_dv, k1 + 3)
                        for x in range(GT):
                            nc.tensor.matmul(P0[b][0:TN, x * D:(x + 1) * D], oM[:, 0, x, :], oV[:, 0, x, 0:D], start=True, stop=True)
                            done = nc.tensor.matmul(P2[b][0:TN, 400 + 4 * x:404 + 4 * x], oM[:, 0, x, :], oEX[:, 0, x, :], start=True, stop=True)
                        done.then_inc(so_pe, 1)
                        pe.wait_ge(so_done, k)
                    over(pe, counter, g, chunk)

                def x2_t(g, b, g0):
                    pe.wait_ge(s_x2, g + 1)
                    for x in range(GT):
                        done = nc.tensor.transpose(P1[b][:, x * TN:(x + 1) * TN], x2[:, b, x, :], idn[0:TN, 0:TN])
                    done.then_inc(s_x2p, 1)

                def h1(g, b, g0):
                    pe.wait_ge(s_xt, g + 1)
                    pe.wait_ge(s_ag, g + 1)
                    nc.tensor.matmul(P0[b][:, 0:GN], K["W1a"][:, :], XT[:, b, :], start=True, stop=False)
                    nc.tensor.matmul(P0[b][:, 0:GN], K["W1b"][:, :], AT[:, b, :], start=False, stop=True).then_inc(s_h1p, 1)

                def h2(g, b, g0):
                    pe.wait_ge(s_h1, g + 1)
                    nc.tensor.matmul(P1[b][:, 0:GN], K["W2"][:, :], H1[:, b, :], start=True, stop=True).then_inc(s_h2p, 1)

                def h3(g, b, g0):
                    pe.wait_ge(s_h2, g + 1)
                    for x in range(GT):
                        done = nc.tensor.matmul(P0[b][0:TN, x * D:(x + 1) * D], H2[:, b, x * TN:(x + 1) * TN], K["W3"][:, :], start=True, stop=True)
                    done.then_inc(s_h3p, 1)

                def x3_t(g, b, g0):
                    pe.wait_ge(s_x3, g + 1)
                    for x in range(GT):
                        done = nc.tensor.transpose(P1[b][:, x * TN:(x + 1) * TN], x2[:, b, x, :], idn[0:TN, 0:TN])
                    done.then_inc(s_x3p, 1)

                def r0_product(g, b, g0):
                    pe.wait_ge(s_x3t, g + 1)
                    for x in range(GT):
                        done = nc.tensor.matmul(P3[b][0:TN, x * D:(x + 1) * D], XT[:, b, x * TN:(x + 1) * TN], K["V0"][:, :], start=True, stop=True)
                    done.then_inc(s_r0p, 1)
                in_pairs(pe, [a_rows, edge_sums, max_columns, node_max, over_max, edge_values, sums, over_sums, x2_t, h1, h2,
                              h3, x3_t, r0_product])

            @block.scalar
            def _(act):
                counter = Counter(act)

                def indices(g, b, g0):
                    wait(act, s_num, g - 1)
                    nc.scalar.copy(cur[:, b, :, 0], K["idx_dst"][:, bass.ds(GT * g, GT)]).then_inc(s_cur, 1)

                def onehot_t(g, b, g0):
                    act.wait_ge(s_mtp, g + 1)
                    nc.scalar.copy(MT[:, b, :, :], P1[b][0:TN, :].rearrange("p (c e) -> p c e", c=GT)).then_inc(s_mt, 1)
                    act.wait_ge(s_agp, g + 1)
                    nc.scalar.copy(AT[:, b, :], P3[b][:, 0:GN]).then_inc(s_ag, 1)

                def exps(g, b, g0):
                    act.wait_ge(s_exs_in, g + 1)
                    nc.scalar.activation(EXS[:, b, :, :], EXS[:, b, :, :], ACT.Exp).then_inc(s_exs, 1)
                    act.wait_ge(s_exa, g + 1)
                    nc.scalar.activation(EX[:, b, :, :], EX[:, b, :, :], ACT.Exp).then_inc(s_ex, 1)

                def over_skip(g, b, g0):
                    over(act, counter, g, lambda c, before, k: act.sem_inc(so_ex, 1))

                def over_exp(g, b, g0):
                    def chunk(c, before, k):
                        act.wait_ge(so_ch, OC * before + 7)
                        nc.scalar.activation(oEX[:, 0, :, :], oEX[:, 0, :, :], ACT.Exp).then_inc(so_ex, 1)
                    over(act, counter, g, chunk)

                def elu(g, b, g0):
                    act.wait_ge(s_mn, g + 1)
                    nc.scalar.activation(tmp[:, b, :, :], tmp[:, b, :, :], ACT.Exp).then_inc(s_elu, 1)

                def root(n):
                    def step(g, b, g0):
                        act.wait_ge(s_var, 3 * g0 + nth(g, b, g0, n))
                        nc.scalar.activation(mv[:, b, :, 1], mv[:, b, :, 1], ACT.Sqrt, bias=K["eps"][0:TN, 0:1]).then_inc(s_std, 1)
                    return step

                def x2_t(g, b, g0):
                    act.wait_ge(s_x2p, g + 1)
                    nc.scalar.copy(XT[:, b, :], P1[b][:, 0:GN]).then_inc(s_xt, 1)

                def h1(g, b, g0):
                    act.wait_ge(s_h1p, g + 1)
                    nc.scalar.activation(H1[:, b, :], P0[b][:, 0:GN], ACT.Relu, bias=K["b1c"][:, 0:1]).then_inc(s_h1, 1)

                def h2(g, b, g0):
                    act.wait_ge(s_h2p, g + 1)
                    nc.scalar.activation(H2[:, b, :], P1[b][:, 0:GN], ACT.Relu, bias=K["b2c"][:, 0:1]).then_inc(s_h2, 1)

                def x3_t(g, b, g0):
                    act.wait_ge(s_x3p, g + 1)
                    nc.scalar.copy(XT[:, b, :], P1[b][:, 0:GN]).then_inc(s_x3t, 1)
                in_pairs(act, [indices, onehot_t, over_skip, exps, over_exp, elu, root(0), x2_t, h1, h2, root(1), root(2), x3_t])

            @block.vector
            def _(dve):
                counter = Counter(dve)
                CH = 34
                n_ch = [0]

                def chain(g0):
                    def seq(ins):
                        n_ch[0] += 1
                        ins.then_inc(s_ch, 1)
                        dve.wait_ge(s_ch, CH * g0 + n_ch[0])
                    return seq

                def make_onehot(M_, rel):
                    return nc.vector.tensor_tensor(M_, K["iota"][:, 0:TN].unsqueeze(1).to_broadcast([P, GT, TN]),
                                                   rel.unsqueeze(2).to_broadcast([P, GT, TN]), ALU.is_equal)

                def a_columns(V_, A_, s, rel):
                    nc.vector.tensor_copy(A_[:, s, 0, :].rearrange("p (c h) -> p c h", c=GT), V_[:, s, :, D:D + HEADS])
                    return nc.vector.tensor_copy(A_[:, s, 1, :].rearrange("p (c h) -> p c h", c=GT),
                                                 rel.unsqueeze(2).to_broadcast([P, GT, HEADS]))

                def running_max(seq, bank, s, dT_, ne_, rB_, rm_):
                    seq(nc.vector.tensor_copy(dT_[:, s, :], bank[0:16, P:2 * P]))
                    seq(nc.vector.tensor_tensor(ne_[:, s, 1:P], dT_[:, s, 1:P], dT_[:, s, 0:P - 1], ALU.not_equal))
                    seq(nc.vector.tensor_scalar(rB_[:, s, :], ne_[:, s, 0:P], -BIG, None, ALU.mult))
                    seq(nc.vector.tensor_tensor_scan(rm_[:, s, :], rB_[:, s, :], bank[0:16, 0:P], -BIG, ALU.add, ALU.max))
                    return nc.vector.tensor_tensor(rm_[:, s, :], rm_[:, s, :], ne_[:, s, 1:P + 1], ALU.mult)

                def chunk_max(seq, psum, out, b):
                    seq(nc.vector.tensor_scalar(z4[:, b, :], psum[:, :, HEADS], 0.0, -BIG, ALU.is_equal, ALU.mult))
                    seq(nc.vector.tensor_tensor(out, psum[:, :, 0:HEADS], z4[:, b, :].unsqueeze(2).to_broadcast([TN, GT, HEADS]), ALU.add))

                def exponent(seq, V_, s, pn, EX_):
                    seq(nc.vector.tensor_tensor(EX_[:, s, :, :], pn[:, :, 0:HEADS], V_[:, s, :, D:D + HEADS], ALU.add))
                    seq(nc.vector.scalar_tensor_tensor(EX_[:, s, :, :], EX_[:, s, :, :], 0.2, EX_[:, s, :, :], ALU.mult, ALU.max))
                    seq(nc.vector.tensor_tensor(EX_[:, s, :, :], EX_[:, s, :, :], pn[:, :, HEADS:2 * HEADS], ALU.subtract))
                    return nc.vector.tensor_scalar(EX_[:, s, :, :], EX_[:, s, :, :], 0.0, None, ALU.min)

                nc.vector.memset(ne[:, :, :], 1.0)
                nc.vector.memset(one[:, :, :], 1.0)
                nc.vector.memset(RM[:, :, :, :], 1.0)
                nc.vector.memset(oRM[:, :, :, :], 1.0).then_inc(s_ch, 1)

                def first(g, b, g0):
                    if b == 0:
                        n_ch[0] = 1
                    if isinstance(g, int) and g == 0:
                        dve.wait_ge(s_ch, 1)
                    wait(dve, s_num, g - 1)
                    rel = K["rel_dst"][:, bass.ds(GT * g, GT)]
                    make_onehot(M[:, b, :, :], rel).then_inc(s_hot, 1)
                    dve.wait_ge(s_g[b], use(g, b, 64) + 64)
                    a_columns(V, A16, b, rel).then_inc(s_a16, 1)

                def run_max(g, b, g0):
                    dve.wait_ge(s_q, g + 1)
                    running_max(chain(g0), P0[b], b, dT, ne, rB, rm).then_inc(s_rm, 1)

                def max_columns(g, b, g0):
                    dve.wait_ge(s_q2, g + 1)
                    nc.vector.tensor_copy(RM[:, b, :, 0:HEADS], P2[b][:, 0:16].rearrange("p (c h) -> p c h", c=GT)).then_inc(s_rmc, 1)

                def node_max(g, b, g0):
                    seq = chain(g0)
                    dve.wait_ge(s_pg, g + 1)
                    dve.wait_ge(s_ld[b], use(g, b, 96) + 96)
                    chunk_max(seq, P2[b][0:TN, 64:64 + 20].rearrange("p (c h) -> p c h", c=GT), Gm[:, b, :, :], b)
                    seq(nc.vector.tensor_tensor(Gm[:, b, :, :], Gm[:, b, :, :], SELF[:, b, :, D:D + HEADS], ALU.max))

                def over_edges(g, before, k):
                    seq = over_seq(before, 0)
                    dve.wait_ge(so_e, k * 128)
                    nc.vector.tensor_scalar(oi[:, :, 0], oe[:, :, 0], N - 1, None, ALU.min)
                    seq(nc.vector.tensor_copy(of[:, :], oe[:, :, 1]))
                    seq(nc.vector.tensor_tensor(of[:, :], of[:, :], K["tbase"][:, bass.ds(GT * g, GT)], ALU.subtract))
                    make_onehot(oM[:, 0, :, :], of[:, :]).then_inc(so_hot, 1)
                    dve.wait_ge(so_hot, k)

                def over_seq(before, used):
                    n = [used]

                    def seq(ins):
                        n[0] += 1
                        ins.then_inc(so_ch, 1)
                        dve.wait_ge(so_ch, OC * before + n[0])
                    return seq

                def over_max(g, b, g0):
                    def chunk(c, before, k):
                        over_edges(g, before, k)
                        seq = over_seq(before, 2)
                        d = 3 * before
                        dve.wait_ge(so_g, k * 64)
                        a_columns(oV, oA16, 0, of[:, :]).then_inc(so_dv, 1)
                        dve.wait_ge(so_pe, d + 1)
                        running_max(seq, P0[b], 0, odT, one, orB, orm).then_inc(so_dv, 1)
                        dve.wait_ge(so_pe, d + 2)
                        nc.vector.tensor_copy(oRM[:, 0, :, 0:HEADS], P0[b][:, 256:272].rearrange("p (c h) -> p c h", c=GT)).then_inc(so_dv, 1)
                        dve.wait_ge(so_pe, d + 3)
                        chunk_max(seq, P0[b][0:TN, 320:340].rearrange("p (c h) -> p c h", c=GT), oG[:, :, :], b)
                        seq(nc.vector.tensor_tensor(Gm[:, b, :, :], Gm[:, b, :, :], oG[:, :, :], ALU.max))
                        dve.sem_inc(so_done, 1)
                        dve.wait_ge(so_done, k)
                    over(dve, counter, g, chunk)

                def node_values(g, b, g0):
                    seq = chain(g0)
                    adst = SELF[:, b, :, D + HEADS:TW]
                    nc.vector.tensor_copy(N8[:, b, :, 0:HEADS], adst)
                    nc.vector.tensor_tensor(EXS[:, b, :, :], SELF[:, b, :, D:D + HEADS], adst, ALU.add)
                    seq(nc.vector.tensor_tensor(Gm[:, b, :, :], Gm[:, b, :, :], adst, ALU.add))
                    nc.vector.scalar_tensor_tensor(N8[:, b, :, HEADS:2 * HEADS], Gm[:, b, :, :], 0.2, Gm[:, b, :, :], ALU.mult, ALU.max).then_inc(s_n8, 1)
                    seq(nc.vector.scalar_tensor_tensor(EXS[:, b, :, :], EXS[:, b, :, :], 0.2, EXS[:, b, :, :], ALU.mult, ALU.max))
                    nc.vector.tensor_tensor(EXS[:, b, :, :], EXS[:, b, :, :], N8[:, b, :, HEADS:2 * HEADS], ALU.subtract).then_inc(s_exs_in, 1)

                def edge_exponent(g, b, g0):
                    dve.wait_ge(s_pn, g + 1)
                    exponent(chain(g0), V, b, P2[b][:, 128:160].rearrange("p (c v) -> p c v", c=GT), EX).then_inc(s_exa, 1)

                def messages(g, b, g0):
                    dve.wait_ge(s_ex, g + 1)
                    nc.vector.tensor_tensor(heads(VX[:, b, :, :]), heads(V[:, b, :, 0:D]),
                                            EX[:, b, :, :].unsqueeze(3).to_broadcast([P, GT, HEADS, HD]), ALU.mult).then_inc(s_vx, 1)
                    dve.wait_ge(s_exs, g + 1)
                    chain(g0)(nc.vector.tensor_tensor(heads(NUM[:, b, :, :]), heads(SELF[:, b, :, 0:D]),
                                                      EXS[:, b, :, :].unsqueeze(3).to_broadcast([TN, GT, HEADS, HD]), ALU.mult))

                def totals(g, b, g0):
                    seq = chain(g0)
                    dve.wait_ge(s_num, g + 1)
                    nc.vector.tensor_tensor(NUM[:, b, :, :], P0[b][0:TN, :].rearrange("p (c d) -> p c d", c=GT), NUM[:, b, :, :], ALU.add)
                    seq(nc.vector.tensor_tensor(DEN[:, b, :, :], P2[b][0:TN, 256:272].rearrange("p (c h) -> p c h", c=GT), EXS[:, b, :, :], ALU.add))

                def over_sums(g, b, g0):
                    def chunk(c, before, k):
                        over_edges(g, before, k)
                        seq = over_seq(before, 2)
                        d = 3 * before
                        dve.wait_ge(s_ag, g + 1)
                        dve.wait_ge(so_g, k * 64)
                        dve.sem_inc(so_dv, 1)
                        dve.wait_ge(so_pe, d + 1)
                        nc.vector.tensor_copy(oMT[:, 0, :, :], P1[b][0:TN, :].rearrange("p (c e) -> p c e", c=GT)).then_inc(so_dv, 1)
                        dve.wait_ge(so_pe, d + 2)
                        seq(nc.vector.tensor_tensor(AT[:, b, :], AT[:, b, :], P1[b][:, 0:GN], ALU.add))
                        seq(exponent(seq, oV, 0, P2[b][:, 300:332].rearrange("p (c v) -> p c v", c=GT), oEX))
                        dve.wait_ge(so_ex, k)
                        nc.vector.tensor_tensor(heads(oV[:, 0, :, 0:D]), heads(oV[:, 0, :, 0:D]),
                                                oEX[:, 0, :, :].unsqueeze(3).to_broadcast([P, GT, HEADS, HD]), ALU.mult).then_inc(so_dv, 1)
                        dve.wait_ge(so_pe, d + 3)
                        nc.vector.tensor_tensor(NUM[:, b, :, :], P0[b][0:TN, :].rearrange("p (c d) -> p c d", c=GT), NUM[:, b, :, :], ALU.add)
                        seq(nc.vector.tensor_tensor(DEN[:, b, :, :], P2[b][0:TN, 400:416].rearrange("p (c h) -> p c h", c=GT), DEN[:, b, :, :], ALU.add))
                        seq(nc.vector.memset(of[:, 0:1], 0.0))
                        dve.sem_inc(so_done, 1)
                        dve.wait_ge(so_done, k)
                    over(dve, counter, g, chunk)

                def attention(g, b, g0):
                    seq = chain(g0)
                    seq(nc.vector.tensor_scalar(DEN[:, b, :, :], DEN[:, b, :, :], 1e-16, None, ALU.add))
                    seq(nc.vector.reciprocal(DEN[:, b, :, :], DEN[:, b, :, :]))
                    seq(nc.vector.tensor_tensor(heads(NUM[:, b, :, :]), heads(NUM[:, b, :, :]),
                                                DEN[:, b, :, :].unsqueeze(3).to_broadcast([TN, GT, HEADS, HD]), ALU.mult))
                    seq(nc.vector.tensor_tensor(NUM[:, b, :, :], NUM[:, b, :, :], K["batt"][0:TN, :].unsqueeze(1).to_broadcast([TN, GT, D]), ALU.add))
                    nc.vector.tensor_scalar(tmp[:, b, :, :], NUM[:, b, :, :], 0.0, None, ALU.min).then_inc(s_mn, 1)

                def norm(seq, x, out, g, b, g0, n):
                    return layer_norm(nc, dve, seq, x, stats[:, b, :, :], mv[:, b, :, :], out, s_var, s_std, 3 * g0 + nth(g, b, g0, n), passed)

                def norm_x2(g, b, g0):
                    seq = chain(g0)
                    dve.wait_ge(s_elu, g + 1)
                    seq(nc.vector.scalar_tensor_tensor(NUM[:, b, :, :], NUM[:, b, :, :], 0.0, tmp[:, b, :, :], ALU.max, ALU.add))
                    seq(nc.vector.scalar_tensor_tensor(NUM[:, b, :, :], NUM[:, b, :, :], -1.0, X[:, b, :, :], ALU.add, ALU.add))
                    norm(seq, NUM[:, b, :, :], x2[:, b, :, :], g, b, g0, 0).then_inc(s_x2, 1)

                def norm_mlp(g, b, g0):
                    seq = chain(g0)

                    def row(name):
                        return K[name][0:TN, :].unsqueeze(1).to_broadcast([TN, GT, D])
                    dve.wait_ge(s_h3p, g + 1)
                    seq(nc.vector.tensor_tensor(tmp[:, b, :, :], P0[b][0:TN, :].rearrange("p (c d) -> p c d", c=GT), row("b3"), ALU.add))
                    seq(norm(seq, tmp[:, b, :, :], NUM[:, b, :, :], g, b, g0, 1))
                    seq(nc.vector.tensor_tensor(NUM[:, b, :, :], NUM[:, b, :, :], row("gamma"), ALU.mult))
                    seq(nc.vector.tensor_tensor(NUM[:, b, :, :], NUM[:, b, :, :], row("beta"), ALU.add))
                    seq(nc.vector.scalar_tensor_tensor(tmp[:, b, :, :], x2[:, b, :, :], 2.0, NUM[:, b, :, :], ALU.mult, ALU.add))

                def norm_x3(g, b, g0):
                    seq = chain(g0)
                    norm(seq, tmp[:, b, :, :], x2[:, b, :, :], g, b, g0, 2).then_inc(s_x3, 1)
                    dve.wait_ge(s_x3, g + 1)
                    wait(dve, s_st[b], use(g, b, 32))
                    nc.vector.tensor_tensor(y0[:, b, :, :], x2[:, b, :, :],
                                            K["isq"][:, bass.ds(GT * g, GT)].unsqueeze(2).to_broadcast([TN, GT, D]), ALU.mult)

                def finish(g, b, g0):
                    dve.wait_ge(s_r0p, g + 1)
                    nc.vector.tensor_tensor(r0[:, b, :, :], P3[b][0:TN, :].rearrange("p (c d) -> p c d", c=GT), x2[:, b, :, :], ALU.add).then_inc(s_fin, 1)
                in_pairs(dve, [first, run_max, max_columns, node_max, over_max, node_values, edge_exponent, messages, totals,
                               over_sums, attention, norm_x2, norm_mlp, norm_x3, finish])
                assert n_ch[0] == CH + 1


def build(nc, t, stop=99):
    ctx = ExitStack()
    with ctx:
        def sb(name, shape, dt=FP32):
            return ctx.enter_context(nc.sbuf_tensor(name, shape, dt))

        K = {
            "ident": sb("ident", [P, P]), "ltri": sb("ltri", [P, P]), "ones": sb("ones", [P, P]),
            "ones_bf": sb("ones_bf", [P, P], BF16), "zeros_bf": sb("zeros_bf", [P, P], BF16),
            "ltri_bf": sb("ltri_bf", [P, P], BF16), "iota": sb("iota", [P, GN]), "tbase": sb("tbase", [P, T]),
            "eps": sb("eps", [P, 1]), "deg_src": sb("deg_src", [TN, T]), "deg_dst": sb("deg_dst", [TN, T]),
        }
        constants_phase(nc, K)
        prep_phase(nc, K, t["edges"], t["row_dram"], t["bin_dram"], t["by_src"])
        for name, width, dt in (("W01", D, FP32), ("W02", D, FP32), ("W1a", D, FP32), ("W1b", D, FP32), ("W2", D, FP32),
                                ("W3", D, FP32), ("Watt", TW, FP32), ("V0", D, FP32), ("V1", D, FP32), ("V2", D, FP32),
                                ("V3", D, FP32), ("b01", D, FP32), ("b02", D, FP32), ("batt", D, FP32), ("b3", D, FP32),
                                ("gamma", D, FP32), ("beta", D, FP32), ("b1c", 1, FP32), ("b2c", 1, FP32),
                                ("idx_dst", T, I32), ("rel_dst", T, FP32), ("idx_src", G, I32), ("rel_src", G, FP32)):
            K[name] = sb(name, [P, width], dt)
        for name, width in (("inv_dst", T), ("isq", T), ("inv_src", T)):
            K[name] = sb(name, [TN, width])
        for name, width in (("starts", T), ("bstarts", G), ("more_dst", G), ("more_src", G)):
            K[name] = sb(name, [1, width], I32)
        weights_phase(nc, K, t)
        index_phase(nc, K, t)
        if stop < 1:
            return
        sums_pass(nc, K, t, "hyper1", HG, t["x"], K["W01"], t["m1"], scale=K["inv_dst"])
        if stop < 2:
            return
        node_pass(nc, K, t, "node1", t["m1"], K["b01"], t["h1"])
        sums_pass(nc, K, t, "hyper2", HG, t["h1"], K["W02"], t["m2"], scale=K["inv_dst"])
        if stop < 3:
            return
        node_pass(nc, K, t, "node2", t["m2"], K["b02"], t["x1"], x_in=t["x"], att_out=t["att"])
        if stop < 4:
            return
        attention_pass(nc, K, t)
        if stop < 5:
            return
        sums_pass(nc, K, t, "cheb1", G, t["y0"], K["V1"], t["y1"], read_r=t["r0"], write_r=t["r1"])
        sums_pass(nc, K, t, "cheb2", G, t["y1"], K["V2"], t["y2"], read_r=t["r1"], write_r=t["r2"], minus=t["y0"], twice=2.0)
        sums_pass(nc, K, t, "cheb3", G, t["y2"], K["V3"], t["out"], read_r=t["r2"], norm=True)


_WEIGHTS = ["L0_gnn_W1", "L0_gnn_b1", "L0_gnn_W2", "L0_gnn_b2", "L1_gnn_W", "L1_gnn_att_src", "L1_gnn_att_dst",
            "L1_gnn_bias", "L2_gnn_W1", "L2_gnn_b1", "L2_gnn_W2", "L2_gnn_b2", "L2_gnn_W3", "L2_gnn_b3",
            "L2_gnn_gamma", "L2_gnn_beta", "L3_gnn_weights"]
_SCRATCH = {"row_dram": ((2, T), I32), "bin_dram": ((2, G), I32), "by_src": ((EP, 2), I32), "m1": ((HE, D), FP32),
            "m2": ((HE, D), FP32), "h1": ((N, D), FP32), "x1": ((N, D), FP32), "att": ((N, TW), FP32),
            "y0": ((N, D), FP32), "y1": ((N, D), FP32), "y2": ((N, D), FP32), "r0": ((N, D), FP32),
            "r1": ((N, D), FP32), "r2": ((N, D), FP32)}


def kernel(**inputs):
    import concourse.bacc as _bacc
    from concourse.bass_utils import run_bass_kernel_spmd as _run

    nc = _bacc.Bacc("TRN2", target_bir_lowering=False, num_devices=1)
    edges = np.full((EP, 2), PAD, np.int32)
    edges[:E, 0] = inputs["src"]
    edges[:E, 1] = inputs["dst"]
    features = np.zeros((E + P, D), np.float32)
    features[:E] = inputs["edge_attr_128"]
    arrays = {"x": np.ascontiguousarray(inputs["x"]), "edges": edges, "edge_attr": features}
    for name in _WEIGHTS:
        arrays[name] = np.ascontiguousarray(inputs[name])
    t = {name: nc.dram_tensor(name, a.shape, mybir.dt.from_np(a.dtype), kind="ExternalInput").ap()
         for name, a in arrays.items()}
    for name, (shape, dt) in _SCRATCH.items():
        t[name] = nc.dram_tensor(name, shape, dt, kind="Internal").ap()
    t["out"] = nc.dram_tensor("out", (N, D), FP32, kind="ExternalOutput").ap()
    build(nc, t)
    r = _run(nc, [arrays], core_ids=[0])
    return r.results[0]["out"]
```

```python
import numpy as np
import concourse.bass as bass
from concourse import mybir
from contextlib import ExitStack

FP32 = mybir.dt.float32
FP16 = mybir.dt.float16
BF16 = mybir.dt.bfloat16
I32 = mybir.dt.int32
ALU = mybir.AluOpType
ACT = mybir.ActivationFunctionType
AX = mybir.AxisListType

N = 50000
E = 50000
D = 128
P = 128
TN = 100
GT = 4
GN = TN * GT
T = N // TN
G = N // GN
HE = 10000
HG = HE // GN
NJ = 400
EP = P * NJ
JB = NJ // GT
PAD = 60000
HA, HB = 25, 20
MAGIC = 12582912.0
BIG = 1.0e30
HEADS, HD = 4, 32
TW = D + 2 * HEADS
EPS = 1e-5
AHEAD = 3 * GT


class Mem:

    def __init__(self, nc, ctx, phase):
        self.nc, self.ctx, self.phase, self.sems = nc, ctx, phase, []
        ctx.callback(self.clear)

    def sb(self, name, shape, dt=FP32):
        return self.ctx.enter_context(self.nc.sbuf_tensor(f"{self.phase}_{name}", shape, dt))

    def ps(self, name, shape, dt=FP32):
        return self.ctx.enter_context(self.nc.psum_tensor(f"{self.phase}_{name}", shape, dt))

    def sem(self, name):
        self.sems.append(self.nc.alloc_semaphore(f"{self.phase}_{name}"))
        return self.sems[-1]

    def clear(self):
        self.nc.clear_and_free_semaphores(self.sems)
        self.nc.all_engine_barrier()


def prep_phase(nc, K, edges, row_dram, bin_dram, by_src):
    with ExitStack() as ctx:
        m = Mem(nc, ctx, "prep")
        passed = m.sem("passed")
        pa = m.sb("pa", [P, NJ, 2], I32)
        pb = m.sb("pb", [JB, GT, P, 2], I32)
        srcf = m.sb("srcf", [P, NJ])
        dstf = m.sb("dstf", [P, NJ])
        grp = m.sb("grp", [P, NJ])
        rem = m.sb("rem", [P, NJ])
        io16 = m.sb("io16", [P, GN], FP16)
        dgrp = m.sb("dgrp", [P, NJ])
        drem = m.sb("drem", [P, NJ])
        ohk = m.sb("ohk", [P, NJ, G], BF16)
        og = m.sb("og", [P, 4, P], BF16)
        orr = m.sb("orr", [P, 4, GN], BF16)
        rs = m.sb("rs", [JB, GT, P])
        rd = m.sb("rd", [JB, GT, P])
        rk = m.sb("rk", [JB, GT, P])
        rl = m.sb("rl", [JB, GT, P])
        kcol = m.sb("kcol", [P, NJ])
        pay = m.sb("pay", [P, NJ, 2], I32)
        curp = m.sb("curp", [P, 4, 1], I32)
        curv = m.sb("curv", [P, 4, 2], I32)
        hist = m.sb("hist", [G, GT])
        hscan = m.sb("hscan", [G, GT])
        histn = m.sb("histn", [G, GN])
        cnt = m.sb("cnt", [G, NJ])
        scan = m.sb("scan", [G, NJ])
        binb = m.sb("binb", [G, 1])
        baset = m.sb("baset", [JB, GT, G])
        prod = m.sb("prod", [P, 4, G])
        pos = m.sb("pos", [P, NJ])
        posi = m.sb("posi", [P, NJ], I32)
        rowi = m.sb("rowi", [G, GT], I32)
        cnti = m.sb("cnti", [G, GT], I32)
        bini = m.sb("bini", [G, 2], I32)
        small = m.sb("small", [P, 4])
        nlow = m.sb("nlow", [1, 4])
        nlowi = m.sb("nlowi", [1, 1], I32)
        blank = m.sb("blank", [P, NJ, 2], I32)
        p_h = m.ps("p_h", [G, GN])
        p_d = m.ps("p_d", [G, GN])
        p_c = m.ps("p_c", [G, NJ])
        p_t = [m.ps(f"p_t{i}", [P, 512]) for i in range(2)]
        p_r = [m.ps(f"p_r{i}", [P, 512]) for i in range(2)]
        s_ld = m.sem("load")
        s_v = m.sem("dve")
        s_pe = m.sem("pe")
        s_og = m.sem("onehot_src")
        s_ogu = m.sem("onehot_src_used")
        s_io = m.sem("iota")
        s_rank = m.sem("rank")
        s_pos = m.sem("pos")
        s_scat = [m.sem(f"scatter{i}") for i in range(4)]
        s_cur = m.sem("scatter_operands")
        s_st = m.sem("store")
        s_bl = m.sem("blank_list")
        with nc.Block() as block:
            at = {}

            @block.sync
            def _(sp):
                sp.dma_start(pa[:, :, :], edges.rearrange("(p j) c -> p j c", p=P)).then_inc(s_ld, 16)
                sp.dma_start(pb[:, :, :, :], edges.rearrange("(b q p) c -> q b p c", b=GT, q=JB)).then_inc(s_ld, 16)
                sp.wait_ge(s_io, 3)
                sp.dma_start(by_src.rearrange("(p j) c -> p j c", p=P), blank[:, :, :]).then_inc(s_bl, 16)
                sp.wait_ge(s_bl, 16)
                sp.wait_ge(s_st, 1)
                sp.dma_start(row_dram[0, :].rearrange("(a b) -> a b", a=G), rowi[:, :]).then_inc(s_st, 16)
                sp.dma_start(row_dram[1, :].rearrange("(a b) -> a b", a=G), cnti[:, :]).then_inc(s_st, 16)
                sp.wait_ge(s_st, 34)
                sp.dma_start(bin_dram.rearrange("c g -> g c"), bini[:, :], allow_slow_non_contiguous=True).then_inc(s_st, 16)
                sp.wait_ge(s_st, 50)

            @block.gpsimd
            def _(pool):
                nc.gpsimd.iota(io16[:, :], [[1, GN]], 0, 0, allow_small_or_imprecise_dtypes=True).then_inc(s_io, 1)
                nc.gpsimd.memset(blank[:, :, 1:2], 0).then_inc(s_io, 1)
                nc.gpsimd.memset(blank[:, :, 0:1], PAD).then_inc(s_io, 1)
                pool.wait_ge(s_bl, 16)
                pool.wait_ge(s_pos, 1)
                quads = pool.value_load(nlowi[0:1, 0:1], min_val=1, max_val=JB)
                with pool.Fori(0, quads) as i:
                    alone(pool, s_cur, i + 1, passed)
                    for c in range(4):
                        pool.indirect_dma_start(by_src[:, :], bass.IndirectOffsetOnAxis(ap=curp[:, c, :], axis=0),
                                                curv[:, c, :], None, bounds_check=E - 1, oob_is_err=False)\
                            .then_inc(s_scat[c], 16)
                for c in range(4):
                    alone(pool, s_scat[c], 16 * quads, passed)

            @block.scalar
            def _(act):
                act.wait_ge(s_pos, 1)
                quads = act.value_load(nlowi[0:1, 0:1], min_val=1, max_val=JB)
                with act.Fori(0, 1) as _one:
                    nc.scalar.copy(curp[:, :, 0], posi[:, 0:4])
                    nc.scalar.copy(curv[:, :, :], pay[:, 0:4, :]).then_inc(s_cur, 1)
                with act.If(quads > 1):
                    with act.Fori(1, quads) as i:
                        for c in range(4):
                            act.wait_ge(s_scat[c], 16 * i)
                        nc.scalar.copy(curp[:, :, 0], posi[:, bass.ds(4 * i, 4)])
                        nc.scalar.copy(curv[:, :, :], pay[:, bass.ds(4 * i, 4), :]).then_inc(s_cur, 1)

            @block.vector
            def _(dve):
                n = [0]

                def seq(ins):
                    n[0] += 1
                    ins.then_inc(s_v, 1)
                    dve.wait_ge(s_v, n[0])

                def whole(out, x, a, b):
                    seq(nc.vector.tensor_scalar(out, x, a, b, ALU.mult, ALU.add))
                    seq(nc.vector.tensor_scalar(out, out, MAGIC, -MAGIC, ALU.add, ALU.add))

                dve.wait_ge(s_ld, 32)
                dve.wait_ge(s_io, 1)
                seq(nc.vector.tensor_copy(srcf[:, :], pa[:, :, 0]))
                seq(nc.vector.tensor_copy(dstf[:, :], pa[:, :, 1]))
                whole(dgrp[:, :], dstf[:, :], 1.0 / GN, 0.5 / GN - 0.5)
                seq(nc.vector.scalar_tensor_tensor(drem[:, :], dgrp[:, :], -float(GN), dstf[:, :], ALU.mult, ALU.add))
                with dve.Fori(0, JB) as i:
                    dve.wait_ge(s_ogu, 4 * i + 1)
                    for c in range(4):
                        nc.vector.tensor_scalar(og[:, c, 0:G], io16[:, 0:G], dgrp[:, bass.ds(4 * i + c, 1)], None, ALU.is_equal)
                        nc.vector.tensor_scalar(orr[:, c, :], io16[:, :], drem[:, bass.ds(4 * i + c, 1)], None,
                                                ALU.is_equal).then_inc(s_og, 1)
                whole(grp[:, :], srcf[:, :], 1.0 / GN, 0.5 / GN - 0.5)
                seq(nc.vector.scalar_tensor_tensor(rem[:, :], grp[:, :], -float(GN), srcf[:, :], ALU.mult, ALU.add))
                seq(nc.vector.tensor_copy(rs[:, :, :], pb[:, :, :, 0]))
                seq(nc.vector.tensor_copy(rd[:, :, :], pb[:, :, :, 1]))
                whole(rk[:, :, :], rs[:, :, :], 1.0 / GN, 0.5 / GN - 0.5)
                seq(nc.vector.tensor_scalar(rl[:, :, :], rd[:, :, :], float(HE - 1), 1000.0, ALU.is_ge, ALU.mult))
                seq(nc.vector.tensor_tensor(rk[:, :, :], rk[:, :, :], rl[:, :, :], ALU.add))
                at["rows"] = n[0]
                for x in range(3):
                    dve.wait_ge(s_pe, x + 2)
                    if x < 2:
                        seq(nc.vector.tensor_copy(pay[:, :, x], p_t[x % 2][:, 0:NJ]))
                    else:
                        seq(nc.vector.tensor_copy(kcol[:, :], p_t[x % 2][:, 0:NJ]))
                    at[f"evac{x}"] = n[0]
                seq(nc.vector.tensor_tensor(ohk[:, :, :], kcol[:, :].unsqueeze(2).to_broadcast([P, NJ, G]),
                                            io16[:, 0:G].unsqueeze(1).to_broadcast([P, NJ, G]), ALU.is_equal))
                at["key_onehots"] = n[0]
                dve.wait_ge(s_pe, 1)
                seq(nc.vector.tensor_copy(histn[:, :], p_h[:, :]))
                seq(nc.vector.tensor_reduce(hist[:, :], histn[:, :].rearrange("g (t n) -> g t n", t=GT), AX.X, ALU.add))
                seq(nc.vector.tensor_tensor_scan(hscan[:, :], hist[:, :], hist[:, :], 0.0, ALU.add, ALU.bypass))
                at["hist"] = n[0]
                dve.wait_ge(s_pe, 5)
                seq(nc.vector.tensor_copy(K["deg_dst"][:, :].rearrange("p (g t) -> p t g", t=GT),
                                          p_t[0][0:TN, 0:GT * G].rearrange("p (t g) -> p t g", t=GT)))
                at["deg_dst"] = n[0]
                seq(nc.vector.tensor_copy(small[0:G, 1:2], p_t[0][0:G, 501:502]))
                seq(nc.vector.tensor_scalar(hscan[:, :], hscan[:, :], small[0:G, 1:2], None, ALU.add))
                seq(nc.vector.tensor_tensor(hscan[:, :], hscan[:, :], hist[:, :], ALU.subtract))
                seq(nc.vector.tensor_copy(rowi[:, :], hscan[:, :]))
                whole(hist[:, :], hist[:, :], 1.0 / P, -1.0 / P + 0.5 / P - 0.5)
                seq(nc.vector.tensor_scalar(hist[:, :], hist[:, :], 0.0, None, ALU.max))
                seq(nc.vector.tensor_copy(cnti[:, :], hist[:, :]))
                nc.vector.memset(small[:, 3:4], 0.0).then_inc(s_st, 1)
                dve.wait_ge(s_pe, 6)
                seq(nc.vector.tensor_copy(cnt[:, :], p_c[:, :]))
                seq(nc.vector.tensor_tensor_scan(scan[:, :], cnt[:, :], cnt[:, :], 0.0, ALU.add, ALU.bypass))
                at["scan"] = n[0]
                dve.wait_ge(s_pe, 7)
                seq(nc.vector.tensor_copy(binb[:, :], p_t[1][0:G, 500:501]))
                seq(nc.vector.tensor_tensor(cnt[:, :], scan[:, :], cnt[:, :], ALU.subtract))
                seq(nc.vector.tensor_scalar(cnt[:, :], cnt[:, :], binb[:, 0:1], None, ALU.add))
                at["base"] = n[0]
                seq(nc.vector.tensor_copy(bini[:, 0:1], binb[:, :]))
                whole(binb[:, :], scan[:, NJ - 1:NJ], 1.0 / P, -1.0 / P + 0.5 / P - 0.5)
                seq(nc.vector.tensor_scalar(binb[:, :], binb[:, :], 0.0, None, ALU.max))
                seq(nc.vector.tensor_copy(bini[:, 1:2], binb[:, :]))
                nc.vector.memset(small[:, 2:3], 0.0).then_inc(s_st, 1)
                dve.wait_ge(s_pe, 8)
                seq(nc.vector.tensor_copy(baset[:, :, :], p_t[0][0:JB, 0:GT * G].rearrange("q (b g) -> q b g", b=GT)))
                at["baset"] = n[0]
                seq(nc.vector.tensor_scalar(rl[:, :, :], rd[:, :, :], float(HE - 1), None, ALU.is_lt))
                seq(nc.vector.tensor_reduce(small[0:JB, 0:1], rl[:, :, :].rearrange("q b p -> q (b p)"), AX.X, ALU.add))
                at["nlow"] = n[0]
                dve.wait_ge(s_pe, 9)
                seq(nc.vector.tensor_copy(nlow[:, 0:1], p_t[1][0:1, 501:502]))
                whole(nlow[:, 0:1], nlow[:, 0:1], 0.25 / P, 0.5 - 0.125 / P)
                seq(nc.vector.tensor_scalar(nlow[:, 0:1], nlow[:, 0:1], 1.0, None, ALU.max))
                seq(nc.vector.tensor_copy(nlowi[:, :], nlow[:, 0:1]))
                for i in range(JB):
                    dve.wait_ge(s_rank, i + 1)
                    seq(nc.vector.tensor_tensor(prod[:, :, :], ohk[:, 4 * i:4 * i + 4, :],
                                                p_r[i % 2][:, 0:4 * G].rearrange("p (c g) -> p c g", c=4), ALU.mult))
                    at[f"prod{i}"] = n[0]
                    seq(nc.vector.tensor_reduce(pos[:, 4 * i:4 * i + 4], prod[:, :, :], AX.X, ALU.add))
                seq(nc.vector.tensor_scalar(kcol[:, :], kcol[:, :], float(G), 1.0e6, ALU.is_ge, ALU.mult))
                seq(nc.vector.tensor_tensor(pos[:, :], pos[:, :], kcol[:, :], ALU.add))
                nc.vector.tensor_copy(posi[:, :], pos[:, :]).then_inc(s_pos, 1)
                with dve.Fori(0, JB) as i:
                    dve.wait_ge(s_ogu, 4 * i + NJ + 2)
                    for c in range(4):
                        nc.vector.tensor_scalar(og[:, c, 0:G], io16[:, 0:G], grp[:, bass.ds(4 * i + c, 1)], None, ALU.is_equal)
                        nc.vector.tensor_scalar(orr[:, c, :], io16[:, :], rem[:, bass.ds(4 * i + c, 1)], None,
                                                ALU.is_equal).then_inc(s_og, 1)
                dve.wait_ge(s_pe, 10)
                seq(nc.vector.tensor_copy(K["deg_rows"][:, :], p_d[:, :]))
                at["histd"] = n[0]
                dve.wait_ge(s_pe, 11)
                nc.vector.tensor_copy(K["deg_src"][:, :].rearrange("p (g t) -> p t g", t=GT),
                                      p_t[0][0:TN, 0:GT * G].rearrange("p (t g) -> p t g", t=GT))

            @block.tensor
            def _(pe):
                idn, ones_bf, ltri_bf = K["ident"], K["ones_bf"], K["ltri_bf"]

                def count_nodes(pe, out, used):
                    nc.tensor.matmul(out[:, :], K["zeros_bf"][:, 0:G], K["zeros_bf"][:, 0:1].to_broadcast([P, GN]),
                                     start=True, stop=False).then_inc(s_ogu, 1)
                    seen = used - 1 if used else 0
                    with pe.Fori(0, JB) as i:
                        for c in range(4):
                            pe.wait_ge(s_og, 4 * i + c + 1 + seen)
                            nc.tensor.matmul(out[:, :], og[:, c, 0:G], orr[:, c, :], start=False, stop=False).then_inc(s_ogu, 1)
                    nc.tensor.matmul(out[:, :], K["zeros_bf"][:, 0:G], K["zeros_bf"][:, 0:1].to_broadcast([P, GN]),
                                     start=False, stop=True).then_inc(s_pe, 1)

                count_nodes(pe, p_h, 0)
                pe.wait_ge(s_v, at["rows"])
                for x, rows in enumerate((rs, rd, rk)):
                    if x == 2:
                        pe.wait_ge(s_v, at["evac0"])
                    for b in range(GT):
                        last = nc.tensor.transpose(p_t[x % 2][:, b * JB:(b + 1) * JB], rows[:, b, :], idn[0:JB, 0:JB])
                    last.then_inc(s_pe, 1)
                pe.wait_ge(s_v, at["hist"])
                for b in range(GT):
                    nc.tensor.transpose(p_t[0][0:TN, b * G:(b + 1) * G], histn[:, b * TN:(b + 1) * TN], idn[0:G, 0:G])
                nc.tensor.matmul(p_t[0][0:G, 501:502], K["ltri"][0:G, 0:G], hscan[:, GT - 1:GT], start=True, stop=True).then_inc(s_pe, 1)
                pe.wait_ge(s_v, at["key_onehots"])
                for j in range(NJ):
                    last = nc.tensor.matmul(p_c[:, j:j + 1], ohk[:, j, :], ones_bf[:, 0:1], start=True, stop=True)
                last.then_inc(s_pe, 1)
                pe.wait_ge(s_v, at["scan"])
                nc.tensor.matmul(p_t[1][0:G, 500:501], K["ltri"][0:G, 0:G], scan[:, NJ - 1:NJ], start=True, stop=True).then_inc(s_pe, 1)
                pe.wait_ge(s_v, at["base"])
                for b in range(GT):
                    last = nc.tensor.transpose(p_t[0][0:JB, b * G:(b + 1) * G], cnt[:, b * JB:(b + 1) * JB], idn[0:G, 0:G])
                last.then_inc(s_pe, 1)
                pe.wait_ge(s_v, at["nlow"])
                nc.tensor.matmul(p_t[1][0:1, 501:502], small[0:JB, 0:1], K["ones"][0:JB, 0:1], start=True, stop=True).then_inc(s_pe, 1)
                for i in range(JB):
                    if i >= 2:
                        pe.wait_ge(s_v, at[f"prod{i - 2}"])
                    nc.tensor.matmul(p_r[i % 2][:, 0:4 * G], ltri_bf[:, :],
                                     ohk[:, 4 * i:4 * i + 4, :].rearrange("p c g -> p (c g)"), start=True, stop=False)
                    for c in range(4):
                        b, q = divmod(4 * i + c, JB)
                        last = nc.tensor.matmul(p_r[i % 2][:, c * G:(c + 1) * G], idn[0:JB, q:q + 1].to_broadcast([JB, P]),
                                                baset[:, b, :], start=False, stop=c == 3)
                    last.then_inc(s_rank, 1)
                count_nodes(pe, p_d, NJ + 1)
                pe.wait_ge(s_v, at["histd"])
                for b in range(GT):
                    last = nc.tensor.transpose(p_t[0][0:TN, b * G:(b + 1) * G], K["deg_rows"][:, b * TN:(b + 1) * TN], idn[0:G, 0:G])
                last.then_inc(s_pe, 1)


def constants_phase(nc, K):
    with ExitStack() as ctx:
        m = Mem(nc, ctx, "const")
        passed = m.sem("passed")
        s_m = m.sem("memset")
        s_d = m.sem("done")
        with nc.Block() as block:
            @block.gpsimd
            def _(pool):
                nc.gpsimd.memset(K["ident"][:, :], 0.0).then_inc(s_m, 1)
                nc.gpsimd.memset(K["ltri"][:, :], 1.0).then_inc(s_m, 1)
                nc.gpsimd.memset(K["ones"][:, :], 1.0).then_inc(s_m, 1)
                nc.gpsimd.memset(K["eps"][:, :], EPS).then_inc(s_m, 1)
                nc.gpsimd.memset(K["ones_bf"][:, :], 1.0).then_inc(s_m, 1)
                nc.gpsimd.memset(K["zeros_bf"][:, :], 0.0).then_inc(s_m, 1)
                nc.gpsimd.iota(K["iota"][:, :], [[1, GN]], 0, 0, allow_small_or_imprecise_dtypes=True).then_inc(s_m, 1)
                nc.gpsimd.iota(K["tbase"][:, :], [[TN, T]], 0, 0, allow_small_or_imprecise_dtypes=True).then_inc(s_m, 1)
                pool.wait_ge(s_m, 8)
                nc.gpsimd.affine_select(out=K["ident"][:, :], in_=K["ident"][:, :], compare_op=ALU.not_equal, fill=1.0,
                                        base=0, pattern=[[-1, P]], channel_multiplier=1).then_inc(s_d, 1)
                nc.gpsimd.affine_select(out=K["ltri"][:, :], in_=K["ltri"][:, :], compare_op=ALU.is_gt, fill=0.0,
                                        base=0, pattern=[[1, P]], channel_multiplier=-1).then_inc(s_d, 1)

            @block.vector
            def _(dve):
                dve.wait_ge(s_d, 2)
                nc.vector.tensor_copy(K["ltri_bf"][:, :], K["ltri"][:, :]).then_inc(s_d, 1)
                dve.wait_ge(s_d, 3)



def index_phase(nc, K, t):
    with ExitStack() as ctx:
        m = Mem(nc, ctx, "index")
        passed = m.sem("passed")
        row = m.sb("row", [1, 2, T], I32)
        bins = m.sb("bins", [1, 2, G], I32)
        many = m.sb("many", [G, 2, T], I32)
        more = m.sb("more", [G, 2, G])
        left = m.sb("left", [G, G])
        after = m.sb("after", [G, 2])
        afteri = m.sb("afteri", [G, 4], I32)
        anyi = m.sb("anyi", [1, 2], I32)
        de = m.sb("de", [P, T, 2], I32)
        se = m.sb("se", [P, G, 2], I32)
        f = m.sb("f", [P, T])
        s_row = m.sem("rows")
        s_de = m.sem("dst_chunks")
        s_se = m.sem("src_chunks")
        s_v = m.sem("dve")
        s_deg = m.sem("degree")
        s_isq = m.sem("inverse_root")
        s_after = m.sem("after")
        s_list = m.sem("list")
        QUADS = T // GT
        SPQ = QUADS - QUADS // 3
        with nc.Block() as block:
            def dst_chunks(eng, g):
                first = [eng.alloc_register(f"first{c}") for c in range(GT)]
                eng.load(first, row[0:1, 0, bass.ds(GT * g, GT)])
                for c in range(GT):
                    at = eng.snap(first[c], min_val=0, max_val=E)
                    eng.dma_start(de[:, bass.ds(GT * g + c, 1), :].rearrange("p o c -> p (o c)"),
                                  t["edges"][bass.ds(at, P), :]).then_inc(s_de, 16)

            @block.sync
            def _(sp):
                sp.dma_start(row[:, :, :], t["row_dram"].unsqueeze(0)).then_inc(s_row, 16)
                sp.dma_start(bins[:, :, :], t["bin_dram"].unsqueeze(0)).then_inc(s_row, 16)
                sp.dma_start(many[:, 0, :], t["row_dram"][1:2, :].to_broadcast([G, T])).then_inc(s_row, 16)
                sp.dma_start(many[:, 1, 0:G], t["bin_dram"][1:2, :].to_broadcast([G, G])).then_inc(s_row, 16)
                sp.wait_ge(s_row, 64)
                with sp.Fori(0, SPQ) as g:
                    dst_chunks(sp, g)
                sp.wait_ge(s_after, 1)
                for x, side in enumerate(("next_dst", "next_src")):
                    sp.dma_start(K[side][0:1, 1:G + 1], afteri[:, x:x + 1], allow_slow_non_contiguous=True).then_inc(s_list, 16)
                    sp.dma_start(K[side][0:1, 0:1], anyi[:, x:x + 1]).then_inc(s_list, 16)
                sp.wait_ge(s_list, 64)

            @block.scalar
            def _(act):
                act.wait_ge(s_row, 64)
                act.sem_inc(passed, 1)
                with act.Fori(0, (G - 1) // GT) as i:
                    first = [act.alloc_register(f"bin{c}") for c in range(GT)]
                    act.load(first, bins[0:1, 0, bass.ds(GT * i, GT)])
                    for c in range(GT):
                        at = act.snap(first[c], min_val=0, max_val=E)
                        act.dma_start(se[:, bass.ds(GT * i + c, 1), :].rearrange("p o c -> p (o c)"),
                                      t["by_src"][bass.ds(at, P), :]).then_inc(s_se, 16)
                at = act.value_load(bins[0:1, 0, G - 1:G], min_val=0, max_val=E)
                act.dma_start(se[:, G - 1, :], t["by_src"][bass.ds(at, P), :]).then_inc(s_se, 16)
                with act.Fori(SPQ, QUADS) as g:
                    dst_chunks(act, g)
                act.wait_ge(s_deg, 1)
                nc.scalar.activation(K["isq"][:, :], K["inv_dst"][:, :], ACT.Sqrt).then_inc(s_isq, 1)
                act.wait_ge(s_isq, 1)

            @block.vector
            def _(dve):
                n = [0]

                def seq(ins):
                    n[0] += 1
                    ins.then_inc(s_v, 1)
                    dve.wait_ge(s_v, n[0])

                dve.wait_ge(s_row, 64)
                seq(nc.vector.tensor_copy(K["starts"][:, :], row[:, 0, :]))
                seq(nc.vector.tensor_copy(K["bstarts"][:, :], bins[:, 0, :]))
                seq(nc.vector.tensor_reduce(K["more_dst"][:, :], row[:, 1, :].rearrange("o (g c) -> o g c", c=GT), AX.X, ALU.max))
                seq(nc.vector.tensor_copy(K["more_src"][:, :], bins[:, 1, :]))
                seq(nc.vector.tensor_reduce(more[:, 0, :], many[:, 0, :].rearrange("o (g c) -> o g c", c=GT), AX.X, ALU.max))
                seq(nc.vector.tensor_copy(more[:, 1, :], many[:, 1, 0:G]))
                seq(nc.vector.tensor_scalar(left[:, :], K["iota"][0:G, 0:G], -1.0, float(G), ALU.mult, ALU.add))
                for x in range(2):
                    seq(nc.vector.tensor_scalar(more[:, x, :], more[:, x, :], 0.0, None, ALU.is_gt))
                    seq(nc.vector.tensor_tensor(more[:, x, :], more[:, x, :], left[:, :], ALU.mult))
                    seq(nc.vector.tensor_reduce(after[0:1, x:x + 1], more[0:1, x, :], AX.X, ALU.max))
                    seq(nc.vector.tensor_scalar(anyi[:, x:x + 1], after[0:1, x:x + 1], -1.0, float(G), ALU.mult, ALU.add))
                    seq(nc.vector.tensor_tensor(more[:, x, :], more[:, x, :], K["ltri"][0:G, 0:G], ALU.mult))
                    seq(nc.vector.tensor_reduce(after[:, x:x + 1], more[:, x, :], AX.X, ALU.max))
                seq(nc.vector.tensor_scalar(afteri[:, 0:2], after[:, :], -1.0, float(G), ALU.mult, ALU.add))
                dve.sem_inc(s_after, 1)
                seq(nc.vector.tensor_scalar(f[0:TN, :], K["deg_dst"][:, :], 1.0, None, ALU.max))
                nc.vector.reciprocal(K["inv_dst"][:, :], f[0:TN, :]).then_inc(s_deg, 1)
                dve.wait_ge(s_isq, 1)
                seq(nc.vector.tensor_tensor(f[0:TN, :], f[0:TN, :], K["isq"][:, :], ALU.mult))
                seq(nc.vector.tensor_tensor(f[0:TN, :], f[0:TN, :], K["isq"][:, :], ALU.mult))
                seq(nc.vector.tensor_scalar(f[0:TN, :], f[0:TN, :], -0.5, 1.5, ALU.mult, ALU.add))
                seq(nc.vector.tensor_tensor(K["isq"][:, :], K["isq"][:, :], f[0:TN, :], ALU.mult))
                seq(nc.vector.tensor_scalar(f[0:TN, :], K["deg_src"][:, :], 1.0, None, ALU.max))
                seq(nc.vector.reciprocal(K["inv_src"][:, :], f[0:TN, :]))
                dve.wait_ge(s_se, 16 * G)
                seq(nc.vector.tensor_copy(f[:, 0:G], se[:, :, 0]))
                seq(nc.vector.tensor_tensor(K["rel_src"][:, 0:G], f[:, 0:G], K["tbase"][:, 0:T:GT], ALU.subtract))
                seq(nc.vector.tensor_copy(K["idx_src"][:, 0:G], se[:, :, 1]))
                dve.wait_ge(s_de, 16 * T)
                seq(nc.vector.tensor_copy(f[:, :], de[:, :, 1]))
                seq(nc.vector.tensor_tensor(K["rel_dst"][:, 0:T], f[:, :], K["tbase"][:, :], ALU.subtract))
                seq(nc.vector.tensor_scalar(K["idx_dst"][:, 0:T], de[:, :, 0], N - 1, None, ALU.min))
                seq(nc.vector.memset(K["rel_dst"][:, T:T + AHEAD], -1.0))
                seq(nc.vector.memset(K["idx_dst"][:, T:T + AHEAD], 0))
                seq(nc.vector.memset(K["rel_src"][:, G:G + 3], -1.0))
                seq(nc.vector.memset(K["idx_src"][:, G:G + 3], 0))


def groups(eng, n, body):
    for g in range(4):
        body(g, g, g == n - 1)
    with eng.Fori(1, (n - 1) // 4) as i:
        for q in range(4):
            body(4 * i + q, q, False)
    body(n - 1, 0, True)


def earlier(g, q, slots, n):
    return n * (g // slots) if isinstance(g, int) else (n // slots) * (g - q % slots)


def wait(eng, sem, value):
    if not isinstance(value, int) or value > 0:
        eng.wait_ge(sem, value)


def at_most(eng, value, top):
    return (value - (value - top) * (value > top)).with_bounds(min_val=0, max_val=top)


def alone(eng, sem, value, passed):
    if not isinstance(value, int) or value > 0:
        eng.wait_ge(sem, value)
        eng.sem_inc(passed, 1)


class Beyond:

    def __init__(self, eng, K, passed, side, counted=None):
        self.eng, self.passed = eng, passed
        self.more, self.after = K["more_" + side], K["next_" + side]
        self.group = eng.alloc_register()
        eng.load([self.group], self.after[0:1, 0:1])
        if counted:
            self.count = counted.count
        else:
            self.count = eng.alloc_register()
            eng.reg_mov(self.count, 0)

    def each(self, g, chunk):
        eng = self.eng
        eng.sem_inc(self.passed, 1)
        with eng.If(eng.snap(self.group, min_val=0, max_val=G) == g):
            more = eng.value_load(self.more[0:1, bass.ds(g, 1)], min_val=0, max_val=NJ)
            eng.load([self.group], self.after[0:1, bass.ds(g + 1, 1)])
            with eng.Fori(0, more) as c:
                before = eng.snap(self.count, min_val=0, max_val=1 << 20)
                eng.reg_add(self.count, self.count, 1)
                chunk(c, before, before + 1)


class Overflow:

    def __init__(self, nc, m, K, t, table, width):
        self.nc, self.K, self.t, self.table, self.width = nc, K, t, table, width
        self.e = m.sb("over_e", [P, GT, 2], I32)
        self.i = m.sb("over_i", [P, GT, 1], I32)
        self.f = m.sb("over_f", [P, GT])
        self.M = m.sb("over_M", [P, GT, TN])
        self.V = m.sb("over_V", [P, GT, width])
        self.s_e = m.sem("over_edges")
        self.s_f = m.sem("over_float")
        self.s_r = m.sem("over_rel")
        self.s_hot = m.sem("over_onehot")
        self.s_g = m.sem("over_gather")
        self.s_mm = m.sem("over_sum")
        self.s_done = m.sem("over_added")


def layer_norm(nc, dve, seq, x, stats, mv, out, s_var, s_std, n, passed):
    for c in range(GT):
        last = nc.vector.bn_stats(stats[:, c, :], x[:, c, :])
    seq(last)
    dve.sem_inc(passed, 1)
    for c in range(GT):
        last = nc.vector.bn_aggr(mv[:, c, :], stats[:, c, :])
    last.then_inc(s_var, 1)
    dve.wait_ge(s_std, n)
    seq(nc.vector.reciprocal(mv[:, :, 1], mv[:, :, 1]))
    seq(nc.vector.tensor_tensor(out, x, mv[:, :, 0:1].to_broadcast([TN, GT, D]), ALU.subtract))
    return nc.vector.tensor_tensor(out, out, mv[:, :, 1:2].to_broadcast([TN, GT, D]), ALU.mult)


def deviation(nc, act, K, mv, s_var, s_std, g):
    act.wait_ge(s_var, g + 1)
    nc.scalar.activation(mv[:, :, 1], mv[:, :, 1], ACT.Sqrt, bias=K["eps"][0:TN, 0:1]).then_inc(s_std, 1)


def sums_pass(nc, K, t, name, n, table, weight, out, scale=None, read_r=None, write_r=None,
              minus=None, twice=1.0, norm=False):
    cheb = read_r is not None
    with ExitStack() as ctx:
        m = Mem(nc, ctx, name)
        passed = m.sem("passed")
        V = m.sb("V", [P, 4, GT, D])
        M = m.sb("M", [P, 4, GT, TN])
        cur = m.sb("cur", [P, 4, GT, 1], I32)
        ST = m.sb("ST", [D, 2, GN])
        R = m.sb("R", [TN, 2, GT, D])
        Y = m.sb("Y", [TN, 2, GT, D])
        yo = m.sb("yo", [TN, 2, GT, D])
        tmp = m.sb("tmp", [TN, GT, D])
        stats = m.sb("stats", [TN, GT, 6])
        mv = m.sb("mv", [TN, GT, 2])
        o = Overflow(nc, m, K, t, table, D)
        pst = [m.ps(f"pst{i}", [P, 512]) for i in range(2)]
        pout = [m.ps(f"pout{i}", [P, 512]) for i in range(2)]
        psn = [m.ps(f"psn{i}", [P, 512]) for i in range(2)]
        pov = m.ps("pov", [P, 512])
        s_cur = m.sem("indices")
        s_g = [m.sem(f"gathered{i}") for i in range(4)]
        s_hot = m.sem("onehot")
        s_sum = m.sem("summed")
        s_ev = m.sem("sum_in_sbuf")
        s_pr = m.sem("projected")
        s_ch = m.sem("dve_chain")
        s_fin = m.sem("finished")
        s_var = m.sem("variance")
        s_std = m.sem("deviation")
        s_ld = [m.sem(f"loaded{i}") for i in range(2)]
        s_st = [m.sem(f"stored{i}") for i in range(2)]
        loads = (1 if cheb else 0) + (1 if minus is not None else 0)
        stores = 1 + (1 if write_r is not None else 0)

        def rows(a, g):
            return a[bass.ds(g * GN, GN), :].rearrange("(c p) d -> p c d", p=TN)

        def scal(a, g):
            return a[:, bass.ds(GT * g, GT)].unsqueeze(2).to_broadcast([TN, GT, D])

        with nc.Block() as block:
            @block.gpsimd
            def _(pool):
                beyond = Beyond(pool, K, passed, "dst")

                def gather(g, q):
                    alone(pool, s_sum, g - 3, passed)
                    alone(pool, s_cur, g + 1, passed)
                    for x in range(GT):
                        pool.indirect_dma_start(V[:, q, x, :], None, table[:, :],
                                                bass.IndirectOffsetOnAxis(ap=cur[:, q, x, :], axis=0)).then_inc(s_g[q], 16)

                def overflow(g):
                    def chunk(c, before, k):
                        for x in range(GT):
                            first = pool.value_load(K["starts"][0:1, bass.ds(GT * g + x, 1)], min_val=0, max_val=E)
                            at = at_most(pool, first + (c + 1) * P, E)
                            pool.dma_start(o.e[:, x, :], t["edges"][bass.ds(at, P), :]).then_inc(o.s_e, 16)
                        alone(pool, o.s_hot, k, passed)
                        for x in range(GT):
                            pool.indirect_dma_start(o.V[:, x, :], None, table[:, :],
                                                    bass.IndirectOffsetOnAxis(ap=o.i[:, x, :], axis=0)).then_inc(o.s_g, 16)
                        alone(pool, o.s_done, k, passed)
                    beyond.each(g, chunk)

                def body(g, q, last):
                    if not last:
                        gather(g + 1, (q + 1) % 4)
                    overflow(g)
                gather(0, 0)
                groups(pool, n, body)

            @block.scalar
            def _(act):
                def indices(g, q):
                    wait(act, s_sum, g - 3)
                    nc.scalar.copy(cur[:, q, :, 0], K["idx_dst"][:, bass.ds(GT * g, GT)]).then_inc(s_cur, 1)

                def copy_sums(g, b):
                    act.wait_ge(s_sum, g + 1)
                    wait(act, s_pr, g - 1)
                    nc.scalar.copy(ST[:, b, :], pst[b][:, 0:GN]).then_inc(s_ev, 1)

                def body(g, q, last):
                    if not (isinstance(g, int) and g + 3 >= n):
                        indices(g + 3, (q + 3) % 4)
                    if not last:
                        copy_sums(g + 1, (q + 1) % 2)
                    if norm:
                        deviation(nc, act, K, mv, s_var, s_std, g)
                for g in range(3):
                    indices(g, g)
                copy_sums(0, 0)
                groups(act, n, body)

            @block.tensor
            def _(pe):
                beyond = Beyond(pe, K, passed, "dst")

                def sums(g, q):
                    b = q % 2
                    pe.wait_ge(s_g[q], earlier(g, q, 4, 64) + 64)
                    pe.wait_ge(s_hot, g + 1)
                    wait(pe, s_ev, g - 1)
                    for x in range(GT):
                        last = nc.tensor.matmul(pst[b][:, x * TN:(x + 1) * TN], V[:, q, x, :], M[:, q, x, :], start=True, stop=True)
                    last.then_inc(s_sum, 1)

                def overflow(g):
                    def chunk(c, before, k):
                        pe.wait_ge(o.s_g, k * 64)
                        for x in range(GT):
                            last = nc.tensor.matmul(pov[:, x * TN:(x + 1) * TN], o.V[:, x, :], o.M[:, x, :], start=True, stop=True)
                        last.then_inc(o.s_mm, 1)
                        pe.wait_ge(o.s_done, k)
                    beyond.each(g, chunk)

                def project(g, b):
                    pe.wait_ge(s_ev, g + 1)
                    wait(pe, s_fin, g - 1)
                    for x in range(GT):
                        last = nc.tensor.matmul(pout[b][0:TN, x * D:(x + 1) * D], ST[:, b, x * TN:(x + 1) * TN], weight[:, :], start=True, stop=True)
                    if cheb and not norm:
                        for x in range(GT):
                            last = nc.tensor.transpose(psn[b][0:TN, x * D:(x + 1) * D], ST[:, b, x * TN:(x + 1) * TN], K["ident"][:, :])
                    last.then_inc(s_pr, 1)

                def body(g, q, last):
                    if not last:
                        sums(g + 1, (q + 1) % 4)
                    overflow(g)
                    project(g, q % 2)
                sums(0, 0)
                groups(pe, n, body)

            @block.vector
            def _(dve):
                beyond = Beyond(dve, K, passed, "dst")
                CH = 5 if norm else 1 if minus is None else 2

                def onehot(g, q):
                    wait(dve, s_sum, g - 3)
                    nc.vector.tensor_tensor(M[:, q, :, :], K["iota"][:, 0:TN].unsqueeze(1).to_broadcast([P, GT, TN]),
                                            K["rel_dst"][:, bass.ds(GT * g, GT)].unsqueeze(2).to_broadcast([P, GT, TN]),
                                            ALU.is_equal).then_inc(s_hot, 1)

                def overflow(g, b):
                    def chunk(c, before, k):
                        dve.wait_ge(s_ev, g + 1)
                        dve.wait_ge(o.s_e, k * 64)
                        nc.vector.tensor_scalar(o.i[:, :, 0], o.e[:, :, 0], N - 1, None, ALU.min)
                        nc.vector.tensor_copy(o.f[:, :], o.e[:, :, 1]).then_inc(o.s_f, 1)
                        dve.wait_ge(o.s_f, k)
                        nc.vector.tensor_tensor(o.f[:, :], o.f[:, :], K["tbase"][:, bass.ds(GT * g, GT)], ALU.subtract).then_inc(o.s_r, 1)
                        dve.wait_ge(o.s_r, k)
                        nc.vector.tensor_tensor(o.M[:, :, :], K["iota"][:, 0:TN].unsqueeze(1).to_broadcast([P, GT, TN]),
                                                o.f[:, :].unsqueeze(2).to_broadcast([P, GT, TN]), ALU.is_equal).then_inc(o.s_hot, 1)
                        dve.wait_ge(o.s_mm, k)
                        nc.vector.tensor_tensor(ST[:, b, :], ST[:, b, :], pov[:, 0:GN], ALU.add).then_inc(o.s_done, 1)
                        dve.wait_ge(o.s_done, k)
                    beyond.each(g, chunk)

                def finish(g, b):
                    n_ch = [0]

                    def seq(ins):
                        n_ch[0] += 1
                        ins.then_inc(s_ch, 1)
                        dve.wait_ge(s_ch, CH * g + n_ch[0])
                    dve.wait_ge(s_pr, g + 1)
                    wait(dve, s_st[b], earlier(g, b, 2, 16 * stores))
                    v = pout[b][0:TN, :].rearrange("p (c d) -> p c d", c=GT)
                    if not cheb:
                        nc.vector.tensor_tensor(yo[:, b, :, :], v, scal(scale, g), ALU.mult).then_inc(s_fin, 1)
                        return
                    wait(dve, s_fin, g)
                    seq(nc.vector.tensor_tensor(tmp[:, :, :], v, scal(K["isq"], g), ALU.mult))
                    dve.wait_ge(s_ld[b], earlier(g, b, 2, 16 * loads) + 16 * loads)
                    if not norm:
                        nc.vector.tensor_tensor(R[:, b, :, :], R[:, b, :, :], tmp[:, :, :], ALU.add)
                        sn = psn[b][0:TN, :].rearrange("p (c d) -> p c d", c=GT)
                        scaled = nc.vector.tensor_tensor(yo[:, b, :, :], sn, scal(K["inv_dst"], g), ALU.mult)
                        if minus is None:
                            scaled.then_inc(s_fin, 1)
                        else:
                            seq(scaled)
                            nc.vector.scalar_tensor_tensor(yo[:, b, :, :], yo[:, b, :, :], twice, Y[:, b, :, :],
                                                           ALU.mult, ALU.subtract).then_inc(s_fin, 1)
                        return
                    seq(nc.vector.tensor_tensor(tmp[:, :, :], R[:, b, :, :], tmp[:, :, :], ALU.add))
                    layer_norm(nc, dve, seq, tmp[:, :, :], stats, mv, yo[:, b, :, :], s_var, s_std, g + 1, passed).then_inc(s_fin, 1)

                def body(g, q, last):
                    if not (isinstance(g, int) and g + 2 >= n):
                        onehot(g + 2, (q + 2) % 4)
                    overflow(g, q % 2)
                    finish(g, q % 2)
                onehot(0, 0)
                onehot(1, 1)
                groups(dve, n, body)

            @block.sync
            def _(sp):
                def load(g, b):
                    alone(sp, s_fin, g - 1, passed)
                    if write_r is not None:
                        alone(sp, s_st[b], earlier(g, b, 2, 16 * stores), passed)
                    if cheb:
                        sp.dma_start(R[:, b, :, :], rows(read_r, g)).then_inc(s_ld[b], 16)
                    if minus is not None:
                        sp.dma_start(Y[:, b, :, :], rows(minus, g)).then_inc(s_ld[b], 16)

                def body(g, q, last):
                    b = q % 2
                    if not last and loads:
                        load(g + 1, 1 - b)
                    alone(sp, s_fin, g + 1, passed)
                    sp.dma_start(rows(out, g), yo[:, b, :, :]).then_inc(s_st[b], 16)
                    if write_r is not None:
                        sp.dma_start(rows(write_r, g), R[:, b, :, :]).then_inc(s_st[b], 16)
                if loads:
                    load(0, 0)
                groups(sp, n, body)
                sp.wait_ge(s_st[0], 16 * stores * ((n + 1) // 2))
                sp.wait_ge(s_st[1], 16 * stores * ((n - 1) // 2))


def weights_phase(nc, K, t):
    with ExitStack() as ctx:
        m = Mem(nc, ctx, "weights")
        passed = m.sem("passed")
        att = m.sb("att", [P, 2, D])
        prod = m.sb("prod", [P, 2, D])
        w3 = m.sb("w3", [D, 4, D])
        s_ld = m.sem("loaded")
        s_v = m.sem("dve")
        with nc.Block() as block:
            @block.sync
            def _(sp):
                for dst, src in ((K["W01"], t["L0_gnn_W1"]), (K["W02"], t["L0_gnn_W2"]), (K["W1a"], t["L2_gnn_W1"][0:D, :]),
                                 (K["W1b"], t["L2_gnn_W1"][D:2 * D, :]), (K["W2"], t["L2_gnn_W2"]), (K["W3"], t["L2_gnn_W3"])):
                    sp.dma_start(dst[:, :], src).then_inc(s_ld, 16)
                sp.dma_start(K["Watt"][:, 0:D], t["L1_gnn_W"]).then_inc(s_ld, 16)
                sp.dma_start(w3[:, :, :], t["L3_gnn_weights"].rearrange("k f o -> f k o")).then_inc(s_ld, 16)
                for x, name in enumerate(("L1_gnn_att_src", "L1_gnn_att_dst")):
                    sp.dma_start(att[:, x, :], t[name].rearrange("h d -> (h d)").unsqueeze(0).to_broadcast([P, D])).then_inc(s_ld, 16)
                for key, name in (("b01", "L0_gnn_b1"), ("b02", "L0_gnn_b2"), ("batt", "L1_gnn_bias"), ("b3", "L2_gnn_b3"),
                                  ("gamma", "L2_gnn_gamma"), ("beta", "L2_gnn_beta")):
                    sp.dma_start(K[key][:, :], t[name].unsqueeze(0).to_broadcast([P, D])).then_inc(s_ld, 16)
                for key, name in (("b1c", "L2_gnn_b1"), ("b2c", "L2_gnn_b2")):
                    sp.dma_start(K[key][:, :], t[name].unsqueeze(1)).then_inc(s_ld, 16)
                sp.wait_ge(s_ld, 16 * 18)

            @block.vector
            def _(dve):
                dve.wait_ge(s_ld, 16 * 18)
                nc.vector.tensor_tensor(prod[:, :, :], K["Watt"][:, 0:D].unsqueeze(1).to_broadcast([P, 2, D]), att[:, :, :],
                                        ALU.mult).then_inc(s_v, 1)
                dve.wait_ge(s_v, 1)
                nc.vector.tensor_reduce(K["Watt"][:, D:TW], prod[:, :, :].rearrange("p x (h d) -> p (x h) d", d=HD), AX.X, ALU.add)
                nc.vector.tensor_tensor(K["V0"][:, :], w3[:, 0, :], w3[:, 2, :], ALU.subtract)
                nc.vector.tensor_tensor(K["V1"][:, :], w3[:, 1, :], w3[:, 3, :], ALU.subtract)
                nc.vector.tensor_scalar(K["V2"][:, :], w3[:, 2, :], 2.0, None, ALU.mult)
                nc.vector.tensor_scalar(K["V3"][:, :], w3[:, 3, :], 2.0, None, ALU.mult).then_inc(s_v, 1)
                dve.wait_ge(s_v, 2)


def node_pass(nc, K, t, name, table, bias, out, x_in=None, att_out=None):
    second = x_in is not None
    with ExitStack() as ctx:
        m = Mem(nc, ctx, name)
        passed = m.sem("passed")
        V = m.sb("V", [P, 4, D])
        M = m.sb("M", [P, 4, GN])
        L = m.sb("L", [G, 4, D])
        cur = m.sb("cur", [P, 4, 1], I32)
        S = m.sb("S", [TN, 2, GT, D])
        lastrow = m.sb("lastrow", [P, D])
        X = m.sb("X", [TN, 2, GT, D])
        O = m.sb("O", [TN, 2, GT, D])
        XT = m.sb("XT", [D, 2, GN])
        A = m.sb("A", [TN, 2, GT, TW])
        stats = m.sb("stats", [TN, GT, 6])
        mv = m.sb("mv", [TN, GT, 2])
        oe = m.sb("over_e", [P, 2], I32)
        oi = m.sb("over_i", [P, 1], I32)
        of = m.sb("over_f", [P, 1])
        oM = m.sb("over_M", [P, GN])
        oV = m.sb("over_V", [P, D])
        oS = m.sb("over_S", [TN, GT, D])
        ps = [m.ps(f"ps{i}", [P, 512]) for i in range(2)]
        pt = m.ps("pt", [P, 512])
        pa = [m.ps(f"pa{i}", [P, 512]) for i in range(2)]
        pov = m.ps("pov", [P, 512])
        s_row = m.sem("last_row")
        s_cur = m.sem("indices")
        s_g = [m.sem(f"gathered{i}") for i in range(4)]
        s_hot = m.sem("operands")
        s_sum = m.sem("summed")
        s_ev = m.sem("sum_in_sbuf")
        s_bias = m.sem("bias_added")
        s_ch = m.sem("dve_chain")
        s_fin = m.sem("finished")
        s_var = m.sem("variance")
        s_std = m.sem("deviation")
        s_tr = m.sem("transposed")
        s_xt = m.sem("transpose_in_sbuf")
        s_at = m.sem("attention_rows")
        s_ac = m.sem("attention_in_sbuf")
        s_ld = [m.sem(f"loaded{i}") for i in range(2)]
        s_st = [m.sem(f"stored{i}") for i in range(2)]
        s_sa = [m.sem(f"stored_att{i}") for i in range(2)]
        so_e, so_f, so_rel, so_hot, so_g, so_mm, so_sc, so_done = [m.sem(f"over_{x}") for x in (
            "edges", "float", "rel", "onehot", "gather", "sum", "scaled", "added")]

        def rows(a, g):
            return a[bass.ds(g * GN, GN), :].rearrange("(c p) d -> p c d", p=TN)

        with nc.Block() as block:
            @block.gpsimd
            def _(pool):
                beyond = Beyond(pool, K, passed, "src")

                def gather(g, q):
                    alone(pool, s_sum, g - 3, passed)
                    alone(pool, s_cur, g + 1, passed)
                    pool.indirect_dma_start(V[:, q, :], None, table[:, :],
                                            bass.IndirectOffsetOnAxis(ap=cur[:, q, :], axis=0)).then_inc(s_g[q], 16)

                def add_bias(g, b):
                    if second:
                        pool.wait_ge(s_ld[b], earlier(g, b, 2, 16) + 16)
                    else:
                        pool.wait_ge(s_ev, g + 1)
                    a = X if second else S
                    nc.gpsimd.tensor_tensor(a[:, b, :, :], a[:, b, :, :], bias[0:TN, :].unsqueeze(1).to_broadcast([TN, GT, D]),
                                            ALU.add).then_inc(s_bias, 1)

                def overflow(g):
                    def chunk(c, before, k):
                        first = pool.value_load(K["bstarts"][0:1, bass.ds(g, 1)], min_val=0, max_val=E)
                        at = at_most(pool, first + (c + 1) * P, E)
                        pool.dma_start(oe[:, :], t["by_src"][bass.ds(at, P), :]).then_inc(so_e, 16)
                        alone(pool, so_rel, k, passed)
                        pool.indirect_dma_start(oV[:, :], None, table[:, :],
                                                bass.IndirectOffsetOnAxis(ap=oi[:, :], axis=0)).then_inc(so_g, 16)
                        alone(pool, so_done, k, passed)
                    beyond.each(g, chunk)

                def body(g, q, last):
                    if not (isinstance(g, int) and g + 2 >= G):
                        gather(g + 2, (q + 2) % 4)
                    add_bias(g, q % 2)
                    overflow(g)
                gather(0, 0)
                gather(1, 1)
                groups(pool, G, body)
                pool.wait_ge(s_g[1], 16 * ((G - 1) // 4 + 1))

            @block.scalar
            def _(act):
                def indices(g, q):
                    wait(act, s_sum, g - 3)
                    nc.scalar.copy(cur[:, q, :], K["idx_src"][:, bass.ds(g, 1)]).then_inc(s_cur, 1)

                def scaled_sums(g, b):
                    act.wait_ge(s_sum, g + 1)
                    wait(act, s_fin, g - 1)
                    for x in range(GT):
                        done = nc.scalar.activation(S[:, b, x, :], ps[b][0:TN, x * D:(x + 1) * D], ACT.Copy,
                                                    scale=K["inv_src"][:, bass.ds(GT * g + x, 1)])
                    done.then_inc(s_ev, 1)

                def attention_rows(g, b):
                    act.wait_ge(s_at, g + 1)
                    wait(act, s_sa[b], earlier(g, b, 2, 16))
                    for h in range(2):
                        done = nc.scalar.copy(A[:, b, 2 * h:2 * h + 2, :],
                                              pa[h][0:TN, 0:2 * TW].rearrange("p (c d) -> p c d", c=2))
                    done.then_inc(s_ac, 1)

                def body(g, q, last):
                    b = q % 2
                    if not (isinstance(g, int) and g + 3 >= G):
                        indices(g + 3, (q + 3) % 4)
                    if not last:
                        scaled_sums(g + 1, 1 - b)
                    if second:
                        deviation(nc, act, K, mv, s_var, s_std, g)
                        if not (isinstance(g, int) and g == 0):
                            attention_rows(g - 1, 1 - b)
                        act.wait_ge(s_tr, g + 1)
                        nc.scalar.copy(XT[:, b, :], pt[:, 0:GN]).then_inc(s_xt, 1)
                for g in range(3):
                    indices(g, g)
                scaled_sums(0, 0)
                groups(act, G, body)
                if second:
                    attention_rows(G - 1, 0)

            @block.tensor
            def _(pe):
                beyond = Beyond(pe, K, passed, "src")

                def sums(g, q):
                    b = q % 2
                    pe.wait_ge(s_hot, g + 1)
                    wait(pe, s_ev, g - 1)
                    for x in range(GT):
                        nc.tensor.matmul(ps[b][0:TN, x * D:(x + 1) * D], K["deg_rows"][:, x * TN:(x + 1) * TN], L[:, q, :], start=True, stop=False)
                        last = nc.tensor.matmul(ps[b][0:TN, x * D:(x + 1) * D], M[:, q, x * TN:(x + 1) * TN], V[:, q, :], start=False, stop=True)
                    last.then_inc(s_sum, 1)

                def overflow(g):
                    def chunk(c, before, k):
                        pe.wait_ge(so_hot, k)
                        for x in range(GT):
                            last = nc.tensor.matmul(pov[0:TN, x * D:(x + 1) * D], oM[:, x * TN:(x + 1) * TN], oV[:, :], start=True, stop=True)
                        last.then_inc(so_mm, 1)
                        pe.wait_ge(so_done, k)
                    beyond.each(g, chunk)

                def attention_rows(g, b):
                    pe.wait_ge(s_xt, g + 1)
                    wait(pe, s_ac, g)
                    for x in range(GT):
                        done = nc.tensor.matmul(pa[x // 2][0:TN, (x % 2) * TW:(x % 2 + 1) * TW],
                                                XT[:, b, x * TN:(x + 1) * TN], K["Watt"][:, :], start=True, stop=True)
                    done.then_inc(s_at, 1)

                def body(g, q, last):
                    b = q % 2
                    if not last:
                        sums(g + 1, (q + 1) % 4)
                    overflow(g)
                    if second:
                        if not (isinstance(g, int) and g == 0):
                            attention_rows(g - 1, 1 - b)
                        pe.wait_ge(s_fin, g + 1)
                        wait(pe, s_xt, g)
                        for x in range(GT):
                            done = nc.tensor.transpose(pt[:, x * TN:(x + 1) * TN], O[:, b, x, :], K["ident"][0:TN, 0:TN])
                        done.then_inc(s_tr, 1)
                sums(0, 0)
                groups(pe, G, body)
                if second:
                    attention_rows(G - 1, 0)

            @block.vector
            def _(dve):
                beyond = Beyond(dve, K, passed, "src")
                CH = 4 if second else 0

                def operands(g, q):
                    wait(dve, s_sum, g - 3)
                    nc.vector.tensor_scalar(M[:, q, :], K["iota"][:, :], K["rel_src"][:, bass.ds(g, 1)], None, ALU.is_equal)
                    nc.vector.tensor_scalar(L[:, q, :], lastrow[0:G, :], K["ident"][0:G, bass.ds(g, 1)], None, ALU.mult)
                    dve.wait_ge(s_g[q], earlier(g, q, 4, 16) + 16)
                    nc.vector.tensor_tensor(V[:, q, :], V[:, q, :], lastrow[:, :], ALU.subtract).then_inc(s_hot, 1)

                def overflow(g, b):
                    def chunk(c, before, k):
                        dve.wait_ge(so_e, k * 16)
                        nc.vector.tensor_copy(oi[:, :], oe[:, 1:2])
                        nc.vector.tensor_copy(of[:, :], oe[:, 0:1]).then_inc(so_f, 1)
                        dve.wait_ge(so_f, k)
                        nc.vector.tensor_tensor(of[:, :], of[:, :], K["tbase"][:, bass.ds(GT * g, 1)], ALU.subtract).then_inc(so_rel, 1)
                        dve.wait_ge(so_rel, k)
                        nc.vector.tensor_scalar(oM[:, :], K["iota"][:, :], of[:, 0:1], None, ALU.is_equal)
                        dve.wait_ge(so_g, k * 16)
                        nc.vector.tensor_tensor(oV[:, :], oV[:, :], lastrow[:, :], ALU.subtract).then_inc(so_hot, 1)
                        dve.wait_ge(so_mm, k)
                        nc.vector.tensor_tensor(oS[:, :, :], pov[0:TN, :].rearrange("p (c d) -> p c d", c=GT),
                                                K["inv_src"][:, bass.ds(GT * g, GT)].unsqueeze(2).to_broadcast([TN, GT, D]),
                                                ALU.mult).then_inc(so_sc, 1)
                        dve.wait_ge(so_sc, k)
                        nc.vector.tensor_tensor(S[:, b, :, :], S[:, b, :, :], oS[:, :, :], ALU.add).then_inc(so_done, 1)
                        dve.wait_ge(so_done, k)
                    beyond.each(g, chunk)

                def finish(g, b):
                    n_ch = [0]

                    def seq(ins):
                        n_ch[0] += 1
                        ins.then_inc(s_ch, 1)
                        dve.wait_ge(s_ch, CH * g + n_ch[0])
                    wait(dve, s_st[b], earlier(g, b, 2, 16))
                    if not second:
                        nc.vector.tensor_scalar(O[:, b, :, :], S[:, b, :, :], 0.0, None, ALU.max).then_inc(s_fin, 1)
                        return
                    wait(dve, s_tr, g - 1)
                    seq(nc.vector.tensor_tensor(S[:, b, :, :], S[:, b, :, :], X[:, b, :, :], ALU.add))
                    layer_norm(nc, dve, seq, S[:, b, :, :], stats, mv, O[:, b, :, :], s_var, s_std, g + 1, passed).then_inc(s_fin, 1)
                    assert n_ch[0] == CH, n_ch

                def body(g, q, last):
                    if not (isinstance(g, int) and g + 2 >= G):
                        operands(g + 2, (q + 2) % 4)
                    dve.wait_ge(s_ev, g + 1)
                    dve.wait_ge(s_bias, g + 1)
                    overflow(g, q % 2)
                    finish(g, q % 2)
                dve.wait_ge(s_row, 16)
                operands(0, 0)
                operands(1, 1)
                groups(dve, G, body)

            @block.sync
            def _(sp):
                sp.dma_start(lastrow[:, :], table[HE - 1:HE, :].to_broadcast([P, D])).then_inc(s_row, 16)

                def body(g, q, last):
                    b = q % 2
                    if not last and second:
                        alone(sp, s_fin, g, passed)
                        sp.dma_start(X[:, 1 - b, :, :], rows(x_in, g + 1)).then_inc(s_ld[1 - b], 16)
                    if second and not (isinstance(g, int) and g == 0):
                        alone(sp, s_ac, g, passed)
                        sp.dma_start(rows(att_out, g - 1), A[:, 1 - b, :, :]).then_inc(s_sa[1 - b], 16)
                    alone(sp, s_fin, g + 1, passed)
                    sp.dma_start(rows(out, g), O[:, b, :, :]).then_inc(s_st[b], 16)
                if second:
                    sp.dma_start(X[:, 0, :, :], rows(x_in, 0)).then_inc(s_ld[0], 16)
                groups(sp, G, body)
                if second:
                    sp.wait_ge(s_ac, G)
                    sp.dma_start(rows(att_out, G - 1), A[:, 0, :, :]).then_inc(s_sa[0], 16)
                for b in range(2):
                    sp.wait_ge(s_st[b], 16 * ((G + 1 - b) // 2))
                    if second:
                        sp.wait_ge(s_sa[b], 16 * ((G + 1 - b) // 2))


def in_pairs(eng, steps):
    def run(pair):
        for step in steps:
            for g, b in pair:
                step(g, b, pair[0][0])
    run([(0, 0), (1, 1)])
    with eng.Fori(1, (G - 1) // 2) as i:
        run([(2 * i, 0), (2 * i + 1, 1)])
    run([(G - 1, 0)])


def attention_pass(nc, K, t):
    with ExitStack() as ctx:
        m = Mem(nc, ctx, "att")
        passed = m.sem("passed")
        V = m.sb("V", [P, 2, GT, TW])
        VX = m.sb("VX", [P, 2, GT, D])
        M = m.sb("M", [P, 2, GT, TN])
        MT = m.sb("MT", [TN, 2, GT, P])
        cur = m.sb("cur", [P, 2, GT, 1], I32)
        EA = m.sb("EA", [P, 2, GT, D])
        SELF = m.sb("SELF", [TN, 2, GT, TW])
        X = m.sb("X", [TN, 2, GT, D])
        A16 = m.sb("A16", [P, 2, 2, GT * HEADS])
        dT = m.sb("dT", [GT * HEADS, 2, P])
        ne = m.sb("ne", [GT * HEADS, 2, P + 1])
        rB = m.sb("rB", [GT * HEADS, 2, P])
        rm = m.sb("rm", [GT * HEADS, 2, P])
        RM = m.sb("RM", [P, 2, GT, HEADS + 1])
        z4 = m.sb("z4", [TN, 2, GT])
        Gm = m.sb("Gm", [TN, 2, GT, HEADS])
        N8 = m.sb("N8", [TN, 2, GT, 2 * HEADS])
        EXS = m.sb("EXS", [TN, 2, GT, HEADS])
        EX = m.sb("EX", [P, 2, GT, HEADS])
        NUM = m.sb("NUM", [TN, 2, GT, D])
        DEN = m.sb("DEN", [TN, 2, GT, HEADS])
        tmp = m.sb("tmp", [TN, 2, GT, D])
        x2 = m.sb("x2", [TN, 2, GT, D])
        XT = m.sb("XT", [D, 2, GN])
        AT = m.sb("AT", [D, 2, GN])
        H1 = m.sb("H1", [D, 2, GN])
        H2 = m.sb("H2", [D, 2, GN])
        y0 = m.sb("y0", [TN, 2, GT, D])
        r0 = m.sb("r0", [TN, 2, GT, D])
        stats = m.sb("stats", [TN, 2, GT, 6])
        mv = m.sb("mv", [TN, 2, GT, 2])
        oe = m.sb("oe", [P, GT, 2], I32)
        oi = m.sb("oi", [P, GT, 1], I32)
        of = m.sb("of", [P, GT])
        oM = m.sb("oM", [P, 1, GT, TN])
        oV = m.sb("oV", [P, 1, GT, TW])
        oMT = m.sb("oMT", [TN, 1, GT, P])
        oEA = m.sb("oEA", [P, 1, GT, D])
        oA16 = m.sb("oA16", [P, 1, 2, GT * HEADS])
        odT = m.sb("odT", [GT * HEADS, 1, P])
        one = m.sb("one", [GT * HEADS, 1, P + 1])
        orB = m.sb("orB", [GT * HEADS, 1, P])
        orm = m.sb("orm", [GT * HEADS, 1, P])
        oRM = m.sb("oRM", [P, 1, GT, HEADS + 1])
        oG = m.sb("oG", [TN, GT, HEADS])
        oEX = m.sb("oEX", [P, 1, GT, HEADS])
        P0, P1, P2, P3 = [[m.ps(f"p{i}{b}", [P, 512]) for b in range(2)] for i in range(4)]
        s_cur, s_hot, s_a16, s_q, s_rm, s_q2, s_rmc, s_pg, s_n8, s_mtp, s_mt, s_pn, s_exa, s_ex, s_vx, s_num, s_exs_in, \
            s_exs, s_agp, s_ag, s_mn, s_elu, s_x2, s_x2p, s_xt, s_h1p, s_h1, s_h2p, s_h2, s_h3p, s_x3, s_x3p, s_x3t, \
            s_r0p, s_fin, s_ch, s_var, s_std = [m.sem(x) for x in (
                "indices", "onehot", "a_columns", "a_rows_psum", "max_rows", "max_columns_psum", "max_columns", "node_max_psum",
                "node_values", "onehot_t_psum", "onehot_t", "edge_values_psum", "edge_exponent", "edge_exp", "messages",
                "sums_psum", "self_exponent", "self_exp", "edge_sums_psum", "edge_sums", "elu_exponent", "elu_exp", "x2",
                "x2_t_psum", "x2_t", "h1_psum", "h1", "h2_psum", "h2", "h3_psum", "x3", "x3_t_psum", "x3_t", "r0_psum",
                "finished", "dve_chain", "variance", "deviation")]
        s_g = [m.sem(f"gathered{i}") for i in range(2)]
        s_ld = [m.sem(f"loaded{i}") for i in range(2)]
        s_st = [m.sem(f"stored{i}") for i in range(2)]
        so_e, so_hot, so_g, so_pe, so_dv, so_ex, so_done, so_ch = [m.sem(f"over_{x}") for x in (
            "edges", "onehot", "gather", "pe_step", "dve_step", "exp", "done", "chain")]

        def rows(a, g):
            return a[bass.ds(g * GN, GN), :].rearrange("(c p) d -> p c d", p=TN)

        def use(g, b, n):
            return n * (g // 2) if isinstance(g, int) else (n // 2) * (g - b)

        def heads(a):
            return a.rearrange("p c (h d) -> p c h d", h=HEADS)

        def beyond(eng):
            maxima = Beyond(eng, K, passed, "dst")
            return maxima, Beyond(eng, K, passed, "dst", maxima)

        OC = 9

        def nth(g, b, g0, n):
            return n * (1 if isinstance(g0, int) and g0 == G - 1 else 2) + b + 1

        with nc.Block() as block:
            @block.gpsimd
            def _(pool):
                for_max, for_sums = beyond(pool)

                def gather(g, b, g0):
                    alone(pool, s_num, g - 1, passed)
                    alone(pool, s_cur, g + 1, passed)
                    for x in range(GT):
                        pool.indirect_dma_start(V[:, b, x, :], None, t["att"][:, :],
                                                bass.IndirectOffsetOnAxis(ap=cur[:, b, x, :], axis=0)).then_inc(s_g[b], 16)

                def over_gather(chunks):
                    def step(g, b, g0):
                        def chunk(c, before, k):
                            for x in range(GT):
                                first = pool.value_load(K["starts"][0:1, bass.ds(GT * g + x, 1)], min_val=0, max_val=E)
                                at = at_most(pool, first + (c + 1) * P, E)
                                pool.dma_start(oe[:, x, :], t["edges"][bass.ds(at, P), :]).then_inc(so_e, 16)
                                pool.dma_start(oEA[:, 0, x, :], t["edge_attr"][bass.ds(at, P), :]).then_inc(so_e, 16)
                            alone(pool, so_hot, k, passed)
                            for x in range(GT):
                                pool.indirect_dma_start(oV[:, 0, x, :], None, t["att"][:, :],
                                                        bass.IndirectOffsetOnAxis(ap=oi[:, x, :], axis=0)).then_inc(so_g, 16)
                            alone(pool, so_done, k, passed)
                        chunks.each(g, chunk)
                    return step
                in_pairs(pool, [gather, over_gather(for_max), over_gather(for_sums)])

            @block.sync
            def _(sp):
                def load(g, b, g0):
                    alone(sp, s_fin, g - 1, passed)
                    sp.dma_start(SELF[:, b, :, :], rows(t["att"], g)).then_inc(s_ld[b], 16)
                    sp.dma_start(X[:, b, :, :], rows(t["x1"], g)).then_inc(s_ld[b], 16)
                    for x in range(GT):
                        first = sp.value_load(K["starts"][0:1, bass.ds(GT * g + x, 1)], min_val=0, max_val=E)
                        sp.dma_start(EA[:, b, x, :], t["edge_attr"][bass.ds(first, P), :]).then_inc(s_ld[b], 16)

                def store(g, b, g0):
                    alone(sp, s_fin, g + 1, passed)
                    sp.dma_start(rows(t["y0"], g), y0[:, b, :, :]).then_inc(s_st[b], 16)
                    sp.dma_start(rows(t["r0"], g), r0[:, b, :, :]).then_inc(s_st[b], 16)
                in_pairs(sp, [load, store])
                sp.wait_ge(s_st[0], 32 * ((G + 1) // 2))
                sp.wait_ge(s_st[1], 32 * ((G - 1) // 2))

            @block.tensor
            def _(pe):
                for_max, for_sums = beyond(pe)
                idn = K["ident"]

                def a_rows(g, b, g0):
                    pe.wait_ge(s_a16, g + 1)
                    wait(pe, s_fin, g - 1)
                    for x in range(2):
                        done = nc.tensor.transpose(P0[b][0:16, x * P:(x + 1) * P], A16[:, b, x, :], idn[:, :])
                    done.then_inc(s_q, 1)
                    for x in range(GT):
                        done = nc.tensor.transpose(P1[b][0:TN, x * P:(x + 1) * P], M[:, b, x, :], idn[:, :])
                    done.then_inc(s_mtp, 1)

                def edge_sums(g, b, g0):
                    pe.wait_ge(s_ld[b], use(g, b, 96) + 96)
                    for x in range(GT):
                        done = nc.tensor.matmul(P3[b][:, x * TN:(x + 1) * TN], EA[:, b, x, :], M[:, b, x, :], start=True, stop=True)
                    done.then_inc(s_agp, 1)

                def max_columns(g, b, g0):
                    alone(pe, s_rm, g + 1, passed)
                    nc.tensor.transpose(P2[b][:, 0:16], rm[:, b, :], idn[0:16, 0:16]).then_inc(s_q2, 1)

                def node_max(g, b, g0):
                    pe.wait_ge(s_rmc, g + 1)
                    for x in range(GT):
                        done = nc.tensor.matmul(P2[b][0:TN, 64 + 5 * x:69 + 5 * x], M[:, b, x, :], RM[:, b, x, :], start=True, stop=True)
                    done.then_inc(s_pg, 1)

                def over_max(g, b, g0):
                    def chunk(c, before, k):
                        k1 = 3 * before
                        pe.wait_ge(so_dv, k1 + 1)
                        for x in range(2):
                            done = nc.tensor.transpose(P0[b][0:16, x * P:(x + 1) * P], oA16[:, 0, x, :], idn[:, :])
                        done.then_inc(so_pe, 1)
                        alone(pe, so_dv, k1 + 2, passed)
                        nc.tensor.transpose(P0[b][:, 256:272], orm[:, 0, :], idn[0:16, 0:16]).then_inc(so_pe, 1)
                        pe.wait_ge(so_dv, k1 + 3)
                        for x in range(GT):
                            done = nc.tensor.matmul(P0[b][0:TN, 320 + 5 * x:325 + 5 * x], oM[:, 0, x, :], oRM[:, 0, x, :], start=True, stop=True)
                        done.then_inc(so_pe, 1)
                        pe.wait_ge(so_done, k)
                    for_max.each(g, chunk)

                def edge_values(g, b, g0):
                    pe.wait_ge(s_mt, g + 1)
                    pe.wait_ge(s_n8, g + 1)
                    for x in range(GT):
                        done = nc.tensor.matmul(P2[b][:, 128 + 8 * x:136 + 8 * x], MT[:, b, x, :], N8[:, b, x, :], start=True, stop=True)
                    done.then_inc(s_pn, 1)

                def sums(g, b, g0):
                    pe.wait_ge(s_vx, g + 1)
                    for x in range(GT):
                        nc.tensor.matmul(P0[b][0:TN, x * D:(x + 1) * D], M[:, b, x, :], VX[:, b, x, :], start=True, stop=True)
                        done = nc.tensor.matmul(P2[b][0:TN, 256 + 4 * x:260 + 4 * x], M[:, b, x, :], EX[:, b, x, :], start=True, stop=True)
                    done.then_inc(s_num, 1)

                def over_sums(g, b, g0):
                    def chunk(c, before, k):
                        k1 = 3 * before
                        pe.wait_ge(so_dv, k1 + 1)
                        for x in range(GT):
                            done = nc.tensor.transpose(P1[b][0:TN, x * P:(x + 1) * P], oM[:, 0, x, :], idn[:, :])
                        done.then_inc(so_pe, 1)
                        pe.wait_ge(so_dv, k1 + 2)
                        for x in range(GT):
                            nc.tensor.matmul(P2[b][:, 300 + 8 * x:308 + 8 * x], oMT[:, 0, x, :], N8[:, b, x, :], start=True, stop=True)
                        for x in range(GT):
                            done = nc.tensor.matmul(P1[b][:, x * TN:(x + 1) * TN], oEA[:, 0, x, :], oM[:, 0, x, :], start=True, stop=True)
                        done.then_inc(so_pe, 1)
                        pe.wait_ge(so_dv, k1 + 3)
                        for x in range(GT):
                            nc.tensor.matmul(P0[b][0:TN, x * D:(x + 1) * D], oM[:, 0, x, :], oV[:, 0, x, 0:D], start=True, stop=True)
                            done = nc.tensor.matmul(P2[b][0:TN, 400 + 4 * x:404 + 4 * x], oM[:, 0, x, :], oEX[:, 0, x, :], start=True, stop=True)
                        done.then_inc(so_pe, 1)
                        pe.wait_ge(so_done, k)
                    for_sums.each(g, chunk)

                def x2_t(g, b, g0):
                    pe.wait_ge(s_x2, g + 1)
                    for x in range(GT):
                        done = nc.tensor.transpose(P1[b][:, x * TN:(x + 1) * TN], x2[:, b, x, :], idn[0:TN, 0:TN])
                    done.then_inc(s_x2p, 1)

                def h1(g, b, g0):
                    pe.wait_ge(s_xt, g + 1)
                    pe.wait_ge(s_ag, g + 1)
                    nc.tensor.matmul(P0[b][:, 0:GN], K["W1a"][:, :], XT[:, b, :], start=True, stop=False)
                    nc.tensor.matmul(P0[b][:, 0:GN], K["W1b"][:, :], AT[:, b, :], start=False, stop=True).then_inc(s_h1p, 1)

                def h2(g, b, g0):
                    pe.wait_ge(s_h1, g + 1)
                    nc.tensor.matmul(P1[b][:, 0:GN], K["W2"][:, :], H1[:, b, :], start=True, stop=True).then_inc(s_h2p, 1)

                def h3(g, b, g0):
                    pe.wait_ge(s_h2, g + 1)
                    for x in range(GT):
                        done = nc.tensor.matmul(P0[b][0:TN, x * D:(x + 1) * D], H2[:, b, x * TN:(x + 1) * TN], K["W3"][:, :], start=True, stop=True)
                    done.then_inc(s_h3p, 1)

                def x3_t(g, b, g0):
                    pe.wait_ge(s_x3, g + 1)
                    for x in range(GT):
                        done = nc.tensor.transpose(P1[b][:, x * TN:(x + 1) * TN], x2[:, b, x, :], idn[0:TN, 0:TN])
                    done.then_inc(s_x3p, 1)

                def r0_product(g, b, g0):
                    pe.wait_ge(s_x3t, g + 1)
                    for x in range(GT):
                        done = nc.tensor.matmul(P3[b][0:TN, x * D:(x + 1) * D], XT[:, b, x * TN:(x + 1) * TN], K["V0"][:, :], start=True, stop=True)
                    done.then_inc(s_r0p, 1)
                in_pairs(pe, [a_rows, edge_sums, max_columns, node_max, over_max, edge_values, sums, over_sums, x2_t, h1, h2,
                              h3, x3_t, r0_product])

            @block.scalar
            def _(act):
                for_max, for_sums = beyond(act)

                def indices(g, b, g0):
                    wait(act, s_num, g - 1)
                    nc.scalar.copy(cur[:, b, :, 0], K["idx_dst"][:, bass.ds(GT * g, GT)]).then_inc(s_cur, 1)

                def onehot_t(g, b, g0):
                    act.wait_ge(s_mtp, g + 1)
                    nc.scalar.copy(MT[:, b, :, :], P1[b][0:TN, :].rearrange("p (c e) -> p c e", c=GT)).then_inc(s_mt, 1)
                    act.wait_ge(s_agp, g + 1)
                    nc.scalar.copy(AT[:, b, :], P3[b][:, 0:GN]).then_inc(s_ag, 1)

                def exps(g, b, g0):
                    act.wait_ge(s_exs_in, g + 1)
                    nc.scalar.activation(EXS[:, b, :, :], EXS[:, b, :, :], ACT.Exp).then_inc(s_exs, 1)
                    act.wait_ge(s_exa, g + 1)
                    nc.scalar.activation(EX[:, b, :, :], EX[:, b, :, :], ACT.Exp).then_inc(s_ex, 1)

                def over_skip(g, b, g0):
                    for_max.each(g, lambda c, before, k: act.sem_inc(so_ex, 1))

                def over_exp(g, b, g0):
                    def chunk(c, before, k):
                        act.wait_ge(so_ch, OC * before + 7)
                        nc.scalar.activation(oEX[:, 0, :, :], oEX[:, 0, :, :], ACT.Exp).then_inc(so_ex, 1)
                    for_sums.each(g, chunk)

                def elu(g, b, g0):
                    act.wait_ge(s_mn, g + 1)
                    nc.scalar.activation(tmp[:, b, :, :], tmp[:, b, :, :], ACT.Exp).then_inc(s_elu, 1)

                def root(n):
                    def step(g, b, g0):
                        act.wait_ge(s_var, 3 * g0 + nth(g, b, g0, n))
                        nc.scalar.activation(mv[:, b, :, 1], mv[:, b, :, 1], ACT.Sqrt, bias=K["eps"][0:TN, 0:1]).then_inc(s_std, 1)
                    return step

                def x2_t(g, b, g0):
                    act.wait_ge(s_x2p, g + 1)
                    nc.scalar.copy(XT[:, b, :], P1[b][:, 0:GN]).then_inc(s_xt, 1)

                def h1(g, b, g0):
                    act.wait_ge(s_h1p, g + 1)
                    nc.scalar.activation(H1[:, b, :], P0[b][:, 0:GN], ACT.Relu, bias=K["b1c"][:, 0:1]).then_inc(s_h1, 1)

                def h2(g, b, g0):
                    act.wait_ge(s_h2p, g + 1)
                    nc.scalar.activation(H2[:, b, :], P1[b][:, 0:GN], ACT.Relu, bias=K["b2c"][:, 0:1]).then_inc(s_h2, 1)

                def x3_t(g, b, g0):
                    act.wait_ge(s_x3p, g + 1)
                    nc.scalar.copy(XT[:, b, :], P1[b][:, 0:GN]).then_inc(s_x3t, 1)
                in_pairs(act, [indices, onehot_t, over_skip, exps, over_exp, elu, root(0), x2_t, h1, h2, root(1), root(2), x3_t])

            @block.vector
            def _(dve):
                for_max, for_sums = beyond(dve)
                CH = 34
                n_ch = [0]

                def chain(g0):
                    def seq(ins):
                        n_ch[0] += 1
                        ins.then_inc(s_ch, 1)
                        dve.wait_ge(s_ch, CH * g0 + n_ch[0])
                    return seq

                def make_onehot(M_, rel):
                    return nc.vector.tensor_tensor(M_, K["iota"][:, 0:TN].unsqueeze(1).to_broadcast([P, GT, TN]),
                                                   rel.unsqueeze(2).to_broadcast([P, GT, TN]), ALU.is_equal)

                def a_columns(V_, A_, s, rel):
                    nc.vector.tensor_copy(A_[:, s, 0, :].rearrange("p (c h) -> p c h", c=GT), V_[:, s, :, D:D + HEADS])
                    return nc.vector.tensor_copy(A_[:, s, 1, :].rearrange("p (c h) -> p c h", c=GT),
                                                 rel.unsqueeze(2).to_broadcast([P, GT, HEADS]))

                def running_max(seq, bank, s, dT_, ne_, rB_, rm_):
                    seq(nc.vector.tensor_copy(dT_[:, s, :], bank[0:16, P:2 * P]))
                    seq(nc.vector.tensor_tensor(ne_[:, s, 1:P], dT_[:, s, 1:P], dT_[:, s, 0:P - 1], ALU.not_equal))
                    seq(nc.vector.tensor_scalar(rB_[:, s, :], ne_[:, s, 0:P], -BIG, None, ALU.mult))
                    seq(nc.vector.tensor_tensor_scan(rm_[:, s, :], rB_[:, s, :], bank[0:16, 0:P], -BIG, ALU.add, ALU.max))
                    return nc.vector.tensor_tensor(rm_[:, s, :], rm_[:, s, :], ne_[:, s, 1:P + 1], ALU.mult)

                def chunk_max(seq, psum, out, b):
                    seq(nc.vector.tensor_scalar(z4[:, b, :], psum[:, :, HEADS], 0.0, -BIG, ALU.is_equal, ALU.mult))
                    seq(nc.vector.tensor_tensor(out, psum[:, :, 0:HEADS], z4[:, b, :].unsqueeze(2).to_broadcast([TN, GT, HEADS]), ALU.add))

                def exponent(seq, V_, s, pn, EX_):
                    seq(nc.vector.tensor_tensor(EX_[:, s, :, :], pn[:, :, 0:HEADS], V_[:, s, :, D:D + HEADS], ALU.add))
                    seq(nc.vector.scalar_tensor_tensor(EX_[:, s, :, :], EX_[:, s, :, :], 0.2, EX_[:, s, :, :], ALU.mult, ALU.max))
                    seq(nc.vector.tensor_tensor(EX_[:, s, :, :], EX_[:, s, :, :], pn[:, :, HEADS:2 * HEADS], ALU.subtract))
                    return nc.vector.tensor_scalar(EX_[:, s, :, :], EX_[:, s, :, :], 0.0, None, ALU.min)

                nc.vector.memset(ne[:, :, :], 1.0)
                nc.vector.memset(one[:, :, :], 1.0)
                nc.vector.memset(RM[:, :, :, :], 1.0)
                nc.vector.memset(oRM[:, :, :, :], 1.0).then_inc(s_ch, 1)

                def first(g, b, g0):
                    if b == 0:
                        n_ch[0] = 1
                    if isinstance(g, int) and g == 0:
                        dve.wait_ge(s_ch, 1)
                    wait(dve, s_num, g - 1)
                    rel = K["rel_dst"][:, bass.ds(GT * g, GT)]
                    make_onehot(M[:, b, :, :], rel).then_inc(s_hot, 1)
                    dve.wait_ge(s_g[b], use(g, b, 64) + 64)
                    a_columns(V, A16, b, rel).then_inc(s_a16, 1)

                def run_max(g, b, g0):
                    dve.wait_ge(s_q, g + 1)
                    running_max(chain(g0), P0[b], b, dT, ne, rB, rm).then_inc(s_rm, 1)

                def max_columns(g, b, g0):
                    dve.wait_ge(s_q2, g + 1)
                    nc.vector.tensor_copy(RM[:, b, :, 0:HEADS], P2[b][:, 0:16].rearrange("p (c h) -> p c h", c=GT)).then_inc(s_rmc, 1)

                def node_max(g, b, g0):
                    seq = chain(g0)
                    dve.wait_ge(s_pg, g + 1)
                    dve.wait_ge(s_ld[b], use(g, b, 96) + 96)
                    chunk_max(seq, P2[b][0:TN, 64:64 + 20].rearrange("p (c h) -> p c h", c=GT), Gm[:, b, :, :], b)
                    seq(nc.vector.tensor_tensor(Gm[:, b, :, :], Gm[:, b, :, :], SELF[:, b, :, D:D + HEADS], ALU.max))

                def over_edges(g, before, k):
                    seq = over_seq(before, 0)
                    dve.wait_ge(so_e, k * 128)
                    nc.vector.tensor_scalar(oi[:, :, 0], oe[:, :, 0], N - 1, None, ALU.min)
                    seq(nc.vector.tensor_copy(of[:, :], oe[:, :, 1]))
                    seq(nc.vector.tensor_tensor(of[:, :], of[:, :], K["tbase"][:, bass.ds(GT * g, GT)], ALU.subtract))
                    make_onehot(oM[:, 0, :, :], of[:, :]).then_inc(so_hot, 1)
                    dve.wait_ge(so_hot, k)

                def over_seq(before, used):
                    n = [used]

                    def seq(ins):
                        n[0] += 1
                        ins.then_inc(so_ch, 1)
                        dve.wait_ge(so_ch, OC * before + n[0])
                    return seq

                def over_max(g, b, g0):
                    def chunk(c, before, k):
                        over_edges(g, before, k)
                        seq = over_seq(before, 2)
                        d = 3 * before
                        dve.wait_ge(so_g, k * 64)
                        a_columns(oV, oA16, 0, of[:, :]).then_inc(so_dv, 1)
                        dve.wait_ge(so_pe, d + 1)
                        running_max(seq, P0[b], 0, odT, one, orB, orm).then_inc(so_dv, 1)
                        dve.wait_ge(so_pe, d + 2)
                        nc.vector.tensor_copy(oRM[:, 0, :, 0:HEADS], P0[b][:, 256:272].rearrange("p (c h) -> p c h", c=GT)).then_inc(so_dv, 1)
                        dve.wait_ge(so_pe, d + 3)
                        chunk_max(seq, P0[b][0:TN, 320:340].rearrange("p (c h) -> p c h", c=GT), oG[:, :, :], b)
                        seq(nc.vector.tensor_tensor(Gm[:, b, :, :], Gm[:, b, :, :], oG[:, :, :], ALU.max))
                        dve.sem_inc(so_done, 1)
                        dve.wait_ge(so_done, k)
                    for_max.each(g, chunk)

                def node_values(g, b, g0):
                    seq = chain(g0)
                    adst = SELF[:, b, :, D + HEADS:TW]
                    nc.vector.tensor_copy(N8[:, b, :, 0:HEADS], adst)
                    nc.vector.tensor_tensor(EXS[:, b, :, :], SELF[:, b, :, D:D + HEADS], adst, ALU.add)
                    seq(nc.vector.tensor_tensor(Gm[:, b, :, :], Gm[:, b, :, :], adst, ALU.add))
                    nc.vector.scalar_tensor_tensor(N8[:, b, :, HEADS:2 * HEADS], Gm[:, b, :, :], 0.2, Gm[:, b, :, :], ALU.mult, ALU.max).then_inc(s_n8, 1)
                    seq(nc.vector.scalar_tensor_tensor(EXS[:, b, :, :], EXS[:, b, :, :], 0.2, EXS[:, b, :, :], ALU.mult, ALU.max))
                    nc.vector.tensor_tensor(EXS[:, b, :, :], EXS[:, b, :, :], N8[:, b, :, HEADS:2 * HEADS], ALU.subtract).then_inc(s_exs_in, 1)

                def edge_exponent(g, b, g0):
                    dve.wait_ge(s_pn, g + 1)
                    exponent(chain(g0), V, b, P2[b][:, 128:160].rearrange("p (c v) -> p c v", c=GT), EX).then_inc(s_exa, 1)

                def messages(g, b, g0):
                    dve.wait_ge(s_ex, g + 1)
                    nc.vector.tensor_tensor(heads(VX[:, b, :, :]), heads(V[:, b, :, 0:D]),
                                            EX[:, b, :, :].unsqueeze(3).to_broadcast([P, GT, HEADS, HD]), ALU.mult).then_inc(s_vx, 1)
                    dve.wait_ge(s_exs, g + 1)
                    chain(g0)(nc.vector.tensor_tensor(heads(NUM[:, b, :, :]), heads(SELF[:, b, :, 0:D]),
                                                      EXS[:, b, :, :].unsqueeze(3).to_broadcast([TN, GT, HEADS, HD]), ALU.mult))

                def totals(g, b, g0):
                    seq = chain(g0)
                    dve.wait_ge(s_num, g + 1)
                    nc.vector.tensor_tensor(NUM[:, b, :, :], P0[b][0:TN, :].rearrange("p (c d) -> p c d", c=GT), NUM[:, b, :, :], ALU.add)
                    seq(nc.vector.tensor_tensor(DEN[:, b, :, :], P2[b][0:TN, 256:272].rearrange("p (c h) -> p c h", c=GT), EXS[:, b, :, :], ALU.add))

                def over_sums(g, b, g0):
                    def chunk(c, before, k):
                        over_edges(g, before, k)
                        seq = over_seq(before, 2)
                        d = 3 * before
                        dve.wait_ge(s_ag, g + 1)
                        dve.wait_ge(so_g, k * 64)
                        dve.sem_inc(so_dv, 1)
                        dve.wait_ge(so_pe, d + 1)
                        nc.vector.tensor_copy(oMT[:, 0, :, :], P1[b][0:TN, :].rearrange("p (c e) -> p c e", c=GT)).then_inc(so_dv, 1)
                        dve.wait_ge(so_pe, d + 2)
                        seq(nc.vector.tensor_tensor(AT[:, b, :], AT[:, b, :], P1[b][:, 0:GN], ALU.add))
                        seq(exponent(seq, oV, 0, P2[b][:, 300:332].rearrange("p (c v) -> p c v", c=GT), oEX))
                        dve.wait_ge(so_ex, k)
                        nc.vector.tensor_tensor(heads(oV[:, 0, :, 0:D]), heads(oV[:, 0, :, 0:D]),
                                                oEX[:, 0, :, :].unsqueeze(3).to_broadcast([P, GT, HEADS, HD]), ALU.mult).then_inc(so_dv, 1)
                        dve.wait_ge(so_pe, d + 3)
                        nc.vector.tensor_tensor(NUM[:, b, :, :], P0[b][0:TN, :].rearrange("p (c d) -> p c d", c=GT), NUM[:, b, :, :], ALU.add)
                        seq(nc.vector.tensor_tensor(DEN[:, b, :, :], P2[b][0:TN, 400:416].rearrange("p (c h) -> p c h", c=GT), DEN[:, b, :, :], ALU.add))
                        seq(nc.vector.memset(of[:, 0:1], 0.0))
                        dve.sem_inc(so_done, 1)
                        dve.wait_ge(so_done, k)
                    for_sums.each(g, chunk)

                def attention(g, b, g0):
                    seq = chain(g0)
                    seq(nc.vector.tensor_scalar(DEN[:, b, :, :], DEN[:, b, :, :], 1e-16, None, ALU.add))
                    seq(nc.vector.reciprocal(DEN[:, b, :, :], DEN[:, b, :, :]))
                    seq(nc.vector.tensor_tensor(heads(NUM[:, b, :, :]), heads(NUM[:, b, :, :]),
                                                DEN[:, b, :, :].unsqueeze(3).to_broadcast([TN, GT, HEADS, HD]), ALU.mult))
                    seq(nc.vector.tensor_tensor(NUM[:, b, :, :], NUM[:, b, :, :], K["batt"][0:TN, :].unsqueeze(1).to_broadcast([TN, GT, D]), ALU.add))
                    nc.vector.tensor_scalar(tmp[:, b, :, :], NUM[:, b, :, :], 0.0, None, ALU.min).then_inc(s_mn, 1)

                def norm(seq, x, out, g, b, g0, n):
                    return layer_norm(nc, dve, seq, x, stats[:, b, :, :], mv[:, b, :, :], out, s_var, s_std, 3 * g0 + nth(g, b, g0, n), passed)

                def norm_x2(g, b, g0):
                    seq = chain(g0)
                    dve.wait_ge(s_elu, g + 1)
                    seq(nc.vector.scalar_tensor_tensor(NUM[:, b, :, :], NUM[:, b, :, :], 0.0, tmp[:, b, :, :], ALU.max, ALU.add))
                    seq(nc.vector.scalar_tensor_tensor(NUM[:, b, :, :], NUM[:, b, :, :], -1.0, X[:, b, :, :], ALU.add, ALU.add))
                    norm(seq, NUM[:, b, :, :], x2[:, b, :, :], g, b, g0, 0).then_inc(s_x2, 1)

                def norm_mlp(g, b, g0):
                    seq = chain(g0)

                    def row(name):
                        return K[name][0:TN, :].unsqueeze(1).to_broadcast([TN, GT, D])
                    dve.wait_ge(s_h3p, g + 1)
                    seq(nc.vector.tensor_tensor(tmp[:, b, :, :], P0[b][0:TN, :].rearrange("p (c d) -> p c d", c=GT), row("b3"), ALU.add))
                    seq(norm(seq, tmp[:, b, :, :], NUM[:, b, :, :], g, b, g0, 1))
                    seq(nc.vector.tensor_tensor(NUM[:, b, :, :], NUM[:, b, :, :], row("gamma"), ALU.mult))
                    seq(nc.vector.tensor_tensor(NUM[:, b, :, :], NUM[:, b, :, :], row("beta"), ALU.add))
                    seq(nc.vector.scalar_tensor_tensor(tmp[:, b, :, :], x2[:, b, :, :], 2.0, NUM[:, b, :, :], ALU.mult, ALU.add))

                def norm_x3(g, b, g0):
                    seq = chain(g0)
                    norm(seq, tmp[:, b, :, :], x2[:, b, :, :], g, b, g0, 2).then_inc(s_x3, 1)
                    dve.wait_ge(s_x3, g + 1)
                    wait(dve, s_st[b], use(g, b, 32))
                    nc.vector.tensor_tensor(y0[:, b, :, :], x2[:, b, :, :],
                                            K["isq"][:, bass.ds(GT * g, GT)].unsqueeze(2).to_broadcast([TN, GT, D]), ALU.mult)

                def finish(g, b, g0):
                    dve.wait_ge(s_r0p, g + 1)
                    nc.vector.tensor_tensor(r0[:, b, :, :], P3[b][0:TN, :].rearrange("p (c d) -> p c d", c=GT), x2[:, b, :, :], ALU.add).then_inc(s_fin, 1)
                in_pairs(dve, [first, run_max, max_columns, node_max, over_max, node_values, edge_exponent, messages, totals,
                               over_sums, attention, norm_x2, norm_mlp, norm_x3, finish])
                assert n_ch[0] == CH + 1


def build(nc, t, stop=99):
    ctx = ExitStack()
    with ctx:
        def sb(name, shape, dt=FP32):
            return ctx.enter_context(nc.sbuf_tensor(name, shape, dt))

        K = {
            "ident": sb("ident", [P, P]), "ltri": sb("ltri", [P, P]), "ones": sb("ones", [P, P]),
            "ones_bf": sb("ones_bf", [P, P], BF16), "zeros_bf": sb("zeros_bf", [P, P], BF16),
            "ltri_bf": sb("ltri_bf", [P, P], BF16), "iota": sb("iota", [P, GN]), "tbase": sb("tbase", [P, T]),
            "eps": sb("eps", [P, 1]), "deg_src": sb("deg_src", [TN, T]), "deg_dst": sb("deg_dst", [TN, T]),
            "deg_rows": sb("deg_rows", [G, GN]),
        }
        constants_phase(nc, K)
        prep_phase(nc, K, t["edges"], t["row_dram"], t["bin_dram"], t["by_src"])
        for name, width, dt in (("W01", D, FP32), ("W02", D, FP32), ("W1a", D, FP32), ("W1b", D, FP32), ("W2", D, FP32),
                                ("W3", D, FP32), ("Watt", TW, FP32), ("V0", D, FP32), ("V1", D, FP32), ("V2", D, FP32),
                                ("V3", D, FP32), ("b01", D, FP32), ("b02", D, FP32), ("batt", D, FP32), ("b3", D, FP32),
                                ("gamma", D, FP32), ("beta", D, FP32), ("b1c", 1, FP32), ("b2c", 1, FP32),
                                ("idx_dst", T + AHEAD, I32), ("rel_dst", T + AHEAD, FP32), ("idx_src", G + 3, I32), ("rel_src", G + 3, FP32)):
            K[name] = sb(name, [P, width], dt)
        for name, width in (("inv_dst", T), ("isq", T), ("inv_src", T)):
            K[name] = sb(name, [TN, width])
        for name, width in (("starts", T), ("bstarts", G), ("more_dst", G), ("more_src", G),
                            ("next_dst", G + 1), ("next_src", G + 1)):
            K[name] = sb(name, [1, width], I32)
        weights_phase(nc, K, t)
        index_phase(nc, K, t)
        if stop < 1:
            return
        sums_pass(nc, K, t, "hyper1", HG, t["x"], K["W01"], t["m1"], scale=K["inv_dst"])
        if stop < 2:
            return
        node_pass(nc, K, t, "node1", t["m1"], K["b01"], t["h1"])
        sums_pass(nc, K, t, "hyper2", HG, t["h1"], K["W02"], t["m2"], scale=K["inv_dst"])
        if stop < 3:
            return
        node_pass(nc, K, t, "node2", t["m2"], K["b02"], t["x1"], x_in=t["x"], att_out=t["att"])
        if stop < 4:
            return
        attention_pass(nc, K, t)
        if stop < 5:
            return
        sums_pass(nc, K, t, "cheb1", G, t["y0"], K["V1"], t["y1"], read_r=t["r0"], write_r=t["r1"])
        sums_pass(nc, K, t, "cheb2", G, t["y1"], K["V2"], t["y2"], read_r=t["r1"], write_r=t["r2"], minus=t["y0"], twice=2.0)
        sums_pass(nc, K, t, "cheb3", G, t["y2"], K["V3"], t["out"], read_r=t["r2"], norm=True)


_WEIGHTS = ["L0_gnn_W1", "L0_gnn_b1", "L0_gnn_W2", "L0_gnn_b2", "L1_gnn_W", "L1_gnn_att_src", "L1_gnn_att_dst",
            "L1_gnn_bias", "L2_gnn_W1", "L2_gnn_b1", "L2_gnn_W2", "L2_gnn_b2", "L2_gnn_W3", "L2_gnn_b3",
            "L2_gnn_gamma", "L2_gnn_beta", "L3_gnn_weights"]
_SCRATCH = {"row_dram": ((2, T), I32), "bin_dram": ((2, G), I32), "by_src": ((EP, 2), I32), "m1": ((HE, D), FP32),
            "m2": ((HE, D), FP32), "h1": ((N, D), FP32), "x1": ((N, D), FP32), "att": ((N, TW), FP32),
            "y0": ((N, D), FP32), "y1": ((N, D), FP32), "y2": ((N, D), FP32), "r0": ((N, D), FP32),
            "r1": ((N, D), FP32), "r2": ((N, D), FP32)}


def kernel(**inputs):
    import concourse.bacc as _bacc
    from concourse.bass_utils import run_bass_kernel_spmd as _run

    nc = _bacc.Bacc("TRN2", target_bir_lowering=False, num_devices=1)
    edges = np.full((EP, 2), PAD, np.int32)
    edges[:E, 0] = inputs["src"]
    edges[:E, 1] = inputs["dst"]
    features = np.zeros((E + P, D), np.float32)
    features[:E] = inputs["edge_attr_128"]
    arrays = {"x": np.ascontiguousarray(inputs["x"]), "edges": edges, "edge_attr": features}
    for name in _WEIGHTS:
        arrays[name] = np.ascontiguousarray(inputs[name])
    t = {name: nc.dram_tensor(name, a.shape, mybir.dt.from_np(a.dtype), kind="ExternalInput").ap()
         for name, a in arrays.items()}
    for name, (shape, dt) in _SCRATCH.items():
        t[name] = nc.dram_tensor(name, shape, dt, kind="Internal").ap()
    t["out"] = nc.dram_tensor("out", (N, D), FP32, kind="ExternalOutput").ap()
    build(nc, t)
    r = _run(nc, [arrays], core_ids=[0])
    return r.results[0]["out"]
```

```python
import numpy as np
import concourse.bass as bass
from concourse import mybir
from contextlib import ExitStack

FP32 = mybir.dt.float32
FP16 = mybir.dt.float16
BF16 = mybir.dt.bfloat16
I32 = mybir.dt.int32
ALU = mybir.AluOpType
ACT = mybir.ActivationFunctionType
AX = mybir.AxisListType

N = 50000
E = 50000
D = 128
P = 128
TN = 100
GT = 4
GN = TN * GT
T = N // TN
G = N // GN
HE = 10000
HG = HE // GN
NJ = 400
EP = P * NJ
JB = NJ // GT
PAD = 60000
MAGIC = 12582912.0
BIG = 1.0e30
HEADS, HD = 4, 32
TW = D + 2 * HEADS
EPS = 1e-5
AHEAD = 3 * GT


class Mem:

    def __init__(self, nc, ctx, phase):
        self.nc, self.ctx, self.phase, self.sems = nc, ctx, phase, []
        ctx.callback(self.clear)

    def sb(self, name, shape, dt=FP32):
        return self.ctx.enter_context(self.nc.sbuf_tensor(f"{self.phase}_{name}", shape, dt))

    def ps(self, name, shape, dt=FP32):
        return self.ctx.enter_context(self.nc.psum_tensor(f"{self.phase}_{name}", shape, dt))

    def sem(self, name):
        self.sems.append(self.nc.alloc_semaphore(f"{self.phase}_{name}"))
        return self.sems[-1]

    def clear(self):
        self.nc.clear_and_free_semaphores(self.sems)
        self.nc.all_engine_barrier()


def prep_phase(nc, K, edges, row_dram, bin_dram, by_src):
    with ExitStack() as ctx:
        m = Mem(nc, ctx, "prep")
        passed = m.sem("passed")
        pa = m.sb("pa", [P, NJ, 2], I32)
        pb = m.sb("pb", [JB, GT, P, 2], I32)
        srcf = m.sb("srcf", [P, NJ])
        dstf = m.sb("dstf", [P, NJ])
        grp = m.sb("grp", [P, NJ])
        rem = m.sb("rem", [P, NJ])
        io16 = m.sb("io16", [P, GN], FP16)
        dgrp = m.sb("dgrp", [P, NJ])
        drem = m.sb("drem", [P, NJ])
        ohk = m.sb("ohk", [P, NJ, G], BF16)
        og = m.sb("og", [P, 8, P], BF16)
        orr = m.sb("orr", [P, 8, GN], BF16)
        rs = m.sb("rs", [JB, GT, P])
        rd = m.sb("rd", [JB, GT, P])
        rk = m.sb("rk", [JB, GT, P])
        rl = m.sb("rl", [JB, GT, P])
        kcol = m.sb("kcol", [P, NJ])
        pay = m.sb("pay", [P, NJ, 2], I32)
        curp = m.sb("curp", [P, 4, 1], I32)
        curv = m.sb("curv", [P, 4, 2], I32)
        hist = m.sb("hist", [G, GT])
        hscan = m.sb("hscan", [G, GT])
        histn = m.sb("histn", [G, GN])
        cnt = m.sb("cnt", [G, NJ])
        scan = m.sb("scan", [G, NJ])
        binb = m.sb("binb", [G, 1])
        baset = m.sb("baset", [JB, GT, G])
        prod = m.sb("prod", [P, 4, G])
        pos = m.sb("pos", [P, NJ])
        posi = m.sb("posi", [P, NJ], I32)
        rowi = m.sb("rowi", [G, GT], I32)
        cnti = m.sb("cnti", [G, GT], I32)
        bini = m.sb("bini", [G, 2], I32)
        small = m.sb("small", [P, 4])
        nlow = m.sb("nlow", [1, 4])
        nlowi = m.sb("nlowi", [1, 1], I32)
        blank = m.sb("blank", [P, NJ, 2], I32)
        p_h = m.ps("p_h", [G, GN])
        p_d = m.ps("p_d", [G, GN])
        p_c = m.ps("p_c", [G, NJ])
        p_t = [m.ps(f"p_t{i}", [P, 512]) for i in range(2)]
        p_r = [m.ps(f"p_r{i}", [P, 512]) for i in range(2)]
        s_ld = m.sem("load")
        s_v = m.sem("dve")
        s_pe = m.sem("pe")
        s_og = m.sem("onehot_src")
        s_ogu = m.sem("onehot_src_used")
        s_io = m.sem("iota")
        s_rank = m.sem("rank")
        s_pos = m.sem("pos")
        s_scat = [m.sem(f"scatter{i}") for i in range(4)]
        s_cur = m.sem("scatter_operands")
        s_st = m.sem("store")
        s_bl = m.sem("blank_list")
        with nc.Block() as block:
            at = {}

            @block.sync
            def _(sp):
                sp.dma_start(pa[:, :, :], edges.rearrange("(p j) c -> p j c", p=P)).then_inc(s_ld, 16)
                sp.dma_start(pb[:, :, :, :], edges.rearrange("(b q p) c -> q b p c", b=GT, q=JB)).then_inc(s_ld, 16)
                sp.wait_ge(s_io, 3)
                sp.dma_start(by_src.rearrange("(p j) c -> p j c", p=P), blank[:, :, :]).then_inc(s_bl, 16)
                sp.wait_ge(s_bl, 16)
                sp.wait_ge(s_st, 1)
                sp.dma_start(row_dram[0, :].rearrange("(a b) -> a b", a=G), rowi[:, :]).then_inc(s_st, 16)
                sp.dma_start(row_dram[1, :].rearrange("(a b) -> a b", a=G), cnti[:, :]).then_inc(s_st, 16)
                sp.wait_ge(s_st, 34)
                sp.dma_start(bin_dram.rearrange("c g -> g c"), bini[:, :], allow_slow_non_contiguous=True).then_inc(s_st, 16)
                sp.wait_ge(s_st, 50)

            @block.gpsimd
            def _(pool):
                nc.gpsimd.iota(io16[:, :], [[1, GN]], 0, 0, allow_small_or_imprecise_dtypes=True).then_inc(s_io, 1)
                nc.gpsimd.memset(blank[:, :, 1:2], 0).then_inc(s_io, 1)
                nc.gpsimd.memset(blank[:, :, 0:1], PAD).then_inc(s_io, 1)
                pool.wait_ge(s_bl, 16)
                pool.wait_ge(s_pos, 1)
                quads = pool.value_load(nlowi[0:1, 0:1], min_val=1, max_val=JB)
                with pool.Fori(0, quads) as i:
                    alone(pool, s_cur, i + 1, passed)
                    for c in range(4):
                        pool.indirect_dma_start(by_src[:, :], bass.IndirectOffsetOnAxis(ap=curp[:, c, :], axis=0),
                                                curv[:, c, :], None, bounds_check=E - 1, oob_is_err=False)\
                            .then_inc(s_scat[c], 16)
                for c in range(4):
                    alone(pool, s_scat[c], 16 * quads, passed)

            @block.scalar
            def _(act):
                act.wait_ge(s_pos, 1)
                quads = act.value_load(nlowi[0:1, 0:1], min_val=1, max_val=JB)
                with act.Fori(0, 1) as _one:
                    nc.scalar.copy(curp[:, :, 0], posi[:, 0:4])
                    nc.scalar.copy(curv[:, :, :], pay[:, 0:4, :]).then_inc(s_cur, 1)
                with act.If(quads > 1):
                    with act.Fori(1, quads) as i:
                        for c in range(4):
                            act.wait_ge(s_scat[c], 16 * i)
                        nc.scalar.copy(curp[:, :, 0], posi[:, bass.ds(4 * i, 4)])
                        nc.scalar.copy(curv[:, :, :], pay[:, bass.ds(4 * i, 4), :]).then_inc(s_cur, 1)

            @block.vector
            def _(dve):
                n = [0]

                def seq(ins):
                    n[0] += 1
                    ins.then_inc(s_v, 1)
                    dve.wait_ge(s_v, n[0])

                def whole(out, x, a, b):
                    seq(nc.vector.tensor_scalar(out, x, a, b, ALU.mult, ALU.add))
                    seq(nc.vector.tensor_scalar(out, out, MAGIC, -MAGIC, ALU.add, ALU.add))

                def node_onehots(group, place, used):
                    def quad(i, h):
                        at = 8 * i + 4 * h
                        nc.vector.tensor_tensor(og[:, 4 * h:4 * h + 4, 0:G], io16[:, 0:G].unsqueeze(1).to_broadcast([P, 4, G]),
                                                group[:, bass.ds(at, 4)].unsqueeze(2).to_broadcast([P, 4, G]), ALU.is_equal)
                        for c in range(4):
                            nc.vector.tensor_scalar(orr[:, 4 * h + c, :], io16[:, :], place[:, bass.ds(at + c, 1)], None,
                                                    ALU.is_equal).then_inc(s_og, 1)
                    if used:
                        dve.wait_ge(s_ogu, used)
                    quad(0, 0)
                    quad(0, 1)
                    with dve.Fori(1, NJ // 8) as i:
                        for h in range(2):
                            dve.wait_ge(s_ogu, 8 * i + 4 * h - 3 + used)
                            quad(i, h)

                dve.wait_ge(s_ld, 32)
                dve.wait_ge(s_io, 1)
                seq(nc.vector.tensor_copy(srcf[:, :], pa[:, :, 0]))
                seq(nc.vector.tensor_copy(dstf[:, :], pa[:, :, 1]))
                whole(dgrp[:, :], dstf[:, :], 1.0 / GN, 0.5 / GN - 0.5)
                seq(nc.vector.scalar_tensor_tensor(drem[:, :], dgrp[:, :], -float(GN), dstf[:, :], ALU.mult, ALU.add))
                node_onehots(dgrp, drem, 0)
                whole(grp[:, :], srcf[:, :], 1.0 / GN, 0.5 / GN - 0.5)
                seq(nc.vector.scalar_tensor_tensor(rem[:, :], grp[:, :], -float(GN), srcf[:, :], ALU.mult, ALU.add))
                seq(nc.vector.tensor_copy(rs[:, :, :], pb[:, :, :, 0]))
                seq(nc.vector.tensor_copy(rd[:, :, :], pb[:, :, :, 1]))
                whole(rk[:, :, :], rs[:, :, :], 1.0 / GN, 0.5 / GN - 0.5)
                seq(nc.vector.tensor_scalar(rl[:, :, :], rd[:, :, :], float(HE - 1), 1000.0, ALU.is_ge, ALU.mult))
                seq(nc.vector.tensor_tensor(rk[:, :, :], rk[:, :, :], rl[:, :, :], ALU.add))
                at["rows"] = n[0]
                for x in range(3):
                    dve.wait_ge(s_pe, x + 2)
                    if x < 2:
                        seq(nc.vector.tensor_copy(pay[:, :, x], p_t[x % 2][:, 0:NJ]))
                    else:
                        seq(nc.vector.tensor_copy(kcol[:, :], p_t[x % 2][:, 0:NJ]))
                    at[f"evac{x}"] = n[0]
                seq(nc.vector.tensor_tensor(ohk[:, :, :], kcol[:, :].unsqueeze(2).to_broadcast([P, NJ, G]),
                                            io16[:, 0:G].unsqueeze(1).to_broadcast([P, NJ, G]), ALU.is_equal))
                at["key_onehots"] = n[0]
                dve.wait_ge(s_pe, 1)
                seq(nc.vector.tensor_copy(histn[:, :], p_h[:, :]))
                seq(nc.vector.tensor_reduce(hist[:, :], histn[:, :].rearrange("g (t n) -> g t n", t=GT), AX.X, ALU.add))
                seq(nc.vector.tensor_tensor_scan(hscan[:, :], hist[:, :], hist[:, :], 0.0, ALU.add, ALU.bypass))
                at["hist"] = n[0]
                dve.wait_ge(s_pe, 5)
                seq(nc.vector.tensor_copy(K["deg_dst"][:, :].rearrange("p (g t) -> p t g", t=GT),
                                          p_t[0][0:TN, 0:GT * G].rearrange("p (t g) -> p t g", t=GT)))
                at["deg_dst"] = n[0]
                seq(nc.vector.tensor_copy(small[0:G, 1:2], p_t[0][0:G, 501:502]))
                seq(nc.vector.tensor_scalar(hscan[:, :], hscan[:, :], small[0:G, 1:2], None, ALU.add))
                seq(nc.vector.tensor_tensor(hscan[:, :], hscan[:, :], hist[:, :], ALU.subtract))
                seq(nc.vector.tensor_copy(rowi[:, :], hscan[:, :]))
                whole(hist[:, :], hist[:, :], 1.0 / P, -1.0 / P + 0.5 / P - 0.5)
                seq(nc.vector.tensor_scalar(hist[:, :], hist[:, :], 0.0, None, ALU.max))
                seq(nc.vector.tensor_copy(cnti[:, :], hist[:, :]))
                nc.vector.memset(small[:, 3:4], 0.0).then_inc(s_st, 1)
                dve.wait_ge(s_pe, 6)
                seq(nc.vector.tensor_copy(cnt[:, :], p_c[:, :]))
                seq(nc.vector.tensor_tensor_scan(scan[:, :], cnt[:, :], cnt[:, :], 0.0, ALU.add, ALU.bypass))
                at["scan"] = n[0]
                dve.wait_ge(s_pe, 7)
                seq(nc.vector.tensor_copy(binb[:, :], p_t[1][0:G, 500:501]))
                seq(nc.vector.tensor_tensor(cnt[:, :], scan[:, :], cnt[:, :], ALU.subtract))
                seq(nc.vector.tensor_scalar(cnt[:, :], cnt[:, :], binb[:, 0:1], None, ALU.add))
                at["base"] = n[0]
                seq(nc.vector.tensor_copy(bini[:, 0:1], binb[:, :]))
                whole(binb[:, :], scan[:, NJ - 1:NJ], 1.0 / P, -1.0 / P + 0.5 / P - 0.5)
                seq(nc.vector.tensor_scalar(binb[:, :], binb[:, :], 0.0, None, ALU.max))
                seq(nc.vector.tensor_copy(bini[:, 1:2], binb[:, :]))
                nc.vector.memset(small[:, 2:3], 0.0).then_inc(s_st, 1)
                dve.wait_ge(s_pe, 8)
                seq(nc.vector.tensor_copy(baset[:, :, :], p_t[0][0:JB, 0:GT * G].rearrange("q (b g) -> q b g", b=GT)))
                at["baset"] = n[0]
                seq(nc.vector.tensor_scalar(rl[:, :, :], rd[:, :, :], float(HE - 1), None, ALU.is_lt))
                seq(nc.vector.tensor_reduce(small[0:JB, 0:1], rl[:, :, :].rearrange("q b p -> q (b p)"), AX.X, ALU.add))
                at["nlow"] = n[0]
                dve.wait_ge(s_pe, 9)
                seq(nc.vector.tensor_copy(nlow[:, 0:1], p_t[1][0:1, 501:502]))
                whole(nlow[:, 0:1], nlow[:, 0:1], 0.25 / P, 0.5 - 0.125 / P)
                seq(nc.vector.tensor_scalar(nlow[:, 0:1], nlow[:, 0:1], 1.0, None, ALU.max))
                seq(nc.vector.tensor_copy(nlowi[:, :], nlow[:, 0:1]))
                for i in range(JB):
                    dve.wait_ge(s_rank, i + 1)
                    seq(nc.vector.tensor_tensor(prod[:, :, :], ohk[:, 4 * i:4 * i + 4, :],
                                                p_r[i % 2][:, 0:4 * G].rearrange("p (c g) -> p c g", c=4), ALU.mult))
                    at[f"prod{i}"] = n[0]
                    seq(nc.vector.tensor_reduce(pos[:, 4 * i:4 * i + 4], prod[:, :, :], AX.X, ALU.add))
                seq(nc.vector.tensor_scalar(kcol[:, :], kcol[:, :], float(G), 1.0e6, ALU.is_ge, ALU.mult))
                seq(nc.vector.tensor_tensor(pos[:, :], pos[:, :], kcol[:, :], ALU.add))
                nc.vector.tensor_copy(posi[:, :], pos[:, :]).then_inc(s_pos, 1)
                node_onehots(grp, rem, NJ + 1)
                dve.wait_ge(s_pe, 10)
                seq(nc.vector.tensor_copy(K["deg_rows"][:, :], p_d[:, :]))
                at["histd"] = n[0]
                dve.wait_ge(s_pe, 11)
                nc.vector.tensor_copy(K["deg_src"][:, :].rearrange("p (g t) -> p t g", t=GT),
                                      p_t[0][0:TN, 0:GT * G].rearrange("p (t g) -> p t g", t=GT))

            @block.tensor
            def _(pe):
                idn, ones_bf, ltri_bf = K["ident"], K["ones_bf"], K["ltri_bf"]

                def count_nodes(pe, out, used):
                    nc.tensor.matmul(out[:, :], K["zeros_bf"][:, 0:G], K["zeros_bf"][:, 0:1].to_broadcast([P, GN]),
                                     start=True, stop=False).then_inc(s_ogu, 1)
                    seen = used - 1 if used else 0
                    with pe.Fori(0, NJ // 8) as i:
                        for c in range(8):
                            pe.wait_ge(s_og, 8 * i + c + 1 + seen)
                            nc.tensor.matmul(out[:, :], og[:, c, 0:G], orr[:, c, :], start=False, stop=False).then_inc(s_ogu, 1)
                    nc.tensor.matmul(out[:, :], K["zeros_bf"][:, 0:G], K["zeros_bf"][:, 0:1].to_broadcast([P, GN]),
                                     start=False, stop=True).then_inc(s_pe, 1)

                count_nodes(pe, p_h, 0)
                pe.wait_ge(s_v, at["rows"])
                for x, rows in enumerate((rs, rd, rk)):
                    if x == 2:
                        pe.wait_ge(s_v, at["evac0"])
                    for b in range(GT):
                        last = nc.tensor.transpose(p_t[x % 2][:, b * JB:(b + 1) * JB], rows[:, b, :], idn[0:JB, 0:JB])
                    last.then_inc(s_pe, 1)
                pe.wait_ge(s_v, at["hist"])
                for b in range(GT):
                    nc.tensor.transpose(p_t[0][0:TN, b * G:(b + 1) * G], histn[:, b * TN:(b + 1) * TN], idn[0:G, 0:G])
                nc.tensor.matmul(p_t[0][0:G, 501:502], K["ltri"][0:G, 0:G], hscan[:, GT - 1:GT], start=True, stop=True).then_inc(s_pe, 1)
                pe.wait_ge(s_v, at["key_onehots"])
                for j in range(NJ):
                    last = nc.tensor.matmul(p_c[:, j:j + 1], ohk[:, j, :], ones_bf[:, 0:1], start=True, stop=True)
                last.then_inc(s_pe, 1)
                pe.wait_ge(s_v, at["scan"])
                nc.tensor.matmul(p_t[1][0:G, 500:501], K["ltri"][0:G, 0:G], scan[:, NJ - 1:NJ], start=True, stop=True).then_inc(s_pe, 1)
                pe.wait_ge(s_v, at["base"])
                for b in range(GT):
                    last = nc.tensor.transpose(p_t[0][0:JB, b * G:(b + 1) * G], cnt[:, b * JB:(b + 1) * JB], idn[0:G, 0:G])
                last.then_inc(s_pe, 1)
                pe.wait_ge(s_v, at["nlow"])
                nc.tensor.matmul(p_t[1][0:1, 501:502], small[0:JB, 0:1], K["ones"][0:JB, 0:1], start=True, stop=True).then_inc(s_pe, 1)
                for i in range(JB):
                    if i >= 2:
                        pe.wait_ge(s_v, at[f"prod{i - 2}"])
                    nc.tensor.matmul(p_r[i % 2][:, 0:4 * G], ltri_bf[:, :],
                                     ohk[:, 4 * i:4 * i + 4, :].rearrange("p c g -> p (c g)"), start=True, stop=False)
                    for c in range(4):
                        b, q = divmod(4 * i + c, JB)
                        last = nc.tensor.matmul(p_r[i % 2][:, c * G:(c + 1) * G], idn[0:JB, q:q + 1].to_broadcast([JB, P]),
                                                baset[:, b, :], start=False, stop=c == 3)
                    last.then_inc(s_rank, 1)
                count_nodes(pe, p_d, NJ + 1)
                pe.wait_ge(s_v, at["histd"])
                for b in range(GT):
                    last = nc.tensor.transpose(p_t[0][0:TN, b * G:(b + 1) * G], K["deg_rows"][:, b * TN:(b + 1) * TN], idn[0:G, 0:G])
                last.then_inc(s_pe, 1)


def constants_phase(nc, K):
    with ExitStack() as ctx:
        m = Mem(nc, ctx, "const")
        passed = m.sem("passed")
        s_m = m.sem("memset")
        s_d = m.sem("done")
        with nc.Block() as block:
            @block.gpsimd
            def _(pool):
                nc.gpsimd.memset(K["ident"][:, :], 0.0).then_inc(s_m, 1)
                nc.gpsimd.memset(K["ltri"][:, :], 1.0).then_inc(s_m, 1)
                nc.gpsimd.memset(K["ones"][:, :], 1.0).then_inc(s_m, 1)
                nc.gpsimd.memset(K["eps"][:, :], EPS).then_inc(s_m, 1)
                nc.gpsimd.memset(K["ones_bf"][:, :], 1.0).then_inc(s_m, 1)
                nc.gpsimd.memset(K["zeros_bf"][:, :], 0.0).then_inc(s_m, 1)
                nc.gpsimd.iota(K["iota"][:, :], [[1, GN]], 0, 0, allow_small_or_imprecise_dtypes=True).then_inc(s_m, 1)
                nc.gpsimd.iota(K["tbase"][:, :], [[TN, T]], 0, 0, allow_small_or_imprecise_dtypes=True).then_inc(s_m, 1)
                pool.wait_ge(s_m, 8)
                nc.gpsimd.affine_select(out=K["ident"][:, :], in_=K["ident"][:, :], compare_op=ALU.not_equal, fill=1.0,
                                        base=0, pattern=[[-1, P]], channel_multiplier=1).then_inc(s_d, 1)
                nc.gpsimd.affine_select(out=K["ltri"][:, :], in_=K["ltri"][:, :], compare_op=ALU.is_gt, fill=0.0,
                                        base=0, pattern=[[1, P]], channel_multiplier=-1).then_inc(s_d, 1)

            @block.vector
            def _(dve):
                dve.wait_ge(s_d, 2)
                nc.vector.tensor_copy(K["ltri_bf"][:, :], K["ltri"][:, :]).then_inc(s_d, 1)
                dve.wait_ge(s_d, 3)



def index_phase(nc, K, t):
    with ExitStack() as ctx:
        m = Mem(nc, ctx, "index")
        passed = m.sem("passed")
        row = m.sb("row", [1, 2, T], I32)
        bins = m.sb("bins", [1, 2, G], I32)
        many = m.sb("many", [G, 2, T], I32)
        more = m.sb("more", [G, 2, G])
        left = m.sb("left", [G, G])
        after = m.sb("after", [G, 2])
        afteri = m.sb("afteri", [G, 4], I32)
        anyi = m.sb("anyi", [1, 2], I32)
        de = m.sb("de", [P, T, 2], I32)
        se = m.sb("se", [P, G, 2], I32)
        f = m.sb("f", [P, T])
        s_row = m.sem("rows")
        s_de = m.sem("dst_chunks")
        s_dp = m.sem("dst_chunks_of_pool")
        s_se = m.sem("src_chunks")
        s_v = m.sem("dve")
        s_deg = m.sem("degree")
        s_isq = m.sem("inverse_root")
        s_after = m.sem("after")
        s_list = m.sem("list")
        QUADS = T // GT
        SPQ, ACTQ = QUADS * 54 // 125, QUADS * 107 // 125
        with nc.Block() as block:
            def dst_chunks(eng, g, loaded):
                first = [eng.alloc_register(f"first{c}") for c in range(GT)]
                eng.load(first, row[0:1, 0, bass.ds(GT * g, GT)])
                for c in range(GT):
                    at = eng.snap(first[c], min_val=0, max_val=E)
                    eng.dma_start(de[:, bass.ds(GT * g + c, 1), :].rearrange("p o c -> p (o c)"),
                                  t["edges"][bass.ds(at, P), :]).then_inc(loaded, 16)

            @block.sync
            def _(sp):
                sp.dma_start(row[:, :, :], t["row_dram"].unsqueeze(0)).then_inc(s_row, 16)
                sp.dma_start(bins[:, :, :], t["bin_dram"].unsqueeze(0)).then_inc(s_row, 16)
                sp.dma_start(many[:, 0, :], t["row_dram"][1:2, :].to_broadcast([G, T])).then_inc(s_row, 16)
                sp.dma_start(many[:, 1, 0:G], t["bin_dram"][1:2, :].to_broadcast([G, G])).then_inc(s_row, 16)
                sp.wait_ge(s_row, 64)
                with sp.Fori(0, SPQ) as g:
                    dst_chunks(sp, g, s_de)
                sp.wait_ge(s_after, 1)
                for x, side in enumerate(("next_dst", "next_src")):
                    sp.dma_start(K[side][0:1, 1:G + 1], afteri[:, x:x + 1], allow_slow_non_contiguous=True).then_inc(s_list, 16)
                    sp.dma_start(K[side][0:1, 0:1], anyi[:, x:x + 1]).then_inc(s_list, 16)
                sp.wait_ge(s_list, 64)

            @block.gpsimd
            def _(pool):
                alone(pool, s_row, 64, passed)
                with pool.Fori(0, (G - 1) // GT) as i:
                    first = [pool.alloc_register(f"bin{c}") for c in range(GT)]
                    pool.load(first, bins[0:1, 0, bass.ds(GT * i, GT)])
                    for c in range(GT):
                        at = pool.snap(first[c], min_val=0, max_val=E)
                        pool.dma_start(se[:, bass.ds(GT * i + c, 1), :].rearrange("p o c -> p (o c)"),
                                      t["by_src"][bass.ds(at, P), :]).then_inc(s_se, 16)
                at = pool.value_load(bins[0:1, 0, G - 1:G], min_val=0, max_val=E)
                pool.dma_start(se[:, G - 1, :], t["by_src"][bass.ds(at, P), :]).then_inc(s_se, 16)
                with pool.Fori(ACTQ, QUADS) as g:
                    dst_chunks(pool, g, s_dp)

            @block.scalar
            def _(act):
                act.wait_ge(s_row, 64)
                act.sem_inc(passed, 1)
                with act.Fori(SPQ, ACTQ) as g:
                    dst_chunks(act, g, s_de)
                act.wait_ge(s_deg, 1)
                nc.scalar.activation(K["isq"][:, :], K["inv_dst"][:, :], ACT.Sqrt).then_inc(s_isq, 1)
                act.wait_ge(s_isq, 1)

            @block.vector
            def _(dve):
                n = [0]

                def seq(ins):
                    n[0] += 1
                    ins.then_inc(s_v, 1)
                    dve.wait_ge(s_v, n[0])

                dve.wait_ge(s_row, 64)
                seq(nc.vector.tensor_copy(K["starts"][:, :], row[:, 0, :]))
                seq(nc.vector.tensor_copy(K["bstarts"][:, :], bins[:, 0, :]))
                seq(nc.vector.tensor_reduce(K["more_dst"][:, :], row[:, 1, :].rearrange("o (g c) -> o g c", c=GT), AX.X, ALU.max))
                seq(nc.vector.tensor_copy(K["more_src"][:, :], bins[:, 1, :]))
                seq(nc.vector.tensor_reduce(more[:, 0, :], many[:, 0, :].rearrange("o (g c) -> o g c", c=GT), AX.X, ALU.max))
                seq(nc.vector.tensor_copy(more[:, 1, :], many[:, 1, 0:G]))
                seq(nc.vector.tensor_scalar(left[:, :], K["iota"][0:G, 0:G], -1.0, float(G), ALU.mult, ALU.add))
                for x in range(2):
                    seq(nc.vector.tensor_scalar(more[:, x, :], more[:, x, :], 0.0, None, ALU.is_gt))
                    seq(nc.vector.tensor_tensor(more[:, x, :], more[:, x, :], left[:, :], ALU.mult))
                    seq(nc.vector.tensor_reduce(after[0:1, x:x + 1], more[0:1, x, :], AX.X, ALU.max))
                    seq(nc.vector.tensor_scalar(anyi[:, x:x + 1], after[0:1, x:x + 1], -1.0, float(G), ALU.mult, ALU.add))
                    seq(nc.vector.tensor_tensor(more[:, x, :], more[:, x, :], K["ltri"][0:G, 0:G], ALU.mult))
                    seq(nc.vector.tensor_reduce(after[:, x:x + 1], more[:, x, :], AX.X, ALU.max))
                seq(nc.vector.tensor_scalar(afteri[:, 0:2], after[:, :], -1.0, float(G), ALU.mult, ALU.add))
                dve.sem_inc(s_after, 1)
                seq(nc.vector.tensor_scalar(f[0:TN, :], K["deg_dst"][:, :], 1.0, None, ALU.max))
                nc.vector.reciprocal(K["inv_dst"][:, :], f[0:TN, :]).then_inc(s_deg, 1)
                dve.wait_ge(s_isq, 1)
                seq(nc.vector.tensor_tensor(f[0:TN, :], f[0:TN, :], K["isq"][:, :], ALU.mult))
                seq(nc.vector.tensor_tensor(f[0:TN, :], f[0:TN, :], K["isq"][:, :], ALU.mult))
                seq(nc.vector.tensor_scalar(f[0:TN, :], f[0:TN, :], -0.5, 1.5, ALU.mult, ALU.add))
                seq(nc.vector.tensor_tensor(K["isq"][:, :], K["isq"][:, :], f[0:TN, :], ALU.mult))
                seq(nc.vector.tensor_scalar(f[0:TN, :], K["deg_src"][:, :], 1.0, None, ALU.max))
                seq(nc.vector.reciprocal(K["inv_src"][:, :], f[0:TN, :]))
                dve.wait_ge(s_se, 16 * G)
                seq(nc.vector.tensor_copy(f[:, 0:G], se[:, :, 0]))
                seq(nc.vector.tensor_tensor(K["rel_src"][:, 0:G], f[:, 0:G], K["tbase"][:, 0:T:GT], ALU.subtract))
                seq(nc.vector.tensor_copy(K["idx_src"][:, 0:G], se[:, :, 1]))
                dve.wait_ge(s_de, 16 * GT * ACTQ)
                dve.wait_ge(s_dp, 16 * GT * (QUADS - ACTQ))
                seq(nc.vector.tensor_copy(f[:, :], de[:, :, 1]))
                seq(nc.vector.tensor_tensor(K["rel_dst"][:, 0:T], f[:, :], K["tbase"][:, :], ALU.subtract))
                seq(nc.vector.tensor_scalar(K["idx_dst"][:, 0:T], de[:, :, 0], N - 1, None, ALU.min))
                seq(nc.vector.memset(K["rel_dst"][:, T:T + AHEAD], -1.0))
                seq(nc.vector.memset(K["idx_dst"][:, T:T + AHEAD], 0))
                seq(nc.vector.memset(K["rel_src"][:, G:G + 3], -1.0))
                seq(nc.vector.memset(K["idx_src"][:, G:G + 3], 0))


def groups(eng, n, body):
    for g in range(4):
        body(g, g, g == n - 1)
    with eng.Fori(1, (n - 1) // 4) as i:
        for q in range(4):
            body(4 * i + q, q, False)
    body(n - 1, 0, True)


def earlier(g, q, slots, n):
    return n * (g // slots) if isinstance(g, int) else (n // slots) * (g - q % slots)


def wait(eng, sem, value):
    if not isinstance(value, int) or value > 0:
        eng.wait_ge(sem, value)


def at_most(eng, value, top):
    return (value - (value - top) * (value > top)).with_bounds(min_val=0, max_val=top)


def alone(eng, sem, value, passed):
    if not isinstance(value, int) or value > 0:
        eng.wait_ge(sem, value)
        eng.sem_inc(passed, 1)


class Beyond:

    def __init__(self, eng, K, passed, side, counted=None):
        self.eng, self.passed = eng, passed
        self.more, self.after = K["more_" + side], K["next_" + side]
        self.group = eng.alloc_register()
        eng.load([self.group], self.after[0:1, 0:1])
        if counted:
            self.count = counted.count
        else:
            self.count = eng.alloc_register()
            eng.reg_mov(self.count, 0)

    def each(self, g, chunk):
        eng = self.eng
        eng.sem_inc(self.passed, 1)
        with eng.If(eng.snap(self.group, min_val=0, max_val=G) == g):
            more = eng.value_load(self.more[0:1, bass.ds(g, 1)], min_val=0, max_val=NJ)
            eng.load([self.group], self.after[0:1, bass.ds(g + 1, 1)])
            with eng.Fori(0, more) as c:
                before = eng.snap(self.count, min_val=0, max_val=1 << 20)
                eng.reg_add(self.count, self.count, 1)
                chunk(c, before, before + 1)


class Overflow:

    def __init__(self, m, width):
        self.e = m.sb("over_e", [P, GT, 2], I32)
        self.i = m.sb("over_i", [P, GT, 1], I32)
        self.f = m.sb("over_f", [P, GT])
        self.M = m.sb("over_M", [P, GT, TN])
        self.V = m.sb("over_V", [P, GT, width])
        self.s_e = m.sem("over_edges")
        self.s_f = m.sem("over_float")
        self.s_r = m.sem("over_rel")
        self.s_hot = m.sem("over_onehot")
        self.s_g = m.sem("over_gather")
        self.s_mm = m.sem("over_sum")
        self.s_done = m.sem("over_added")


def layer_norm(nc, dve, seq, x, stats, mv, out, s_var, s_std, n, passed):
    for c in range(GT):
        last = nc.vector.bn_stats(stats[:, c, :], x[:, c, :])
    seq(last)
    dve.sem_inc(passed, 1)
    for c in range(GT):
        last = nc.vector.bn_aggr(mv[:, c, :], stats[:, c, :])
    last.then_inc(s_var, 1)
    dve.wait_ge(s_std, n)
    seq(nc.vector.reciprocal(mv[:, :, 1], mv[:, :, 1]))
    seq(nc.vector.tensor_tensor(out, x, mv[:, :, 0:1].to_broadcast([TN, GT, D]), ALU.subtract))
    return nc.vector.tensor_tensor(out, out, mv[:, :, 1:2].to_broadcast([TN, GT, D]), ALU.mult)


def deviation(nc, act, K, mv, s_var, s_std, g):
    act.wait_ge(s_var, g + 1)
    nc.scalar.activation(mv[:, :, 1], mv[:, :, 1], ACT.Sqrt, bias=K["eps"][0:TN, 0:1]).then_inc(s_std, 1)


def sums_pass(nc, K, t, name, n, table, weight, out, scale=None, read_r=None, write_r=None,
              minus=None, twice=1.0, norm=False):
    cheb = read_r is not None
    with ExitStack() as ctx:
        m = Mem(nc, ctx, name)
        passed = m.sem("passed")
        V = m.sb("V", [P, 4, GT, D])
        M = m.sb("M", [P, 4, GT, TN])
        cur = m.sb("cur", [P, 4, GT, 1], I32)
        ST = m.sb("ST", [D, 2, GN])
        R = m.sb("R", [TN, 2, GT, D])
        Y = m.sb("Y", [TN, 2, GT, D])
        yo = m.sb("yo", [TN, 2, GT, D])
        tmp = m.sb("tmp", [TN, GT, D])
        stats = m.sb("stats", [TN, GT, 6])
        mv = m.sb("mv", [TN, GT, 2])
        o = Overflow(m, D)
        pst = [m.ps(f"pst{i}", [P, 512]) for i in range(2)]
        pout = [m.ps(f"pout{i}", [P, 512]) for i in range(2)]
        psn = [m.ps(f"psn{i}", [P, 512]) for i in range(2)]
        pov = m.ps("pov", [P, 512])
        s_cur = m.sem("indices")
        s_g = [m.sem(f"gathered{i}") for i in range(4)]
        s_hot = m.sem("onehot")
        s_sum = m.sem("summed")
        s_ev = m.sem("sum_in_sbuf")
        s_pr = m.sem("projected")
        s_ch = m.sem("dve_chain")
        s_fin = m.sem("finished")
        s_var = m.sem("variance")
        s_std = m.sem("deviation")
        s_ld = [m.sem(f"loaded{i}") for i in range(2)]
        s_st = [m.sem(f"stored{i}") for i in range(2)]
        loads = (1 if cheb else 0) + (1 if minus is not None else 0)
        stores = 1 + (1 if write_r is not None else 0)

        def rows(a, g):
            return a[bass.ds(g * GN, GN), :].rearrange("(c p) d -> p c d", p=TN)

        def scal(a, g):
            return a[:, bass.ds(GT * g, GT)].unsqueeze(2).to_broadcast([TN, GT, D])

        with nc.Block() as block:
            @block.gpsimd
            def _(pool):
                beyond = Beyond(pool, K, passed, "dst")

                def gather(g, q):
                    alone(pool, s_sum, g - 3, passed)
                    alone(pool, s_cur, g + 1, passed)
                    for x in range(GT):
                        pool.indirect_dma_start(V[:, q, x, :], None, table[:, :],
                                                bass.IndirectOffsetOnAxis(ap=cur[:, q, x, :], axis=0)).then_inc(s_g[q], 16)

                def overflow(g):
                    def chunk(c, before, k):
                        for x in range(GT):
                            first = pool.value_load(K["starts"][0:1, bass.ds(GT * g + x, 1)], min_val=0, max_val=E)
                            at = at_most(pool, first + (c + 1) * P, E)
                            pool.dma_start(o.e[:, x, :], t["edges"][bass.ds(at, P), :]).then_inc(o.s_e, 16)
                        alone(pool, o.s_hot, k, passed)
                        for x in range(GT):
                            pool.indirect_dma_start(o.V[:, x, :], None, table[:, :],
                                                    bass.IndirectOffsetOnAxis(ap=o.i[:, x, :], axis=0)).then_inc(o.s_g, 16)
                        alone(pool, o.s_done, k, passed)
                    beyond.each(g, chunk)

                def body(g, q, last):
                    if not last:
                        gather(g + 1, (q + 1) % 4)
                    overflow(g)
                gather(0, 0)
                groups(pool, n, body)

            @block.scalar
            def _(act):
                def indices(g, q):
                    wait(act, s_sum, g - 3)
                    nc.scalar.copy(cur[:, q, :, 0], K["idx_dst"][:, bass.ds(GT * g, GT)]).then_inc(s_cur, 1)

                def copy_sums(g, b):
                    act.wait_ge(s_sum, g + 1)
                    wait(act, s_pr, g - 1)
                    nc.scalar.copy(ST[:, b, :], pst[b][:, 0:GN]).then_inc(s_ev, 1)

                def body(g, q, last):
                    if not (isinstance(g, int) and g + 3 >= n):
                        indices(g + 3, (q + 3) % 4)
                    if not last:
                        copy_sums(g + 1, (q + 1) % 2)
                    if norm:
                        deviation(nc, act, K, mv, s_var, s_std, g)
                for g in range(3):
                    indices(g, g)
                copy_sums(0, 0)
                groups(act, n, body)

            @block.tensor
            def _(pe):
                beyond = Beyond(pe, K, passed, "dst")

                def sums(g, q):
                    b = q % 2
                    pe.wait_ge(s_g[q], earlier(g, q, 4, 64) + 64)
                    pe.wait_ge(s_hot, g + 1)
                    wait(pe, s_ev, g - 1)
                    for x in range(GT):
                        last = nc.tensor.matmul(pst[b][:, x * TN:(x + 1) * TN], V[:, q, x, :], M[:, q, x, :], start=True, stop=True)
                    last.then_inc(s_sum, 1)

                def overflow(g):
                    def chunk(c, before, k):
                        pe.wait_ge(o.s_g, k * 64)
                        for x in range(GT):
                            last = nc.tensor.matmul(pov[:, x * TN:(x + 1) * TN], o.V[:, x, :], o.M[:, x, :], start=True, stop=True)
                        last.then_inc(o.s_mm, 1)
                        pe.wait_ge(o.s_done, k)
                    beyond.each(g, chunk)

                def project(g, b):
                    pe.wait_ge(s_ev, g + 1)
                    wait(pe, s_fin, g - 1)
                    for x in range(GT):
                        last = nc.tensor.matmul(pout[b][0:TN, x * D:(x + 1) * D], ST[:, b, x * TN:(x + 1) * TN], weight[:, :], start=True, stop=True)
                    if cheb and not norm:
                        for x in range(GT):
                            last = nc.tensor.transpose(psn[b][0:TN, x * D:(x + 1) * D], ST[:, b, x * TN:(x + 1) * TN], K["ident"][:, :])
                    last.then_inc(s_pr, 1)

                def body(g, q, last):
                    if not last:
                        sums(g + 1, (q + 1) % 4)
                    overflow(g)
                    project(g, q % 2)
                sums(0, 0)
                groups(pe, n, body)

            @block.vector
            def _(dve):
                beyond = Beyond(dve, K, passed, "dst")
                CH = 5 if norm else 1 if minus is None else 2

                def onehot(g, q):
                    wait(dve, s_sum, g - 3)
                    nc.vector.tensor_tensor(M[:, q, :, :], K["iota"][:, 0:TN].unsqueeze(1).to_broadcast([P, GT, TN]),
                                            K["rel_dst"][:, bass.ds(GT * g, GT)].unsqueeze(2).to_broadcast([P, GT, TN]),
                                            ALU.is_equal).then_inc(s_hot, 1)

                def overflow(g, b):
                    def chunk(c, before, k):
                        dve.wait_ge(s_ev, g + 1)
                        dve.wait_ge(o.s_e, k * 64)
                        nc.vector.tensor_scalar(o.i[:, :, 0], o.e[:, :, 0], N - 1, None, ALU.min)
                        nc.vector.tensor_copy(o.f[:, :], o.e[:, :, 1]).then_inc(o.s_f, 1)
                        dve.wait_ge(o.s_f, k)
                        nc.vector.tensor_tensor(o.f[:, :], o.f[:, :], K["tbase"][:, bass.ds(GT * g, GT)], ALU.subtract).then_inc(o.s_r, 1)
                        dve.wait_ge(o.s_r, k)
                        nc.vector.tensor_tensor(o.M[:, :, :], K["iota"][:, 0:TN].unsqueeze(1).to_broadcast([P, GT, TN]),
                                                o.f[:, :].unsqueeze(2).to_broadcast([P, GT, TN]), ALU.is_equal).then_inc(o.s_hot, 1)
                        dve.wait_ge(o.s_mm, k)
                        nc.vector.tensor_tensor(ST[:, b, :], ST[:, b, :], pov[:, 0:GN], ALU.add).then_inc(o.s_done, 1)
                        dve.wait_ge(o.s_done, k)
                    beyond.each(g, chunk)

                def finish(g, b):
                    n_ch = [0]

                    def seq(ins):
                        n_ch[0] += 1
                        ins.then_inc(s_ch, 1)
                        dve.wait_ge(s_ch, CH * g + n_ch[0])
                    dve.wait_ge(s_pr, g + 1)
                    wait(dve, s_st[b], earlier(g, b, 2, 16 * stores))
                    v = pout[b][0:TN, :].rearrange("p (c d) -> p c d", c=GT)
                    if not cheb:
                        nc.vector.tensor_tensor(yo[:, b, :, :], v, scal(scale, g), ALU.mult).then_inc(s_fin, 1)
                        return
                    wait(dve, s_fin, g)
                    seq(nc.vector.tensor_tensor(tmp[:, :, :], v, scal(K["isq"], g), ALU.mult))
                    dve.wait_ge(s_ld[b], earlier(g, b, 2, 16 * loads) + 16 * loads)
                    if not norm:
                        nc.vector.tensor_tensor(R[:, b, :, :], R[:, b, :, :], tmp[:, :, :], ALU.add)
                        sn = psn[b][0:TN, :].rearrange("p (c d) -> p c d", c=GT)
                        scaled = nc.vector.tensor_tensor(yo[:, b, :, :], sn, scal(K["inv_dst"], g), ALU.mult)
                        if minus is None:
                            scaled.then_inc(s_fin, 1)
                        else:
                            seq(scaled)
                            nc.vector.scalar_tensor_tensor(yo[:, b, :, :], yo[:, b, :, :], twice, Y[:, b, :, :],
                                                           ALU.mult, ALU.subtract).then_inc(s_fin, 1)
                        return
                    seq(nc.vector.tensor_tensor(tmp[:, :, :], R[:, b, :, :], tmp[:, :, :], ALU.add))
                    layer_norm(nc, dve, seq, tmp[:, :, :], stats, mv, yo[:, b, :, :], s_var, s_std, g + 1, passed).then_inc(s_fin, 1)

                def body(g, q, last):
                    if not (isinstance(g, int) and g + 2 >= n):
                        onehot(g + 2, (q + 2) % 4)
                    overflow(g, q % 2)
                    finish(g, q % 2)
                onehot(0, 0)
                onehot(1, 1)
                groups(dve, n, body)

            @block.sync
            def _(sp):
                def load(g, b):
                    alone(sp, s_fin, g - 1, passed)
                    if write_r is not None:
                        alone(sp, s_st[b], earlier(g, b, 2, 16 * stores), passed)
                    if cheb:
                        sp.dma_start(R[:, b, :, :], rows(read_r, g)).then_inc(s_ld[b], 16)
                    if minus is not None:
                        sp.dma_start(Y[:, b, :, :], rows(minus, g)).then_inc(s_ld[b], 16)

                def body(g, q, last):
                    b = q % 2
                    if not last and loads:
                        load(g + 1, 1 - b)
                    alone(sp, s_fin, g + 1, passed)
                    sp.dma_start(rows(out, g), yo[:, b, :, :]).then_inc(s_st[b], 16)
                    if write_r is not None:
                        sp.dma_start(rows(write_r, g), R[:, b, :, :]).then_inc(s_st[b], 16)
                if loads:
                    load(0, 0)
                groups(sp, n, body)
                sp.wait_ge(s_st[0], 16 * stores * ((n + 1) // 2))
                sp.wait_ge(s_st[1], 16 * stores * ((n - 1) // 2))


def weights_phase(nc, K, t):
    with ExitStack() as ctx:
        m = Mem(nc, ctx, "weights")
        passed = m.sem("passed")
        att = m.sb("att", [P, 2, D])
        prod = m.sb("prod", [P, 2, D])
        w3 = m.sb("w3", [D, 4, D])
        s_ld = m.sem("loaded")
        s_v = m.sem("dve")
        with nc.Block() as block:
            @block.sync
            def _(sp):
                for dst, src in ((K["W01"], t["L0_gnn_W1"]), (K["W02"], t["L0_gnn_W2"]), (K["W1a"], t["L2_gnn_W1"][0:D, :]),
                                 (K["W1b"], t["L2_gnn_W1"][D:2 * D, :]), (K["W2"], t["L2_gnn_W2"]), (K["W3"], t["L2_gnn_W3"])):
                    sp.dma_start(dst[:, :], src).then_inc(s_ld, 16)
                sp.dma_start(K["Watt"][:, 0:D], t["L1_gnn_W"]).then_inc(s_ld, 16)
                sp.dma_start(w3[:, :, :], t["L3_gnn_weights"].rearrange("k f o -> f k o")).then_inc(s_ld, 16)
                for x, name in enumerate(("L1_gnn_att_src", "L1_gnn_att_dst")):
                    sp.dma_start(att[:, x, :], t[name].rearrange("h d -> (h d)").unsqueeze(0).to_broadcast([P, D])).then_inc(s_ld, 16)
                for key, name in (("b01", "L0_gnn_b1"), ("b02", "L0_gnn_b2"), ("batt", "L1_gnn_bias"), ("b3", "L2_gnn_b3"),
                                  ("gamma", "L2_gnn_gamma"), ("beta", "L2_gnn_beta")):
                    sp.dma_start(K[key][:, :], t[name].unsqueeze(0).to_broadcast([P, D])).then_inc(s_ld, 16)
                for key, name in (("b1c", "L2_gnn_b1"), ("b2c", "L2_gnn_b2")):
                    sp.dma_start(K[key][:, :], t[name].unsqueeze(1)).then_inc(s_ld, 16)
                sp.wait_ge(s_ld, 16 * 18)

            @block.vector
            def _(dve):
                dve.wait_ge(s_ld, 16 * 18)
                nc.vector.tensor_tensor(prod[:, :, :], K["Watt"][:, 0:D].unsqueeze(1).to_broadcast([P, 2, D]), att[:, :, :],
                                        ALU.mult).then_inc(s_v, 1)
                dve.wait_ge(s_v, 1)
                nc.vector.tensor_reduce(K["Watt"][:, D:TW], prod[:, :, :].rearrange("p x (h d) -> p (x h) d", d=HD), AX.X, ALU.add)
                nc.vector.tensor_scalar(K["batt_less_1"][:, :], K["batt"][:, :], -1.0, None, ALU.add)
                nc.vector.tensor_tensor(K["I_V0"][:, :], w3[:, 0, :], w3[:, 2, :], ALU.subtract).then_inc(s_v, 1)
                dve.wait_ge(s_v, 2)
                nc.vector.tensor_tensor(K["I_V0"][:, :], K["I_V0"][:, :], K["ident"][:, :], ALU.add)
                nc.vector.tensor_tensor(K["V1"][:, :], w3[:, 1, :], w3[:, 3, :], ALU.subtract)
                nc.vector.tensor_scalar(K["V2"][:, :], w3[:, 2, :], 2.0, None, ALU.mult)
                nc.vector.tensor_scalar(K["V3"][:, :], w3[:, 3, :], 2.0, None, ALU.mult).then_inc(s_v, 1)
                dve.wait_ge(s_v, 3)


def node_pass(nc, K, t, name, table, bias, out, x_in=None, att_out=None):
    second = x_in is not None
    with ExitStack() as ctx:
        m = Mem(nc, ctx, name)
        passed = m.sem("passed")
        V = m.sb("V", [P, 4, D])
        M = m.sb("M", [P, 4, GN])
        L = m.sb("L", [G, 4, D])
        cur = m.sb("cur", [P, 4, 1], I32)
        S = m.sb("S", [TN, 2, GT, D])
        lastrow = m.sb("lastrow", [P, D])
        X = m.sb("X", [TN, 2, GT, D])
        O = m.sb("O", [TN, 2, GT, D])
        XT = m.sb("XT", [D, 2, GN])
        A = m.sb("A", [TN, 2, GT, TW])
        stats = m.sb("stats", [TN, GT, 6])
        mv = m.sb("mv", [TN, GT, 2])
        oe = m.sb("over_e", [P, 2], I32)
        oi = m.sb("over_i", [P, 1], I32)
        of = m.sb("over_f", [P, 1])
        oM = m.sb("over_M", [P, GN])
        oV = m.sb("over_V", [P, D])
        oS = m.sb("over_S", [TN, GT, D])
        ps = [m.ps(f"ps{i}", [P, 512]) for i in range(2)]
        pt = m.ps("pt", [P, 512])
        pa = [m.ps(f"pa{i}", [P, 512]) for i in range(2)]
        pov = m.ps("pov", [P, 512])
        s_row = m.sem("last_row")
        s_cur = m.sem("indices")
        s_g = [m.sem(f"gathered{i}") for i in range(4)]
        s_hot = m.sem("operands")
        s_sum = m.sem("summed")
        s_ev = m.sem("sum_in_sbuf")
        s_bias = m.sem("bias_added")
        s_ch = m.sem("dve_chain")
        s_fin = m.sem("finished")
        s_var = m.sem("variance")
        s_std = m.sem("deviation")
        s_tr = m.sem("transposed")
        s_xt = m.sem("transpose_in_sbuf")
        s_at = m.sem("attention_rows")
        s_ac = m.sem("attention_in_sbuf")
        s_ld = [m.sem(f"loaded{i}") for i in range(2)]
        s_st = [m.sem(f"stored{i}") for i in range(2)]
        s_sa = [m.sem(f"stored_att{i}") for i in range(2)]
        so_e, so_f, so_rel, so_hot, so_g, so_mm, so_sc, so_done = [m.sem(f"over_{x}") for x in (
            "edges", "float", "rel", "onehot", "gather", "sum", "scaled", "added")]

        def rows(a, g):
            return a[bass.ds(g * GN, GN), :].rearrange("(c p) d -> p c d", p=TN)

        with nc.Block() as block:
            @block.gpsimd
            def _(pool):
                beyond = Beyond(pool, K, passed, "src")

                def gather(g, q):
                    alone(pool, s_sum, g - 3, passed)
                    alone(pool, s_cur, g + 1, passed)
                    pool.indirect_dma_start(V[:, q, :], None, table[:, :],
                                            bass.IndirectOffsetOnAxis(ap=cur[:, q, :], axis=0)).then_inc(s_g[q], 16)

                def add_bias(g, b):
                    if second:
                        pool.wait_ge(s_ld[b], earlier(g, b, 2, 16) + 16)
                    else:
                        pool.wait_ge(s_ev, g + 1)
                    a = X if second else S
                    nc.gpsimd.tensor_tensor(a[:, b, :, :], a[:, b, :, :], bias[0:TN, :].unsqueeze(1).to_broadcast([TN, GT, D]),
                                            ALU.add).then_inc(s_bias, 1)

                def overflow(g):
                    def chunk(c, before, k):
                        first = pool.value_load(K["bstarts"][0:1, bass.ds(g, 1)], min_val=0, max_val=E)
                        at = at_most(pool, first + (c + 1) * P, E)
                        pool.dma_start(oe[:, :], t["by_src"][bass.ds(at, P), :]).then_inc(so_e, 16)
                        alone(pool, so_rel, k, passed)
                        pool.indirect_dma_start(oV[:, :], None, table[:, :],
                                                bass.IndirectOffsetOnAxis(ap=oi[:, :], axis=0)).then_inc(so_g, 16)
                        alone(pool, so_done, k, passed)
                    beyond.each(g, chunk)

                def body(g, q, last):
                    if not (isinstance(g, int) and g + 2 >= G):
                        gather(g + 2, (q + 2) % 4)
                    add_bias(g, q % 2)
                    overflow(g)
                gather(0, 0)
                gather(1, 1)
                groups(pool, G, body)
                pool.wait_ge(s_g[1], 16 * ((G - 1) // 4 + 1))

            @block.scalar
            def _(act):
                def indices(g, q):
                    wait(act, s_sum, g - 3)
                    nc.scalar.copy(cur[:, q, :], K["idx_src"][:, bass.ds(g, 1)]).then_inc(s_cur, 1)

                def scaled_sums(g, b):
                    act.wait_ge(s_sum, g + 1)
                    wait(act, s_fin, g - 1)
                    for x in range(GT):
                        done = nc.scalar.activation(S[:, b, x, :], ps[b][0:TN, x * D:(x + 1) * D], ACT.Copy,
                                                    scale=K["inv_src"][:, bass.ds(GT * g + x, 1)])
                    done.then_inc(s_ev, 1)

                def attention_rows(g, b):
                    act.wait_ge(s_at, g + 1)
                    wait(act, s_sa[b], earlier(g, b, 2, 16))
                    for h in range(2):
                        done = nc.scalar.copy(A[:, b, 2 * h:2 * h + 2, :],
                                              pa[h][0:TN, 0:2 * TW].rearrange("p (c d) -> p c d", c=2))
                    done.then_inc(s_ac, 1)

                def body(g, q, last):
                    b = q % 2
                    if not (isinstance(g, int) and g + 3 >= G):
                        indices(g + 3, (q + 3) % 4)
                    if second:
                        deviation(nc, act, K, mv, s_var, s_std, g)
                    if not last:
                        scaled_sums(g + 1, 1 - b)
                    if second:
                        if not (isinstance(g, int) and g == 0):
                            attention_rows(g - 1, 1 - b)
                        act.wait_ge(s_tr, g + 1)
                        nc.scalar.copy(XT[:, b, :], pt[:, 0:GN]).then_inc(s_xt, 1)
                for g in range(3):
                    indices(g, g)
                scaled_sums(0, 0)
                groups(act, G, body)
                if second:
                    attention_rows(G - 1, 0)

            @block.tensor
            def _(pe):
                beyond = Beyond(pe, K, passed, "src")

                def sums(g, q):
                    b = q % 2
                    pe.wait_ge(s_hot, g + 1)
                    wait(pe, s_ev, g - 1)
                    for x in range(GT):
                        nc.tensor.matmul(ps[b][0:TN, x * D:(x + 1) * D], K["deg_rows"][:, x * TN:(x + 1) * TN], L[:, q, :], start=True, stop=False)
                        last = nc.tensor.matmul(ps[b][0:TN, x * D:(x + 1) * D], M[:, q, x * TN:(x + 1) * TN], V[:, q, :], start=False, stop=True)
                    last.then_inc(s_sum, 1)

                def overflow(g):
                    def chunk(c, before, k):
                        pe.wait_ge(so_hot, k)
                        for x in range(GT):
                            last = nc.tensor.matmul(pov[0:TN, x * D:(x + 1) * D], oM[:, x * TN:(x + 1) * TN], oV[:, :], start=True, stop=True)
                        last.then_inc(so_mm, 1)
                        pe.wait_ge(so_done, k)
                    beyond.each(g, chunk)

                def attention_rows(g, b):
                    pe.wait_ge(s_xt, g + 1)
                    wait(pe, s_ac, g)
                    for x in range(GT):
                        done = nc.tensor.matmul(pa[x // 2][0:TN, (x % 2) * TW:(x % 2 + 1) * TW],
                                                XT[:, b, x * TN:(x + 1) * TN], K["Watt"][:, :], start=True, stop=True)
                    done.then_inc(s_at, 1)

                def body(g, q, last):
                    b = q % 2
                    if not (isinstance(g, int) and g + 2 >= G):
                        sums(g + 2, (q + 2) % 4)
                    overflow(g)
                    if second:
                        if not (isinstance(g, int) and g == 0):
                            attention_rows(g - 1, 1 - b)
                        pe.wait_ge(s_fin, g + 1)
                        wait(pe, s_xt, g)
                        for x in range(GT):
                            done = nc.tensor.transpose(pt[:, x * TN:(x + 1) * TN], O[:, b, x, :], K["ident"][0:TN, 0:TN])
                        done.then_inc(s_tr, 1)
                sums(0, 0)
                sums(1, 1)
                groups(pe, G, body)
                if second:
                    attention_rows(G - 1, 0)

            @block.vector
            def _(dve):
                beyond = Beyond(dve, K, passed, "src")
                CH = 4 if second else 0

                def operands(g, q):
                    wait(dve, s_sum, g - 3)
                    nc.vector.tensor_scalar(M[:, q, :], K["iota"][:, :], K["rel_src"][:, bass.ds(g, 1)], None, ALU.is_equal)
                    nc.vector.tensor_scalar(L[:, q, :], lastrow[0:G, :], K["ident"][0:G, bass.ds(g, 1)], None, ALU.mult)
                    dve.wait_ge(s_g[q], earlier(g, q, 4, 16) + 16)
                    nc.vector.tensor_tensor(V[:, q, :], V[:, q, :], lastrow[:, :], ALU.subtract).then_inc(s_hot, 1)

                def overflow(g, b):
                    def chunk(c, before, k):
                        dve.wait_ge(so_e, k * 16)
                        nc.vector.tensor_copy(oi[:, :], oe[:, 1:2])
                        nc.vector.tensor_copy(of[:, :], oe[:, 0:1]).then_inc(so_f, 1)
                        dve.wait_ge(so_f, k)
                        nc.vector.tensor_tensor(of[:, :], of[:, :], K["tbase"][:, bass.ds(GT * g, 1)], ALU.subtract).then_inc(so_rel, 1)
                        dve.wait_ge(so_rel, k)
                        nc.vector.tensor_scalar(oM[:, :], K["iota"][:, :], of[:, 0:1], None, ALU.is_equal)
                        dve.wait_ge(so_g, k * 16)
                        nc.vector.tensor_tensor(oV[:, :], oV[:, :], lastrow[:, :], ALU.subtract).then_inc(so_hot, 1)
                        dve.wait_ge(so_mm, k)
                        nc.vector.tensor_tensor(oS[:, :, :], pov[0:TN, :].rearrange("p (c d) -> p c d", c=GT),
                                                K["inv_src"][:, bass.ds(GT * g, GT)].unsqueeze(2).to_broadcast([TN, GT, D]),
                                                ALU.mult).then_inc(so_sc, 1)
                        dve.wait_ge(so_sc, k)
                        nc.vector.tensor_tensor(S[:, b, :, :], S[:, b, :, :], oS[:, :, :], ALU.add).then_inc(so_done, 1)
                        dve.wait_ge(so_done, k)
                    beyond.each(g, chunk)

                def finish(g, b):
                    n_ch = [0]

                    def seq(ins):
                        n_ch[0] += 1
                        ins.then_inc(s_ch, 1)
                        dve.wait_ge(s_ch, CH * g + n_ch[0])
                    wait(dve, s_st[b], earlier(g, b, 2, 16))
                    if not second:
                        nc.vector.tensor_scalar(O[:, b, :, :], S[:, b, :, :], 0.0, None, ALU.max).then_inc(s_fin, 1)
                        return
                    wait(dve, s_tr, g - 1)
                    seq(nc.vector.tensor_tensor(S[:, b, :, :], S[:, b, :, :], X[:, b, :, :], ALU.add))
                    layer_norm(nc, dve, seq, S[:, b, :, :], stats, mv, O[:, b, :, :], s_var, s_std, g + 1, passed).then_inc(s_fin, 1)
                    assert n_ch[0] == CH, n_ch

                def body(g, q, last):
                    if not (isinstance(g, int) and g + 2 >= G):
                        operands(g + 2, (q + 2) % 4)
                    dve.wait_ge(s_ev, g + 1)
                    dve.wait_ge(s_bias, g + 1)
                    overflow(g, q % 2)
                    finish(g, q % 2)
                dve.wait_ge(s_row, 16)
                operands(0, 0)
                operands(1, 1)
                groups(dve, G, body)

            @block.sync
            def _(sp):
                sp.dma_start(lastrow[:, :], table[HE - 1:HE, :].to_broadcast([P, D])).then_inc(s_row, 16)

                def body(g, q, last):
                    b = q % 2
                    if not last and second:
                        alone(sp, s_fin, g, passed)
                        sp.dma_start(X[:, 1 - b, :, :], rows(x_in, g + 1)).then_inc(s_ld[1 - b], 16)
                    if second and not (isinstance(g, int) and g == 0):
                        alone(sp, s_ac, g, passed)
                        sp.dma_start(rows(att_out, g - 1), A[:, 1 - b, :, :]).then_inc(s_sa[1 - b], 16)
                    alone(sp, s_fin, g + 1, passed)
                    sp.dma_start(rows(out, g), O[:, b, :, :]).then_inc(s_st[b], 16)
                if second:
                    sp.dma_start(X[:, 0, :, :], rows(x_in, 0)).then_inc(s_ld[0], 16)
                groups(sp, G, body)
                if second:
                    sp.wait_ge(s_ac, G)
                    sp.dma_start(rows(att_out, G - 1), A[:, 0, :, :]).then_inc(s_sa[0], 16)
                for b in range(2):
                    sp.wait_ge(s_st[b], 16 * ((G + 1 - b) // 2))
                    if second:
                        sp.wait_ge(s_sa[b], 16 * ((G + 1 - b) // 2))


def in_turns(eng, steps):
    def run(**pairs):
        for stage, step in steps:
            pair = pairs.get(stage, [])
            for g, b in pair:
                step(g, b, pair[0][0])

    def pair(g):
        return [(g, 0), (g + 1, 1)]
    run(F=pair(0))
    run(F=pair(2), B=pair(0))
    run(F=pair(4), B=pair(2), C=pair(0))
    with eng.Fori(3, (G - 1) // 2) as i:
        run(F=pair(2 * i), B=pair(2 * i - 2), C=pair(2 * i - 4))
    run(F=[(G - 1, 0)], B=pair(G - 3), C=pair(G - 5))
    run(B=[(G - 1, 0)], C=pair(G - 3))
    run(C=[(G - 1, 0)])


def attention_pass(nc, K, t):
    with ExitStack() as ctx:
        m = Mem(nc, ctx, "att")
        passed = m.sem("passed")
        V = m.sb("V", [P, 2, GT, TW])
        VX = m.sb("VX", [P, 2, GT, D])
        M = m.sb("M", [P, 2, GT, TN])
        MT = m.sb("MT", [TN, 2, GT, P])
        cur = m.sb("cur", [P, 2, GT, 1], I32)
        EA = m.sb("EA", [P, 2, GT, D])
        SELF = m.sb("SELF", [TN, 2, GT, TW])
        X = m.sb("X", [TN, 2, GT, D])
        A16 = m.sb("A16", [P, 2, 2, GT * HEADS])
        dT = m.sb("dT", [GT * HEADS, 2, P])
        ne = m.sb("ne", [GT * HEADS, 2, P + 1])
        rB = m.sb("rB", [GT * HEADS, 2, P])
        rm = m.sb("rm", [GT * HEADS, 2, P])
        RM = m.sb("RM", [P, 2, GT, HEADS + 1])
        z4 = m.sb("z4", [TN, 2, GT])
        Gm = m.sb("Gm", [TN, 2, GT, HEADS])
        N8 = m.sb("N8", [TN, 2, GT, 2 * HEADS])
        EXS = m.sb("EXS", [TN, 2, GT, HEADS])
        EX = m.sb("EX", [P, 2, GT, HEADS])
        NUM = m.sb("NUM", [TN, 2, GT, D])
        DEN = m.sb("DEN", [TN, 2, GT, HEADS])
        Z = m.sb("Z", [TN, 2, GT, D])
        tmp = m.sb("tmp", [TN, 2, GT, D])
        XB = m.sb("XB", [TN, 2, GT, D])
        x2 = m.sb("x2", [TN, 2, GT, D])
        XT = m.sb("XT", [D, 2, GN])
        AT = m.sb("AT", [D, 2, GN])
        H1 = m.sb("H1", [D, 2, GN])
        H2 = m.sb("H2", [D, 2, GN])
        y0 = m.sb("y0", [TN, 2, GT, D])
        r0 = m.sb("r0", [TN, 2, GT, D])
        stats = m.sb("stats", [TN, 2, GT, 6])
        XT3 = m.sb("XT3", [D, 2, GN])
        mlp = m.sb("mlp", [TN, 2, GT, D])
        Z3 = m.sb("Z3", [TN, 2, GT, D])
        x3 = m.sb("x3", [TN, 2, GT, D])
        mv = [m.sb(f"mv{n}", [TN, 2, GT, 3]) for n in range(3)]
        oe = m.sb("oe", [P, GT, 2], I32)
        oi = m.sb("oi", [P, GT, 1], I32)
        of = m.sb("of", [P, GT])
        oM = m.sb("oM", [P, 1, GT, TN])
        oV = m.sb("oV", [P, 1, GT, TW])
        oMT = m.sb("oMT", [TN, 1, GT, P])
        oEA = m.sb("oEA", [P, 1, GT, D])
        oA16 = m.sb("oA16", [P, 1, 2, GT * HEADS])
        odT = m.sb("odT", [GT * HEADS, 1, P])
        one = m.sb("one", [GT * HEADS, 1, P + 1])
        orB = m.sb("orB", [GT * HEADS, 1, P])
        orm = m.sb("orm", [GT * HEADS, 1, P])
        oRM = m.sb("oRM", [P, 1, GT, HEADS + 1])
        oG = m.sb("oG", [TN, GT, HEADS])
        oEX = m.sb("oEX", [P, 1, GT, HEADS])
        FA, FB, BK, CK = [[m.ps(f"{x}{b}", [P, 512]) for b in range(2)] for x in ("front_a", "front_b", "back", "close")]
        QC, PG, PN = 0, 16, 36
        OPN, DN = 400, 432
        s_cur, s_hot, s_a16, s_q, s_rm, s_q2, s_rmc, s_pg, s_n8, s_mtp, s_mt, s_pn, s_exa, s_ex, s_vx, s_num, s_exs_in, \
            s_exs, s_self, s_tot, s_agp, s_ag, s_mn, s_elu, s_res, s_x2, s_xx, s_xb, s_x2p, s_xt, s_h1p, s_h1, s_h2p, s_h2, s_h3p, \
            s_mlp, s_x3, s_y0, s_x3p, s_x3t, s_r0p, s_fin, s_chf, s_chb, s_chc, s_set = [m.sem(x) for x in (
                "indices", "onehot", "a_columns", "a_rows_psum", "max_rows", "max_columns_psum", "max_columns", "node_max_psum",
                "node_values", "onehot_t_psum", "onehot_t", "edge_values_psum", "edge_exponent", "edge_exp", "messages",
                "sums_psum", "self_exponent", "self_exp", "self_message", "totals", "edge_sums_psum", "edge_sums",
                "elu_exponent", "elu_exp", "residual", "x2", "twice_x2", "twice_x2_beta", "x2_t_psum", "x2_t", "h1_psum", "h1", "h2_psum", "h2",
                "h3_psum", "mlp_norm", "x3", "y0", "x3_t_psum", "x3_t", "r0_psum", "finished", "front_chain", "back_chain",
                "close_chain", "ones_set")]
        s_var, s_std, s_nb = [[m.sem(f"{x}{n}") for n in range(3)] for x in ("variance", "deviation", "scale_and_shift")]
        s_g = [m.sem(f"gathered{i}") for i in range(2)]
        s_ld = [m.sem(f"loaded{i}") for i in range(2)]
        s_x = [m.sem(f"loaded_x{i}") for i in range(2)]
        s_st = [m.sem(f"stored{i}") for i in range(2)]
        so_e, so_hot, so_g, so_pe, so_dv, so_ex, so_done, so_ch = [m.sem(f"over_{x}") for x in (
            "edges", "onehot", "gather", "pe_step", "dve_step", "exp", "done", "chain")]

        def rows(a, g):
            return a[bass.ds(g * GN, GN), :].rearrange("(c p) d -> p c d", p=TN)

        def use(g, b, n):
            return n * (g // 2) if isinstance(g, int) else (n // 2) * (g - b)

        def heads(a):
            return a.rearrange("p c (h d) -> p c h d", h=HEADS)

        def beyond(eng):
            maxima = Beyond(eng, K, passed, "dst")
            return maxima, Beyond(eng, K, passed, "dst", maxima)

        OC = 9

        with nc.Block() as block:
            @block.gpsimd
            def _(pool):
                for_max, for_sums = beyond(pool)

                def gather(g, b, g0):
                    alone(pool, s_vx, g - 1, passed)
                    alone(pool, s_cur, g + 1, passed)
                    for x in range(GT):
                        pool.indirect_dma_start(V[:, b, x, :], None, t["att"][:, :],
                                                bass.IndirectOffsetOnAxis(ap=cur[:, b, x, :], axis=0)).then_inc(s_g[b], 16)

                def twice_x2(g, b, g0):
                    pool.wait_ge(s_x2, g + 1)
                    wait(pool, s_var[2], g - 1)
                    nc.gpsimd.tensor_tensor(XB[:, b, :, :], x2[:, b, :, :], x2[:, b, :, :], ALU.add).then_inc(s_xx, 1)
                    pool.wait_ge(s_xx, g + 1)
                    nc.gpsimd.tensor_tensor(XB[:, b, :, :], XB[:, b, :, :], K["beta"][0:TN, :].unsqueeze(1).to_broadcast([TN, GT, D]),
                                            ALU.add).then_inc(s_xb, 1)

                def self_message(g, b, g0):
                    pool.wait_ge(s_exs, g + 1)
                    wait(pool, s_mn, g - 1)
                    nc.gpsimd.tensor_tensor(heads(NUM[:, b, :, :]), heads(SELF[:, b, :, 0:D]),
                                            EXS[:, b, :, :].unsqueeze(3).to_broadcast([TN, GT, HEADS, HD]), ALU.mult).then_inc(s_self, 1)

                def scaled_x3(g, b, g0):
                    pool.wait_ge(s_x3, g + 1)
                    wait(pool, s_st[b], use(g, b, 32))
                    nc.gpsimd.tensor_tensor(y0[:, b, :, :], x3[:, b, :, :],
                                            K["isq"][:, bass.ds(GT * g, GT)].unsqueeze(2).to_broadcast([TN, GT, D]), ALU.mult).then_inc(s_y0, 1)

                def over_gather(chunks):
                    def step(g, b, g0):
                        def chunk(c, before, k):
                            for x in range(GT):
                                first = pool.value_load(K["starts"][0:1, bass.ds(GT * g + x, 1)], min_val=0, max_val=E)
                                at = at_most(pool, first + (c + 1) * P, E)
                                pool.dma_start(oe[:, x, :], t["edges"][bass.ds(at, P), :]).then_inc(so_e, 16)
                                pool.dma_start(oEA[:, 0, x, :], t["edge_attr"][bass.ds(at, P), :]).then_inc(so_e, 16)
                            alone(pool, so_hot, k, passed)
                            for x in range(GT):
                                pool.indirect_dma_start(oV[:, 0, x, :], None, t["att"][:, :],
                                                        bass.IndirectOffsetOnAxis(ap=oi[:, x, :], axis=0)).then_inc(so_g, 16)
                            alone(pool, so_done, k, passed)
                        chunks.each(g, chunk)
                    return step
                in_turns(pool, [("F", gather), ("F", over_gather(for_max)), ("B", twice_x2), ("F", self_message),
                                ("C", scaled_x3), ("F", over_gather(for_sums))])

            @block.sync
            def _(sp):
                def load(g, b, g0):
                    alone(sp, s_tot, g - 1, passed)
                    sp.dma_start(SELF[:, b, :, :], rows(t["att"], g)).then_inc(s_ld[b], 16)
                    for x in range(GT):
                        first = sp.value_load(K["starts"][0:1, bass.ds(GT * g + x, 1)], min_val=0, max_val=E)
                        sp.dma_start(EA[:, b, x, :], t["edge_attr"][bass.ds(first, P), :]).then_inc(s_ld[b], 16)

                def load_x(g, b, g0):
                    alone(sp, s_res, g - 1, passed)
                    sp.dma_start(X[:, b, :, :], rows(t["x1"], g)).then_inc(s_x[b], 16)

                def store(g, b, g0):
                    alone(sp, s_fin, g + 1, passed)
                    sp.dma_start(rows(t["y0"], g), y0[:, b, :, :]).then_inc(s_st[b], 16)
                    sp.dma_start(rows(t["r0"], g), r0[:, b, :, :]).then_inc(s_st[b], 16)

                def store_before(g, b, g0):
                    if not isinstance(g, int):
                        store(g - 2, b, g0)
                    elif g >= 2:
                        store(g - 2, b, g0)
                in_turns(sp, [("F", load), ("C", store_before), ("F", load_x)])
                store(G - 2, 1, 0)
                store(G - 1, 0, 0)
                sp.wait_ge(s_st[0], 32 * ((G + 1) // 2))
                sp.wait_ge(s_st[1], 32 * ((G - 1) // 2))

            @block.tensor
            def _(pe):
                for_max, for_sums = beyond(pe)
                idn = K["ident"]

                def a_rows(g, b, g0):
                    pe.wait_ge(s_a16, g + 1)
                    wait(pe, s_tot, g - 1)
                    for x in range(2):
                        done = nc.tensor.transpose(FA[b][0:16, x * P:(x + 1) * P], A16[:, b, x, :], idn[:, :])
                    done.then_inc(s_q, 1)
                    for x in range(GT):
                        done = nc.tensor.transpose(FB[b][0:TN, x * P:(x + 1) * P], M[:, b, x, :], idn[:, :])
                    done.then_inc(s_mtp, 1)

                def edge_sums(g, b, g0):
                    pe.wait_ge(s_ld[b], use(g, b, 80) + 80)
                    pe.wait_ge(s_mt, g + 1)
                    for x in range(GT):
                        done = nc.tensor.matmul(FB[b][:, x * TN:(x + 1) * TN], EA[:, b, x, :], M[:, b, x, :], start=True, stop=True)
                    done.then_inc(s_agp, 1)

                def max_columns(g, b, g0):
                    alone(pe, s_rm, g + 1, passed)
                    nc.tensor.transpose(FA[b][:, QC:QC + 16], rm[:, b, :], idn[0:16, 0:16]).then_inc(s_q2, 1)

                def node_max(g, b, g0):
                    pe.wait_ge(s_rmc, g + 1)
                    for x in range(GT):
                        at = PG + 5 * x
                        done = nc.tensor.matmul(FA[b][0:TN, at:at + 5], M[:, b, x, :], RM[:, b, x, :], start=True, stop=True)
                    done.then_inc(s_pg, 1)

                def over_max(g, b, g0):
                    def chunk(c, before, k):
                        k1 = 3 * before
                        pe.wait_ge(so_dv, k1 + 1)
                        for x in range(2):
                            done = nc.tensor.transpose(FA[b][0:16, x * P:(x + 1) * P], oA16[:, 0, x, :], idn[:, :])
                        done.then_inc(so_pe, 1)
                        alone(pe, so_dv, k1 + 2, passed)
                        nc.tensor.transpose(FA[b][:, 256:272], orm[:, 0, :], idn[0:16, 0:16]).then_inc(so_pe, 1)
                        pe.wait_ge(so_dv, k1 + 3)
                        for x in range(GT):
                            done = nc.tensor.matmul(FA[b][0:TN, 320 + 5 * x:325 + 5 * x], oM[:, 0, x, :], oRM[:, 0, x, :], start=True, stop=True)
                        done.then_inc(so_pe, 1)
                        pe.wait_ge(so_done, k)
                    for_max.each(g, chunk)

                def edge_values(g, b, g0):
                    pe.wait_ge(s_n8, g + 1)
                    for x in range(GT):
                        at = PN + 8 * x
                        done = nc.tensor.matmul(FA[b][:, at:at + 8], MT[:, b, x, :], N8[:, b, x, :], start=True, stop=True)
                    done.then_inc(s_pn, 1)

                def sums(g, b, g0):
                    pe.wait_ge(s_vx, g + 1)
                    pe.wait_ge(s_ag, g + 1)
                    for x in range(GT):
                        at = DN + 4 * x
                        nc.tensor.matmul(FA[b][0:TN, x * D:(x + 1) * D], M[:, b, x, :], VX[:, b, x, :], start=True, stop=True)
                        done = nc.tensor.matmul(FB[b][0:TN, at:at + 4], M[:, b, x, :], EX[:, b, x, :], start=True, stop=True)
                    done.then_inc(s_num, 1)

                def over_sums(g, b, g0):
                    def chunk(c, before, k):
                        k1 = 3 * before
                        pe.wait_ge(so_dv, k1 + 1)
                        for x in range(GT):
                            done = nc.tensor.transpose(FB[b][0:TN, x * P:(x + 1) * P], oM[:, 0, x, :], idn[:, :])
                        done.then_inc(so_pe, 1)
                        pe.wait_ge(so_dv, k1 + 2)
                        for x in range(GT):
                            nc.tensor.matmul(FB[b][:, OPN + 8 * x:OPN + 8 * x + 8], oMT[:, 0, x, :], N8[:, b, x, :], start=True, stop=True)
                        for x in range(GT):
                            done = nc.tensor.matmul(FB[b][:, x * TN:(x + 1) * TN], oEA[:, 0, x, :], oM[:, 0, x, :], start=True, stop=True)
                        done.then_inc(so_pe, 1)
                        pe.wait_ge(so_dv, k1 + 3)
                        for x in range(GT):
                            nc.tensor.matmul(FA[b][0:TN, x * D:(x + 1) * D], oM[:, 0, x, :], oV[:, 0, x, 0:D], start=True, stop=True)
                            done = nc.tensor.matmul(FB[b][0:TN, DN + 4 * x:DN + 4 * x + 4], oM[:, 0, x, :], oEX[:, 0, x, :], start=True, stop=True)
                        done.then_inc(so_pe, 1)
                        pe.wait_ge(so_done, k)
                    for_sums.each(g, chunk)

                def x2_t(g, b, g0):
                    pe.wait_ge(s_x2, g + 1)
                    for x in range(GT):
                        done = nc.tensor.transpose(BK[b][:, x * TN:(x + 1) * TN], x2[:, b, x, :], idn[0:TN, 0:TN])
                    done.then_inc(s_x2p, 1)

                def h1(g, b, g0):
                    pe.wait_ge(s_xt, g + 1)
                    pe.wait_ge(s_ag, g + 1)
                    nc.tensor.matmul(BK[b][:, 0:GN], K["W1a"][:, :], XT[:, b, :], start=True, stop=False)
                    nc.tensor.matmul(BK[b][:, 0:GN], K["W1b"][:, :], AT[:, b, :], start=False, stop=True).then_inc(s_h1p, 1)

                def h2(g, b, g0):
                    pe.wait_ge(s_h1, g + 1)
                    nc.tensor.matmul(BK[b][:, 0:GN], K["W2"][:, :], H1[:, b, :], start=True, stop=True).then_inc(s_h2p, 1)

                def h3(g, b, g0):
                    pe.wait_ge(s_h2, g + 1)
                    for x in range(GT):
                        done = nc.tensor.matmul(BK[b][0:TN, x * D:(x + 1) * D], H2[:, b, x * TN:(x + 1) * TN], K["W3"][:, :], start=True, stop=True)
                    done.then_inc(s_h3p, 1)

                def x3_t(g, b, g0):
                    pe.wait_ge(s_x3, g + 1)
                    for x in range(GT):
                        done = nc.tensor.transpose(CK[b][:, x * TN:(x + 1) * TN], x3[:, b, x, :], idn[0:TN, 0:TN])
                    done.then_inc(s_x3p, 1)

                def r0_product(g, b, g0):
                    pe.wait_ge(s_x3t, g + 1)
                    for x in range(GT):
                        done = nc.tensor.matmul(CK[b][0:TN, x * D:(x + 1) * D], XT3[:, b, x * TN:(x + 1) * TN], K["I_V0"][:, :], start=True, stop=True)
                    done.then_inc(s_r0p, 1)
                in_turns(pe, [("F", a_rows), ("F", edge_sums), ("F", max_columns), ("B", x2_t), ("F", node_max), ("F", over_max),
                              ("B", h1), ("F", edge_values), ("B", h2), ("B", h3), ("F", sums), ("F", over_sums), ("C", x3_t),
                              ("C", r0_product)])

            @block.scalar
            def _(act):
                for_max, for_sums = beyond(act)

                def indices(g, b):
                    if not isinstance(g, int) or g >= 2:
                        act.wait_ge(s_g[b], use(g, b, 64))
                    nc.scalar.copy(cur[:, b, :, 0], K["idx_dst"][:, bass.ds(GT * g, GT)]).then_inc(s_cur, 1)

                def next_indices(g, b, g0):
                    if not isinstance(g, int) or g < G - 1:
                        indices(g + 2, b)

                def onehot_t(g, b, g0):
                    act.wait_ge(s_mtp, g + 1)
                    nc.scalar.copy(MT[:, b, :, :], FB[b][0:TN, :].rearrange("p (c e) -> p c e", c=GT)).then_inc(s_mt, 1)

                def edge_sums(g, b, g0):
                    act.wait_ge(s_agp, g + 1)
                    wait(act, s_h1p, g - 1)
                    nc.scalar.copy(AT[:, b, :], FB[b][:, 0:GN]).then_inc(s_ag, 1)

                def exps(g, b, g0):
                    act.wait_ge(s_exs_in, g + 1)
                    nc.scalar.activation(EXS[:, b, :, :], EXS[:, b, :, :], ACT.Exp).then_inc(s_exs, 1)
                    act.wait_ge(s_exa, g + 1)
                    nc.scalar.activation(EX[:, b, :, :], EX[:, b, :, :], ACT.Exp).then_inc(s_ex, 1)

                def over_skip(g, b, g0):
                    for_max.each(g, lambda c, before, k: act.sem_inc(so_ex, 1))

                def over_exp(g, b, g0):
                    def chunk(c, before, k):
                        act.wait_ge(so_ch, OC * before + 7)
                        nc.scalar.activation(oEX[:, 0, :, :], oEX[:, 0, :, :], ACT.Exp).then_inc(so_ex, 1)
                    for_sums.each(g, chunk)

                def elu(g, b, g0):
                    act.wait_ge(s_mn, g + 1)
                    nc.scalar.activation(tmp[:, b, :, :], Z[:, b, :, :], ACT.Exp, bias=K["ones"][0:TN, 0:1]).then_inc(s_elu, 1)

                def root(n):
                    def step(g, b, g0):
                        act.wait_ge(s_var[n], g + 1)
                        nc.scalar.activation(mv[n][:, b, :, 1], mv[n][:, b, :, 1], ACT.Sqrt, bias=K["eps"][0:TN, 0:1]).then_inc(s_std[n], 1)
                    return step

                def normed(n, out, x, ready):
                    def step(g, b, g0):
                        act.wait_ge(s_nb[n], g + 1)
                        if n == 0:
                            wait(act, s_xx, g - 1)
                        if n == 2:
                            wait(act, s_fin, g - 1)
                        for c in range(GT):
                            done = nc.scalar.activation(out[:, b, c, :], x[:, b, c, :], ACT.Identity,
                                                        scale=mv[n][:, b, c, 1:2], bias=mv[n][:, b, c, 2:3])
                        done.then_inc(ready, 1)
                    return step

                def x2_t(g, b, g0):
                    act.wait_ge(s_x2p, g + 1)
                    nc.scalar.copy(XT[:, b, :], BK[b][:, 0:GN]).then_inc(s_xt, 1)

                def h1(g, b, g0):
                    act.wait_ge(s_h1p, g + 1)
                    nc.scalar.activation(H1[:, b, :], BK[b][:, 0:GN], ACT.Relu, bias=K["b1c"][:, 0:1]).then_inc(s_h1, 1)

                def h2(g, b, g0):
                    act.wait_ge(s_h2p, g + 1)
                    nc.scalar.activation(H2[:, b, :], BK[b][:, 0:GN], ACT.Relu, bias=K["b2c"][:, 0:1]).then_inc(s_h2, 1)

                def x3_t(g, b, g0):
                    act.wait_ge(s_x3p, g + 1)
                    nc.scalar.copy(XT3[:, b, :], CK[b][:, 0:GN]).then_inc(s_x3t, 1)

                def finish(g, b, g0):
                    act.wait_ge(s_r0p, g + 1)
                    act.wait_ge(s_y0, g + 1)
                    nc.scalar.copy(r0[:, b, :, :], CK[b][0:TN, :].rearrange("p (c d) -> p c d", c=GT)).then_inc(s_fin, 1)
                indices(0, 0)
                indices(1, 1)
                in_turns(act, [("B", elu), ("C", root(1)), ("F", onehot_t), ("C", normed(1, Z3, mlp, s_mlp)), ("B", root(0)),
                               ("F", next_indices), ("F", over_skip), ("B", normed(0, x2, Z, s_x2)), ("B", x2_t), ("C", root(2)),
                               ("B", h1), ("F", edge_sums), ("F", exps), ("B", h2), ("C", normed(2, x3, Z3, s_x3)),
                               ("F", over_exp), ("C", x3_t), ("C", finish)])

            @block.vector
            def _(dve):
                for_max, for_sums = beyond(dve)
                CF, CB, CC = 12, 8, 5
                nf, nb, nk = [0], [0], [0]

                def front_chain(g0):
                    def seq(ins):
                        nf[0] += 1
                        ins.then_inc(s_chf, 1)
                        dve.wait_ge(s_chf, CF * g0 + nf[0])
                    return seq

                def back_chain(g0):
                    def seq(ins):
                        nb[0] += 1
                        ins.then_inc(s_chb, 1)
                        dve.wait_ge(s_chb, CB * g0 + nb[0])
                    return seq

                def close_chain(g0):
                    def seq(ins):
                        nk[0] += 1
                        ins.then_inc(s_chc, 1)
                        dve.wait_ge(s_chc, CC * g0 + nk[0])
                    return seq

                def make_onehot(M_, rel):
                    return nc.vector.tensor_tensor(M_, K["iota"][:, 0:TN].unsqueeze(1).to_broadcast([P, GT, TN]),
                                                   rel.unsqueeze(2).to_broadcast([P, GT, TN]), ALU.is_equal)

                def a_columns(V_, A_, s, rel):
                    nc.vector.tensor_copy(A_[:, s, 0, :].rearrange("p (c h) -> p c h", c=GT), V_[:, s, :, D:D + HEADS])
                    return nc.vector.tensor_copy(A_[:, s, 1, :].rearrange("p (c h) -> p c h", c=GT),
                                                 rel.unsqueeze(2).to_broadcast([P, GT, HEADS]))

                def running_max(seq, bank, s, dT_, ne_, rB_, rm_):
                    seq(nc.vector.tensor_copy(dT_[:, s, :], bank[0:16, P:2 * P]))
                    seq(nc.vector.tensor_tensor(ne_[:, s, 1:P], dT_[:, s, 1:P], dT_[:, s, 0:P - 1], ALU.not_equal))
                    seq(nc.vector.tensor_scalar(rB_[:, s, :], ne_[:, s, 0:P], -BIG, None, ALU.mult))
                    seq(nc.vector.tensor_tensor_scan(rm_[:, s, :], rB_[:, s, :], bank[0:16, 0:P], -BIG, ALU.add, ALU.max))
                    return nc.vector.tensor_tensor(rm_[:, s, :], rm_[:, s, :], ne_[:, s, 1:P + 1], ALU.mult)

                def chunk_max(seq, psum, out, b):
                    seq(nc.vector.tensor_scalar(z4[:, b, :], psum[:, :, HEADS], 0.0, -BIG, ALU.is_equal, ALU.mult))
                    seq(nc.vector.tensor_tensor(out, psum[:, :, 0:HEADS], z4[:, b, :].unsqueeze(2).to_broadcast([TN, GT, HEADS]), ALU.add))

                def exponent(seq, V_, s, pn, EX_):
                    seq(nc.vector.tensor_tensor(EX_[:, s, :, :], pn[:, :, 0:HEADS], V_[:, s, :, D:D + HEADS], ALU.add))
                    seq(nc.vector.scalar_tensor_tensor(EX_[:, s, :, :], EX_[:, s, :, :], 0.2, EX_[:, s, :, :], ALU.mult, ALU.max))
                    seq(nc.vector.tensor_tensor(EX_[:, s, :, :], EX_[:, s, :, :], pn[:, :, HEADS:2 * HEADS], ALU.subtract))
                    return nc.vector.tensor_scalar(EX_[:, s, :, :], EX_[:, s, :, :], 0.0, None, ALU.min)

                nc.vector.memset(ne[:, :, :], 1.0)
                nc.vector.memset(one[:, :, :], 1.0)
                nc.vector.memset(RM[:, :, :, :], 1.0)
                nc.vector.memset(oRM[:, :, :, :], 1.0).then_inc(s_set, 1)
                dve.wait_ge(s_set, 1)

                def first(g, b, g0):
                    if b == 0:
                        nf[0] = 0
                    wait(dve, s_num, g - 1)
                    rel = K["rel_dst"][:, bass.ds(GT * g, GT)]
                    make_onehot(M[:, b, :, :], rel).then_inc(s_hot, 1)
                    dve.wait_ge(s_g[b], use(g, b, 64) + 64)
                    a_columns(V, A16, b, rel).then_inc(s_a16, 1)

                def run_max(g, b, g0):
                    dve.wait_ge(s_q, g + 1)
                    running_max(front_chain(g0), FA[b], b, dT, ne, rB, rm).then_inc(s_rm, 1)

                def max_columns(g, b, g0):
                    dve.wait_ge(s_q2, g + 1)
                    nc.vector.tensor_copy(RM[:, b, :, 0:HEADS], FA[b][:, QC:QC + 16].rearrange("p (c h) -> p c h", c=GT)).then_inc(s_rmc, 1)

                def node_max(g, b, g0):
                    seq = front_chain(g0)
                    dve.wait_ge(s_pg, g + 1)
                    dve.wait_ge(s_ld[b], use(g, b, 80) + 80)
                    at = PG
                    chunk_max(seq, FA[b][0:TN, at:at + 20].rearrange("p (c h) -> p c h", c=GT), Gm[:, b, :, :], b)
                    seq(nc.vector.tensor_tensor(Gm[:, b, :, :], Gm[:, b, :, :], SELF[:, b, :, D:D + HEADS], ALU.max))

                def over_edges(g, before, k):
                    seq = over_seq(before, 0)
                    dve.wait_ge(so_e, k * 128)
                    nc.vector.tensor_scalar(oi[:, :, 0], oe[:, :, 0], N - 1, None, ALU.min)
                    seq(nc.vector.tensor_copy(of[:, :], oe[:, :, 1]))
                    seq(nc.vector.tensor_tensor(of[:, :], of[:, :], K["tbase"][:, bass.ds(GT * g, GT)], ALU.subtract))
                    make_onehot(oM[:, 0, :, :], of[:, :]).then_inc(so_hot, 1)
                    dve.wait_ge(so_hot, k)

                def over_seq(before, used):
                    n = [used]

                    def seq(ins):
                        n[0] += 1
                        ins.then_inc(so_ch, 1)
                        dve.wait_ge(so_ch, OC * before + n[0])
                    return seq

                def over_max(g, b, g0):
                    def chunk(c, before, k):
                        over_edges(g, before, k)
                        seq = over_seq(before, 2)
                        d = 3 * before
                        dve.wait_ge(so_g, k * 64)
                        a_columns(oV, oA16, 0, of[:, :]).then_inc(so_dv, 1)
                        dve.wait_ge(so_pe, d + 1)
                        running_max(seq, FA[b], 0, odT, one, orB, orm).then_inc(so_dv, 1)
                        dve.wait_ge(so_pe, d + 2)
                        nc.vector.tensor_copy(oRM[:, 0, :, 0:HEADS], FA[b][:, 256:272].rearrange("p (c h) -> p c h", c=GT)).then_inc(so_dv, 1)
                        dve.wait_ge(so_pe, d + 3)
                        chunk_max(seq, FA[b][0:TN, 320:340].rearrange("p (c h) -> p c h", c=GT), oG[:, :, :], b)
                        seq(nc.vector.tensor_tensor(Gm[:, b, :, :], Gm[:, b, :, :], oG[:, :, :], ALU.max))
                        dve.sem_inc(so_done, 1)
                        dve.wait_ge(so_done, k)
                    for_max.each(g, chunk)

                def node_values(g, b, g0):
                    seq = front_chain(g0)
                    adst = SELF[:, b, :, D + HEADS:TW]
                    nc.vector.tensor_copy(N8[:, b, :, 0:HEADS], adst)
                    nc.vector.tensor_tensor(EXS[:, b, :, :], SELF[:, b, :, D:D + HEADS], adst, ALU.add)
                    seq(nc.vector.tensor_tensor(Gm[:, b, :, :], Gm[:, b, :, :], adst, ALU.add))
                    nc.vector.scalar_tensor_tensor(N8[:, b, :, HEADS:2 * HEADS], Gm[:, b, :, :], 0.2, Gm[:, b, :, :], ALU.mult, ALU.max).then_inc(s_n8, 1)
                    seq(nc.vector.scalar_tensor_tensor(EXS[:, b, :, :], EXS[:, b, :, :], 0.2, EXS[:, b, :, :], ALU.mult, ALU.max))
                    nc.vector.tensor_tensor(EXS[:, b, :, :], EXS[:, b, :, :], N8[:, b, :, HEADS:2 * HEADS], ALU.subtract).then_inc(s_exs_in, 1)

                def edge_exponent(g, b, g0):
                    dve.wait_ge(s_pn, g + 1)
                    at = PN
                    exponent(front_chain(g0), V, b, FA[b][:, at:at + 32].rearrange("p (c v) -> p c v", c=GT), EX).then_inc(s_exa, 1)

                def messages(g, b, g0):
                    dve.wait_ge(s_ex, g + 1)
                    nc.vector.tensor_tensor(heads(VX[:, b, :, :]), heads(V[:, b, :, 0:D]),
                                            EX[:, b, :, :].unsqueeze(3).to_broadcast([P, GT, HEADS, HD]), ALU.mult).then_inc(s_vx, 1)

                def totals(g, b, g0):
                    dve.wait_ge(s_num, g + 1)
                    dve.wait_ge(s_self, g + 1)
                    at = DN
                    nc.vector.tensor_tensor(NUM[:, b, :, :], FA[b][0:TN, :].rearrange("p (c d) -> p c d", c=GT), NUM[:, b, :, :], ALU.add)
                    nc.vector.tensor_tensor(DEN[:, b, :, :], FB[b][0:TN, at:at + 16].rearrange("p (c h) -> p c h", c=GT), EXS[:, b, :, :], ALU.add).then_inc(s_tot, 1)
                    dve.wait_ge(s_tot, g + 1)

                def over_sums(g, b, g0):
                    def chunk(c, before, k):
                        over_edges(g, before, k)
                        seq = over_seq(before, 2)
                        d = 3 * before
                        dve.wait_ge(s_ag, g + 1)
                        dve.wait_ge(so_g, k * 64)
                        dve.sem_inc(so_dv, 1)
                        dve.wait_ge(so_pe, d + 1)
                        nc.vector.tensor_copy(oMT[:, 0, :, :], FB[b][0:TN, :].rearrange("p (c e) -> p c e", c=GT)).then_inc(so_dv, 1)
                        dve.wait_ge(so_pe, d + 2)
                        seq(nc.vector.tensor_tensor(AT[:, b, :], AT[:, b, :], FB[b][:, 0:GN], ALU.add))
                        seq(exponent(seq, oV, 0, FB[b][:, OPN:OPN + 32].rearrange("p (c v) -> p c v", c=GT), oEX))
                        dve.wait_ge(so_ex, k)
                        nc.vector.tensor_tensor(heads(oV[:, 0, :, 0:D]), heads(oV[:, 0, :, 0:D]),
                                                oEX[:, 0, :, :].unsqueeze(3).to_broadcast([P, GT, HEADS, HD]), ALU.mult).then_inc(so_dv, 1)
                        dve.wait_ge(so_pe, d + 3)
                        nc.vector.tensor_tensor(NUM[:, b, :, :], FA[b][0:TN, :].rearrange("p (c d) -> p c d", c=GT), NUM[:, b, :, :], ALU.add)
                        seq(nc.vector.tensor_tensor(DEN[:, b, :, :], FB[b][0:TN, DN:DN + 16].rearrange("p (c h) -> p c h", c=GT), DEN[:, b, :, :], ALU.add))
                        seq(nc.vector.memset(of[:, 0:1], 0.0))
                        dve.sem_inc(so_done, 1)
                        dve.wait_ge(so_done, k)
                    for_sums.each(g, chunk)

                def row(name):
                    return K[name][0:TN, :].unsqueeze(1).to_broadcast([TN, GT, D])

                def attention(g, b, g0):
                    if b == 0:
                        nb[0] = 0
                    seq = back_chain(g0)
                    seq(nc.vector.tensor_scalar(DEN[:, b, :, :], DEN[:, b, :, :], 1e-16, None, ALU.add))
                    seq(nc.vector.reciprocal(DEN[:, b, :, :], DEN[:, b, :, :]))
                    seq(nc.vector.tensor_tensor(heads(Z[:, b, :, :]), heads(NUM[:, b, :, :]),
                                                DEN[:, b, :, :].unsqueeze(3).to_broadcast([TN, GT, HEADS, HD]), ALU.mult))
                    nc.vector.tensor_tensor(Z[:, b, :, :], Z[:, b, :, :], row("batt_less_1"), ALU.add).then_inc(s_mn, 1)

                def moments(seq, x, b, n):
                    for c in range(GT):
                        last = nc.vector.bn_stats(stats[:, b, c, :], x[:, b, c, :])
                    seq(last)
                    dve.sem_inc(passed, 1)
                    for c in range(GT):
                        last = nc.vector.bn_aggr(mv[n][:, b, c, 0:2], stats[:, b, c, :])
                    last.then_inc(s_var[n], 1)

                def scale_and_shift(n, chain):
                    def step(g, b, g0):
                        if n == 1 and b == 0:
                            nk[0] = 0
                        dve.wait_ge(s_std[n], g + 1)
                        chain(g0)(nc.vector.reciprocal(mv[n][:, b, :, 1], mv[n][:, b, :, 1]))
                        nc.vector.scalar_tensor_tensor(mv[n][:, b, :, 2], mv[n][:, b, :, 0], -1.0, mv[n][:, b, :, 1],
                                                       ALU.mult, ALU.mult).then_inc(s_nb[n], 1)
                    return step

                def x2_sum(g, b, g0):
                    seq = back_chain(g0)
                    dve.wait_ge(s_elu, g + 1)
                    dve.wait_ge(s_x[b], use(g, b, 16) + 16)
                    nc.vector.scalar_tensor_tensor(tmp[:, b, :, :], tmp[:, b, :, :], 1.0, X[:, b, :, :], ALU.min, ALU.add).then_inc(s_res, 1)
                    dve.wait_ge(s_res, g + 1)
                    seq(nc.vector.scalar_tensor_tensor(Z[:, b, :, :], Z[:, b, :, :], -1.0, tmp[:, b, :, :], ALU.max, ALU.add))
                    moments(seq, Z, b, 0)

                def mlp_sum(g, b, g0):
                    seq = back_chain(g0)
                    dve.wait_ge(s_h3p, g + 1)
                    seq(nc.vector.tensor_tensor(mlp[:, b, :, :], BK[b][0:TN, :].rearrange("p (c d) -> p c d", c=GT), row("b3"), ALU.add))
                    moments(seq, mlp, b, 1)

                def x3_sum(g, b, g0):
                    seq = close_chain(g0)
                    dve.wait_ge(s_mlp, g + 1)
                    dve.wait_ge(s_xb, g + 1)
                    seq(nc.vector.tensor_tensor(Z3[:, b, :, :], Z3[:, b, :, :], row("gamma"), ALU.mult))
                    seq(nc.vector.tensor_tensor(Z3[:, b, :, :], Z3[:, b, :, :], XB[:, b, :, :], ALU.add))
                    moments(seq, Z3, b, 2)

                in_turns(dve, [("B", attention), ("F", first), ("C", scale_and_shift(1, close_chain)), ("B", x2_sum),
                               ("B", scale_and_shift(0, back_chain)), ("F", run_max), ("F", max_columns), ("C", x3_sum),
                               ("F", node_max), ("F", over_max), ("F", node_values), ("F", edge_exponent),
                               ("C", scale_and_shift(2, close_chain)), ("F", messages), ("B", mlp_sum), ("F", totals),
                               ("F", over_sums)])
                assert (nf[0], nb[0], nk[0]) == (CF, CB, CC), (nf, nb, nk)


def build(nc, t, stop=99):
    ctx = ExitStack()
    with ctx:
        def sb(name, shape, dt=FP32):
            return ctx.enter_context(nc.sbuf_tensor(name, shape, dt))

        K = {
            "ident": sb("ident", [P, P]), "ltri": sb("ltri", [P, P]), "ones": sb("ones", [P, P]),
            "ones_bf": sb("ones_bf", [P, P], BF16), "zeros_bf": sb("zeros_bf", [P, P], BF16),
            "ltri_bf": sb("ltri_bf", [P, P], BF16), "iota": sb("iota", [P, GN]), "tbase": sb("tbase", [P, T]),
            "eps": sb("eps", [P, 1]), "deg_src": sb("deg_src", [TN, T]), "deg_dst": sb("deg_dst", [TN, T]),
            "deg_rows": sb("deg_rows", [G, GN]),
        }
        constants_phase(nc, K)
        prep_phase(nc, K, t["edges"], t["row_dram"], t["bin_dram"], t["by_src"])
        for name, width, dt in (("W01", D, FP32), ("W02", D, FP32), ("W1a", D, FP32), ("W1b", D, FP32), ("W2", D, FP32),
                                ("W3", D, FP32), ("Watt", TW, FP32), ("I_V0", D, FP32), ("V1", D, FP32), ("V2", D, FP32),
                                ("V3", D, FP32), ("b01", D, FP32), ("b02", D, FP32), ("batt", D, FP32), ("batt_less_1", D, FP32), ("b3", D, FP32),
                                ("gamma", D, FP32), ("beta", D, FP32), ("b1c", 1, FP32), ("b2c", 1, FP32),
                                ("idx_dst", T + AHEAD, I32), ("rel_dst", T + AHEAD, FP32), ("idx_src", G + 3, I32), ("rel_src", G + 3, FP32)):
            K[name] = sb(name, [P, width], dt)
        for name, width in (("inv_dst", T), ("isq", T), ("inv_src", T)):
            K[name] = sb(name, [TN, width])
        for name, width in (("starts", T), ("bstarts", G), ("more_dst", G), ("more_src", G),
                            ("next_dst", G + 1), ("next_src", G + 1)):
            K[name] = sb(name, [1, width], I32)
        weights_phase(nc, K, t)
        index_phase(nc, K, t)
        if stop < 1:
            return
        sums_pass(nc, K, t, "hyper1", HG, t["x"], K["W01"], t["m1"], scale=K["inv_dst"])
        if stop < 2:
            return
        node_pass(nc, K, t, "node1", t["m1"], K["b01"], t["h1"])
        sums_pass(nc, K, t, "hyper2", HG, t["h1"], K["W02"], t["m2"], scale=K["inv_dst"])
        if stop < 3:
            return
        node_pass(nc, K, t, "node2", t["m2"], K["b02"], t["x1"], x_in=t["x"], att_out=t["att"])
        if stop < 4:
            return
        attention_pass(nc, K, t)
        if stop < 5:
            return
        sums_pass(nc, K, t, "cheb1", G, t["y0"], K["V1"], t["y1"], read_r=t["r0"], write_r=t["r1"])
        sums_pass(nc, K, t, "cheb2", G, t["y1"], K["V2"], t["y2"], read_r=t["r1"], write_r=t["r2"], minus=t["y0"], twice=2.0)
        sums_pass(nc, K, t, "cheb3", G, t["y2"], K["V3"], t["out"], read_r=t["r2"], norm=True)


_WEIGHTS = ["L0_gnn_W1", "L0_gnn_b1", "L0_gnn_W2", "L0_gnn_b2", "L1_gnn_W", "L1_gnn_att_src", "L1_gnn_att_dst",
            "L1_gnn_bias", "L2_gnn_W1", "L2_gnn_b1", "L2_gnn_W2", "L2_gnn_b2", "L2_gnn_W3", "L2_gnn_b3",
            "L2_gnn_gamma", "L2_gnn_beta", "L3_gnn_weights"]
_SCRATCH = {"row_dram": ((2, T), I32), "bin_dram": ((2, G), I32), "by_src": ((EP, 2), I32), "m1": ((HE, D), FP32),
            "m2": ((HE, D), FP32), "h1": ((N, D), FP32), "x1": ((N, D), FP32), "att": ((N, TW), FP32),
            "y0": ((N, D), FP32), "y1": ((N, D), FP32), "y2": ((N, D), FP32), "r0": ((N, D), FP32),
            "r1": ((N, D), FP32), "r2": ((N, D), FP32)}


def kernel(**inputs):
    import concourse.bacc as _bacc
    from concourse.bass_utils import run_bass_kernel_spmd as _run

    nc = _bacc.Bacc("TRN2", target_bir_lowering=False, num_devices=1)
    edges = np.full((EP, 2), PAD, np.int32)
    edges[:E, 0] = inputs["src"]
    edges[:E, 1] = inputs["dst"]
    features = np.zeros((E + P, D), np.float32)
    features[:E] = inputs["edge_attr_128"]
    arrays = {"x": np.ascontiguousarray(inputs["x"]), "edges": edges, "edge_attr": features}
    for name in _WEIGHTS:
        arrays[name] = np.ascontiguousarray(inputs[name])
    t = {name: nc.dram_tensor(name, a.shape, mybir.dt.from_np(a.dtype), kind="ExternalInput").ap()
         for name, a in arrays.items()}
    for name, (shape, dt) in _SCRATCH.items():
        t[name] = nc.dram_tensor(name, shape, dt, kind="Internal").ap()
    t["out"] = nc.dram_tensor("out", (N, D), FP32, kind="ExternalOutput").ap()
    build(nc, t)
    r = _run(nc, [arrays], core_ids=[0])
    return r.results[0]["out"]
```
